# Optimizing a Trainium2 kernel written in Bass

```python
import numpy as np
import jax
import jax.numpy as jnp

def _softmax(x, axis=-1):
    return jax.nn.softmax(x, axis=axis)

def _gelu(x):
    return jax.nn.gelu(x, approximate=True)

def _silu(x):
    return jax.nn.silu(x)

def _sigmoid(x):
    return jax.nn.sigmoid(x)

def _layernorm(x, axis=-1, eps=1e-05):
    m = jnp.mean(x, axis=axis, keepdims=True)
    v = jnp.var(x, axis=axis, keepdims=True)
    return (x - m) / jnp.sqrt(v + eps)

def _scatter_add(tgt, idx, src, axis=0):
    return tgt.at[idx].add(src)

def _segment_sum(src, seg, n):
    return jax.ops.segment_sum(src, seg, n)
kernel_name = 'mk_cond_resid_d2_seqx_r2_4241dc'

def setup_inputs(seed: int=0):
    np.random.seed(seed)
    _w = jnp.asarray

    def _rec_inputs():
        import jax
        import jax.numpy as jnp
        _rk = jax.random.key(seed)
        x = -0.0003929 + 0.9999 * jax.random.normal(jax.random.fold_in(_rk, 1), (64, 128, 512), jnp.float32)
        _lenS = 128 - jax.random.randint(jax.random.fold_in(_rk, 7), (64,), 0, max(1, 128 // 4) + 1, jnp.int32)
        _lenS2 = 128 - jax.random.randint(jax.random.fold_in(_rk, 8), (64,), 0, max(1, 128 // 4) + 1, jnp.int32)
        cond_2048 = 0.00782532 + 1.00527 * jax.random.normal(jax.random.fold_in(_rk, 11), (64, 1024), jnp.float32)
        return (x, cond_2048)
    x, cond_2048 = _rec_inputs()

    def _L0_cond_setup():
        import jax, jax.numpy as jnp
        import numpy as np
        B, S, D_MODEL, D_INNER, D_STATE = (4, 2048, 512, 1024, 16)
        key = jax.random.key(seed)
        ks = jax.random.split(key, 12)
        inp = {'x': jax.random.normal(ks[0], (B, S, D_MODEL), jnp.float32), 't_emb': jax.random.normal(ks[1], (B, D_INNER), jnp.float32), 'W_in': jax.random.normal(ks[2], (2 * D_INNER, D_MODEL), jnp.float32) * 0.02, 'W_conv': jax.random.normal(ks[3], (D_INNER, 1, 4), jnp.float32) * 0.1, 'b_conv': jnp.zeros((D_INNER,), jnp.float32), 'ln_g': jnp.ones((D_INNER,), jnp.float32), 'ln_b': jnp.zeros((D_INNER,), jnp.float32), 'W_xproj': jax.random.normal(ks[4], (3 * D_STATE, D_INNER), jnp.float32) * 0.02, 'W_dt': jax.random.normal(ks[5], (D_STATE, D_STATE), jnp.float32) * 0.01, 'b_dt': jax.random.uniform(ks[6], (D_STATE,), jnp.float32) * 0.1, 'A_log': jax.random.normal(ks[7], (D_STATE,), jnp.float32) * 0.1, 'D': jnp.ones((D_INNER,), jnp.float32) * 0.1, 'W_out': jax.random.normal(ks[8], (D_MODEL, D_INNER), jnp.float32) * 0.02}
        return inp
    _L0_cond_all = _L0_cond_setup()
    _L0_cond_in = {k: v for k, v in _L0_cond_all.items() if k in ('W_in', 'W_conv', 'b_conv', 'ln_g', 'ln_b', 'W_xproj', 'W_dt', 'b_dt', 'A_log', 'D', 'W_out')}
    del _L0_cond_all

    def _L1_cond_setup():
        import jax, jax.numpy as jnp
        import numpy as np
        EPS_IN = 1e-05
        EPS_DM = 1e-08

        def _dcoef(weight, style):
            return jax.lax.rsqrt(jnp.einsum('oi,bi->bo', jnp.square(weight), jnp.square(style)) + EPS_DM)
        key = jax.random.key(seed)
        ks = jax.random.split(key, 7)
        B, S, H = (8, 512, 512)
        lim = 1.0 / np.sqrt(H)
        u = lambda k, shp: jax.random.uniform(k, shp, jnp.float32, -lim, lim)
        return {'x': jax.random.normal(ks[0], (B, S, H), jnp.float32), 'q_weight': u(ks[1], (H, H)), 'k_weight': u(ks[2], (H, H)), 'v_weight': u(ks[3], (H, H)), 'w_weight': u(ks[4], (H, H)), 'u_weight': u(ks[5], (H, H)), 'styles': jax.random.normal(ks[6], (B, 2 * H), jnp.float32) * 0.5 + 1.0, 'num_heads': 16}
    _L1_cond_all = _L1_cond_setup()
    _L1_cond_in = {k: v for k, v in _L1_cond_all.items() if k in ('q_weight', 'k_weight', 'v_weight', 'w_weight', 'u_weight')}
    del _L1_cond_all
    return {'x': x, 'cond_2048': cond_2048, 'L0_cond_W_in': _L0_cond_in['W_in'], 'L0_cond_W_conv': _L0_cond_in['W_conv'], 'L0_cond_b_conv': _L0_cond_in['b_conv'], 'L0_cond_ln_g': _L0_cond_in['ln_g'], 'L0_cond_ln_b': _L0_cond_in['ln_b'], 'L0_cond_W_xproj': _L0_cond_in['W_xproj'], 'L0_cond_W_dt': _L0_cond_in['W_dt'], 'L0_cond_b_dt': _L0_cond_in['b_dt'], 'L0_cond_A_log': _L0_cond_in['A_log'], 'L0_cond_D': _L0_cond_in['D'], 'L0_cond_W_out': _L0_cond_in['W_out'], 'L1_cond_q_weight': _L1_cond_in['q_weight'], 'L1_cond_k_weight': _L1_cond_in['k_weight'], 'L1_cond_v_weight': _L1_cond_in['v_weight'], 'L1_cond_w_weight': _L1_cond_in['w_weight'], 'L1_cond_u_weight': _L1_cond_in['u_weight']}

def reference(x, cond_2048, L0_cond_W_in, L0_cond_W_conv, L0_cond_b_conv, L0_cond_ln_g, L0_cond_ln_b, L0_cond_W_xproj, L0_cond_W_dt, L0_cond_b_dt, L0_cond_A_log, L0_cond_D, L0_cond_W_out, L1_cond_q_weight, L1_cond_k_weight, L1_cond_v_weight, L1_cond_w_weight, L1_cond_u_weight):
    import jax
    import jax.numpy as jnp

    def _L0_cond_ref(x, t_emb, W_in, W_conv, b_conv, ln_g, ln_b, W_xproj, W_dt, b_dt, A_log, D, W_out):
        import jax, jax.numpy as jnp
        import numpy as np
        B, S, D_MODEL, D_INNER, D_STATE = (4, 2048, 512, 1024, 16)
        d_inner = W_conv.shape[0]
        d_state = A_log.shape[0]
        xr, gate = jnp.split(x @ W_in.T, 2, axis=-1)
        xr = xr + t_emb[:, None, :]
        xc = jax.lax.conv_general_dilated(xr.transpose(0, 2, 1), W_conv, (1,), [(3, 0)], feature_group_count=d_inner, dimension_numbers=('NCH', 'OIH', 'NCH')) + b_conv[None, :, None]
        xc = jax.nn.silu(xc).transpose(0, 2, 1)
        mu = xc.mean(-1, keepdims=True)
        var = xc.var(-1, keepdims=True)
        xn = (xc - mu) / jnp.sqrt(var + 1e-05) * ln_g + ln_b
        Bm, Cm, dt = jnp.split(xn @ W_xproj.T, 3, axis=-1)
        dt = jnp.tanh(dt @ W_dt.T + b_dt) * 0.01
        A = -jnp.tanh(A_log)
        Ad = 1.0 + dt * A
        Bd = Bm * jnp.minimum(jnp.linalg.norm(xn, axis=-1, keepdims=True), 1.0)
        h0 = jnp.zeros((xn.shape[0], d_state, d_inner), xn.dtype)

        def step(h, inputs):
            ad, bd, xt, ct = inputs
            h = jnp.clip(h * ad[:, :, None] + bd[:, :, None] * xt[:, None, :], -10.0, 10.0)
            yt = jnp.einsum('bd,bdh->bh', ct, h)
            return (h, yt)
        _, ys = jax.lax.scan(step, h0, (Ad.transpose(1, 0, 2), Bd.transpose(1, 0, 2), xn.transpose(1, 0, 2), Cm.transpose(1, 0, 2)))
        y = ys.transpose(1, 0, 2) + D * xn
        return y * jax.nn.silu(gate) @ W_out.T

    def _L1_cond_ref(x, q_weight, k_weight, v_weight, w_weight, u_weight, styles, num_heads):
        import jax, jax.numpy as jnp
        import numpy as np
        EPS_IN = 1e-05
        EPS_DM = 1e-08

        def _dcoef(weight, style):
            return jax.lax.rsqrt(jnp.einsum('oi,bi->bo', jnp.square(weight), jnp.square(style)) + EPS_DM)
        B, S, H = x.shape
        nh = num_heads
        d = H // nh
        scale = jnp.asarray(d, x.dtype) ** (-0.5)
        s1 = styles[:, :H]
        s2 = styles[:, H:]
        x = x * s1[:, None, :]
        mu = jnp.mean(x, axis=-1, keepdims=True)
        var = jnp.mean(jnp.square(x - mu), axis=-1, keepdims=True)
        x = (x - mu) * jax.lax.rsqrt(var + EPS_IN)
        q_dc = _dcoef(q_weight, s1)
        k_dc = _dcoef(k_weight, s1)
        v_dc = _dcoef(v_weight, s1)
        w_dc = _dcoef(w_weight, s2)
        u_dc = _dcoef(u_weight, s2)

        def heads(t):
            return t.reshape(B, S, nh, d).transpose(0, 2, 1, 3)
        q = heads(jnp.einsum('bsh,oh->bso', x, q_weight) * q_dc[:, None, :])
        k = heads(jnp.einsum('bsh,oh->bso', x, k_weight) * k_dc[:, None, :])
        v_flat = jnp.einsum('bsh,oh->bso', x, v_weight) * v_dc[:, None, :] * s2[:, None, :]
        skip = v_flat
        v = heads(v_flat)
        attn = jnp.einsum('bhqd,bhkd->bhqk', q, k) * scale
        attn = jax.nn.softmax(attn, axis=-1)
        out = jnp.einsum('bhqk,bhkd->bhqd', attn, v).transpose(0, 2, 1, 3).reshape(B, S, H)
        out = jnp.einsum('bsh,oh->bso', out, w_weight) * w_dc[:, None, :]
        skip = jnp.einsum('bsh,oh->bso', skip, u_weight) * u_dc[:, None, :]
        return out + skip
    x = x + _L0_cond_ref(x, cond_2048, L0_cond_W_in, L0_cond_W_conv, L0_cond_b_conv, L0_cond_ln_g, L0_cond_ln_b, L0_cond_W_xproj, L0_cond_W_dt, L0_cond_b_dt, L0_cond_A_log, L0_cond_D, L0_cond_W_out)
    x = x + _L1_cond_ref(x, L1_cond_q_weight, L1_cond_k_weight, L1_cond_v_weight, L1_cond_w_weight, L1_cond_u_weight, cond_2048, 16)
    return x

_drawn_inputs = setup_inputs


def setup_inputs(seed=0):
    import zlib

    import numpy as np

    out = dict(_drawn_inputs(seed))
    spreads = {'L0_cond_b_conv': (0.0, 0.1),
     'L0_cond_ln_g': (1.0, 0.2),
     'L0_cond_ln_b': (0.0, 0.1),
     'L0_cond_D': (0.10000000149011612, 0.6)}
    factors = {'L0_cond_W_dt': 34.311, 'L0_cond_b_dt': 27.143, 'L0_cond_A_log': 8.0}
    for name, (base, spread) in spreads.items():
        noise = np.random.default_rng([zlib.crc32(name.encode()), seed]).standard_normal(out[name].shape)
        drawn = base * np.exp(spread * noise) if base else spread * noise
        out[name] = jnp.asarray(drawn.astype(out[name].dtype))
    for name, factor in factors.items():
        out[name] = (out[name] * factor).astype(out[name].dtype)
    return out
```

```python
from contextlib import ExitStack

import concourse.bass as bass
from concourse import mybir

F32 = mybir.dt.float32
BF16 = mybir.dt.bfloat16
ALU = mybir.AluOpType
ACT = mybir.ActivationFunctionType
AX_X = mybir.AxisListType.X

P = 128
NB, S, D, DI, NS = 64, 128, 512, 1024, 16
NP = 3 * NS
NQ = NB // 4
KC, DC = D // P, DI // P
GB = P // NS
NG = NB // GB
HALF = NB // 2
GH = NG // 2
TB = 8
NTB = S // TB
PAIRS = [(0, 0), (0, 1), (0, 2), (1, 0), (1, 1), (2, 0)]
KR = GB * len(PAIRS)
NH, HD = 16, 32
LN_EPS, DC_EPS = 1e-5, 1e-8
CLIP = 10.0


class Memory:

    def __init__(self, nc, ctx, prefix):
        self.nc, self.ctx, self.prefix = nc, ctx, prefix

    def sb(self, name, shape, dtype=F32):
        return self.ctx.enter_context(self.nc.sbuf_tensor(self.prefix + name, shape, dtype))

    def ps(self, name, shape):
        return self.ctx.enter_context(self.nc.psum_tensor(self.prefix + name, shape, F32))

    def sem(self, name):
        return self.ctx.enter_context(self.nc.semaphore(self.prefix + name))


def reached(engine, semaphore, value):
    if not (isinstance(value, int) and value <= 0):
        engine.wait_ge(semaphore, value)


def over(ap, shape):
    return ap.to_broadcast(shape)


def coefficients(nc, d, k):
    with ExitStack() as ctx:
        m = Memory(nc, ctx, "co_")
        weight = m.sb("weight", [P, 2, KC, D])
        squared = m.sb("squared", [P, KC, D])
        style = k["temb"]
        style_sq = m.sb("style_sq", [P, 2 * KC, NB])
        dc = m.sb("dc", [P, 5, KC, NB])
        wx = m.sb("wx", [P, DC, NP])
        wxb = m.sb("wxb", [P, DC, NP])
        lng, lnb = m.sb("lng", [P, DC]), m.sb("lnb", [P, DC])
        ones = m.sb("ones", [P, P])
        sums = [m.ps(f"sums{i}", [P, KC, NB]) for i in range(2)]
        fold = m.ps("fold", [P, 2, NP])
        loaded, w_loaded = m.sem("loaded"), [m.sem(f"w_loaded{i}") for i in range(2)]
        sq_ready, sums_ready, dc_rooted, dve = m.sem("sq_ready"), m.sem("sums_ready"), m.sem("dc_rooted"), m.sem("dve")
        style_ready, fold_ready, biased, sums_taken = m.sem("style_ready"), m.sem("fold_ready"), m.sem("biased"), m.sem("sums_taken")
        n_loads = 12
        block = ctx.enter_context(nc.Block())
        weights = [d["Wq"], d["Wk"], d["Wv"], d["Ww"], d["Wu"]]

        @block.sync
        def _(sp):
            for out, src in [(wx[:], d["Wx"]), (lng[:], d["ln_g"]), (lnb[:], d["ln_b"]),
                             (k["ident"][:], d["ident"]), (k["bdt"][:], d["b_dt"]), (k["alog"][:], d["A_log"]),
                             (k["blockdt"][:], d["W_dt"]),
                             (k["head_mask"][:], d["head_mask"]), (k["pick_mask"][:], d["pick_mask"]),
                             (k["conv_w"][:], d["conv_w"]), (k["conv_b"][:], d["conv_b"]),
                             (k["temb"][:], d["temb"])]:
                sp.dma_start(out, src).then_inc(loaded, 16)
            for i, w in enumerate(weights):
                reached(sp, sq_ready, i - 1)
                sp.dma_start(weight[:, i % 2], w).then_inc(w_loaded[i % 2], 16)

        @block.scalar
        def _(act):
            act.wait_ge(loaded, 16 * n_loads)
            nc.scalar.activation(style_sq[:], style[:], ACT.Square).then_inc(style_ready, 1)
            for i in range(5):
                act.wait_ge(w_loaded[i % 2], 16 * (i // 2 + 1))
                reached(act, sums_ready, i)
                nc.scalar.activation(squared[:], weight[:, i % 2], ACT.Square).then_inc(sq_ready, 1)
            act.wait_ge(biased, 5)
            nc.scalar.activation(dc[:], dc[:], ACT.Sqrt).then_inc(dc_rooted, 1)

        @block.tensor
        def _(pe):
            pe.wait_ge(style_ready, 1)
            for i in range(5):
                pe.wait_ge(sq_ready, i + 1)
                reached(pe, biased, i - 1)
                half = KC * (i >= 3)
                for o in range(KC):
                    for c in range(KC):
                        mm = pe.matmul(sums[i % 2][:, o], squared[:, c, o * P:(o + 1) * P], style_sq[:, half + c],
                                       start=c == 0, stop=c == KC - 1)
                mm.then_inc(sums_ready, 1)
            pe.wait_ge(dve, 3)
            for i, w in enumerate((k["wxg"], wxb)):
                for c in range(DC):
                    mm = pe.matmul(fold[:, i], ones[:], w[:, c], start=c == 0, stop=c == DC - 1)
            mm.then_inc(fold_ready, 1)

        @block.vector
        def _(dv):
            nc.vector.memset(ones[:], 1.0).then_inc(dve, 1)
            dv.wait_ge(loaded, 16 * n_loads)
            nc.vector.tensor_tensor(k["wxg"][:], wx[:], over(lng[:].unsqueeze(2), [P, DC, NP]), ALU.mult).then_inc(dve, 1)
            nc.vector.tensor_tensor(wxb[:], wx[:], over(lnb[:].unsqueeze(2), [P, DC, NP]), ALU.mult).then_inc(dve, 1)
            for i in range(5):
                dv.wait_ge(sums_ready, i + 1)
                nc.vector.tensor_scalar(dc[:, i], sums[i % 2][:], DC_EPS, None, ALU.add).then_inc(biased, 1)
            dv.wait_ge(fold_ready, 1)
            nc.vector.tensor_copy(k["fold"][:], fold[:]).then_inc(dve, 1)
            dv.wait_ge(dc_rooted, 1)
            nc.vector.reciprocal(dc[:], dc[:]).then_inc(dve, 1)
            dv.wait_ge(dve, 5)
            nc.vector.scalar_tensor_tensor(out=k["scales"][:, 0], in0=dc[:, 0], scalar=float(HD) ** -0.5,
                                           in1=dc[:, 1], op0=ALU.mult, op1=ALU.mult).then_inc(dve, 1)
            nc.vector.tensor_tensor(k["scales"][:, 1], dc[:, 2], style[:, KC:2 * KC], ALU.mult).then_inc(dve, 1)
            nc.vector.tensor_copy(k["scales"][:, 2:4], dc[:, 3:5]).then_inc(dve, 1)
            for i, value in enumerate((-0.5, 0.5, -1.0)):
                nc.vector.memset(k["powers"][:, i:i + 1], value).then_inc(dve, 1)


def front(nc, d, k):
    with ExitStack() as ctx:
        m = Memory(nc, ctx, "fr_")
        win = m.sb("win", [P, KC, DI])
        xT = m.sb("xT", [P, 2, KC, 4 * S])
        padded = m.sb("padded", [P, 2, 4, S + 3])
        conv = m.sb("conv", [P, 2, 4, S])
        xc = m.sb("xc", [P, 2, DC, 4 * S])
        xn = m.sb("xn", [P, 2, DI])
        parts = m.sb("parts", [P, 2, 3, DI], BF16)
        rest = m.sb("rest", [P, 2, DI])
        dx = m.sb("dx", [P, 2, DI])
        rows = m.sb("rows", [P, 3, DI])
        bn = m.sb("bn", [P, 2, 2, 6])
        pause = m.sb("pause", [P, 1])
        moments = m.sb("moments", [P, 2, 2])
        var = m.sb("var", [P, 2, 1])
        squares = m.sb("squares", [P, DI])
        stats = m.sb("stats", [P, 2, 4, 4])
        xr_ps = [m.ps(f"xr_ps{i}", [P, 4, S]) for i in range(4)]
        nat_ps = m.ps("nat_ps", [P, DI])
        proj_ps = m.ps("proj_ps", [P, 4, 64])
        sem = m.sem
        consts, x_loaded = sem("consts"), [sem("x_loaded0"), sem("x_loaded1")]
        xr_ready, xp_ready, tap_ready, conv_step, conv_ready = sem("xr_ready"), sem("xp_ready"), sem("tap_ready"), sem("conv_step"), sem("conv_ready")
        silu_ready, nat_ready, proj_ready, proj_taken = sem("silu_ready"), sem("nat_ready"), sem("proj_ready"), sem("proj_taken")
        mom_step, mom_ready, rs_step, rs_ready, xhat_ready, xn_step, xn_ready = (sem("mom_step"), sem("mom_ready"), sem("rs_step"), sem("rs_ready"),
                                                              sem("xhat_ready"), sem("xn_step"), sem("xn_ready"))
        dx_ready, part1, rest1, part2, part3, sq_done = sem("dx_ready"), sem("part1"), sem("rest1"), sem("part2"), sem("part3"), sem("sq_done")
        parts_out, dx_out = [sem("parts_out0"), sem("parts_out1")], [sem("dx_out0"), sem("dx_out1")]
        taken, zeroed = sem("taken"), sem("zeroed")
        block = ctx.enter_context(nc.Block())

        def quads(engine, step):
            step(0, 0, True, False, False)
            step(1, 1, True, True, False)
            with engine.Fori(0, NQ // 2 - 2) as j:
                step(2 * j + 2, 0, True, True, True)
                step(2 * j + 3, 1, True, True, True)
            step(NQ - 2, 0, True, True, True)
            step(NQ - 1, 1, True, True, True)
            step(NQ, 0, False, True, True)


        @block.sync
        def _(sp):
            sp.dma_start(win[:], d["Win"][:, :, 0:DI]).then_inc(consts, 16)
            for i, name in enumerate(("ln_g_row", "ln_b_row", "D_row")):
                sp.dma_start(rows[:, i], over(d[name], [P, DI])).then_inc(consts, 16)
            sp.dma_start(xT[:, 0], d["xT"][0]).then_inc(x_loaded[0], 16)

            def store(b, par, slot):
                n = b
                sp.wait_ge(part3, n + 1)
                for i in range(3):
                    for h in range(2):
                        sp.dma_start(d["xparts"][i, h, bass.ds(b, 1)].rearrange("o t c -> (o t) c"),
                                     parts[:, par, i, h * 512:(h + 1) * 512]).then_inc(parts_out[par], 16)
                sp.wait_ge(dx_ready, n + 1)
                sp.dma_start(d["dx"][bass.ds(b, 1)].rearrange("o t c -> (o t) c"), dx[:, par]).then_inc(dx_out[par], 16)

            def step(q, par, main, nat, late):
                if main:
                    reached(sp, xr_ready, DC * q)
                    if not (isinstance(q, int) and q == NQ - 1):
                        sp.dma_start(xT[:, 1 - par], d["xT"][bass.ds(q + 1, 1)].rearrange("o p c n -> (o p) c n")).then_inc(x_loaded[1 - par], 16)
                for b in range(4):
                    if nat and (late or b > 0):
                        store(4 * q + b - 5, (b + 1) % 2, b)
            quads(sp, step)
            store(NB - 1, 1, 0)
            for par in range(2):
                sp.wait_ge(parts_out[par], 16 * 6 * NB // 2)
                sp.wait_ge(dx_out[par], 16 * NB // 2)

        @block.tensor
        def _(pe):
            pe.wait_ge(consts, 64)

            def inner(q, par, c):
                n = DC * q + c
                if c == 0:
                    pe.wait_ge(x_loaded[par], 8 * q + 16 if par == 0 else 8 * q + 8)
                reached(pe, xp_ready, n - 3)
                for i in range(KC):
                    mm = pe.matmul(xr_ps[c % 4][:].rearrange("p b t -> p (b t)"), win[:, i, c * P:(c + 1) * P], xT[:, par, i],
                                   start=i == 0, stop=i == KC - 1)
                mm.then_inc(xr_ready, 1)

            def natural(q, par, b):
                n = 4 * q + b
                if b == 0:
                    pe.wait_ge(silu_ready, DC * q + DC)
                reached(pe, xhat_ready, n)
                for c in range(DC):
                    mm = pe.transpose(nat_ps[:, c * P:(c + 1) * P], xc[:, par, c, b * S:(b + 1) * S], k["ident"][:])
                mm.then_inc(nat_ready, 1)
                if b == 0:
                    reached(pe, proj_taken, q)
                for c in range(DC):
                    mm = pe.matmul(proj_ps[:, b, 0:NP], xc[:, par, c, b * S:(b + 1) * S], k["wxg"][:, c],
                                   start=c == 0, stop=c == DC - 1)
                mm.then_inc(proj_ready, 1)

            def step(q, par, main, nat, late):
                for b in range(4):
                    if main:
                        inner(q, par, 2 * b)
                        inner(q, par, 2 * b + 1)
                    if nat:
                        natural(q - 1, 1 - par, b)
            quads(pe, step)

        @block.vector
        def _(dv):
            nc.vector.memset(padded[:], 0.0).then_inc(zeroed, 1)
            nc.vector.memset(stats[:], 0.0).then_inc(zeroed, 1)
            dv.wait_ge(zeroed, 2)

            def add_temb(q, par, c):
                n = DC * q + c
                dv.wait_ge(xr_ready, n + 1)
                reached(dv, conv_ready, n - 1)
                emb = k["temb"][:, c, bass.ds(4 * q, 4)].unsqueeze(2)
                nc.vector.tensor_tensor(padded[:, c % 2, :, 3:], xr_ps[c % 4][:], over(emb, [P, 4, S]),
                                        ALU.add).then_inc(xp_ready, 1)

            def taps(n, c):
                dv.wait_ge(tap_ready, n + 1)
                for i in range(1, 4):
                    if i > 1:
                        dv.wait_ge(conv_step, 2 * n + i - 1)
                    op = nc.vector.scalar_tensor_tensor(out=conv[:, c % 2], in0=padded[:, c % 2, :, i:i + S], scalar=k["conv_w"][:, c, i:i + 1],
                                                        in1=conv[:, c % 2], op0=ALU.mult, op1=ALU.add)
                    op.then_inc(conv_step if i < 3 else conv_ready, 1)

            def moment(n, b):
                u = b % 2
                dv.wait_ge(nat_ready, n + 1)
                reached(dv, rs_ready, n - 1)
                nc.vector.bn_stats(bn[:, u, 0], nat_ps[:, 0:512])
                nc.vector.bn_stats(bn[:, u, 1], nat_ps[:, 512:1024]).then_inc(mom_step, 1)
                dv.wait_ge(mom_step, 2 * n + 1)
                nc.vector.memset(pause[:], 0.0)
                nc.vector.bn_aggr(moments[:, u], bn[:, u].rearrange("p a b -> p (a b)")).then_inc(mom_step, 1)
                dv.wait_ge(mom_step, 2 * n + 2)
                nc.vector.tensor_scalar(var[:, u], moments[:, u, 1:2], LN_EPS, None, ALU.add).then_inc(mom_ready, 1)

            def split(n, par):
                dv.wait_ge(part1, n + 1)
                nc.vector.tensor_tensor(rest[:, par], xn[:, par], parts[:, par, 0], ALU.subtract).then_inc(rest1, 1)
                dv.wait_ge(part2, n + 1)
                nc.vector.tensor_tensor(parts[:, par, 2], rest[:, par], parts[:, par, 1], ALU.subtract).then_inc(part3, 1)

            def step(q, par, main, nat, late):
                for b in range(4):
                    for c in (2 * b, 2 * b + 1):
                        if main:
                            add_temb(q, par, c)
                        if (main or c == 0) and not (isinstance(q, int) and q == 0 and c == 0):
                            taps(DC * q + c - 1, (c - 1) % DC)
                    if nat:
                        moment(4 * q + b - 4, b)
                        if late or b > 0:
                            split(4 * q + b - 5, (b + 1) % 2)
                        if b == 0 and late:
                            dv.wait_ge(proj_ready, 4 * q - 4)
                            nc.vector.tensor_copy(k["proj"][:, bass.ds(4 * q - 8, 4)], proj_ps[:, :, 0:NP]).then_inc(proj_taken, 1)
                            dv.wait_ge(sq_done, 4 * q - 4)
                            nc.vector.tensor_copy(k["stats"][:, bass.ds(4 * q - 8, 4)], stats[:, par]).then_inc(taken, 1)
            quads(dv, step)
            split(NB - 1, 1)
            dv.wait_ge(proj_ready, NB)
            nc.vector.tensor_copy(k["proj"][:, NB - 4:NB], proj_ps[:, :, 0:NP]).then_inc(proj_taken, 1)
            dv.wait_ge(sq_done, NB)
            nc.vector.tensor_copy(k["stats"][:, NB - 4:NB], stats[:, 1]).then_inc(taken, 1)

        @block.scalar
        def _(act):
            def tap0(q, c):
                n = DC * q + c
                act.wait_ge(xp_ready, n + 1)
                reached(act, silu_ready, n - 1)
                nc.scalar.activation(conv[:, c % 2], padded[:, c % 2, :, 0:S], ACT.Identity, bias=k["conv_b"][:, c:c + 1],
                                     scale=k["conv_w"][:, c, 0:1]).then_inc(tap_ready, 1)

            def normalise(n, par, b):
                act.wait_ge(rs_ready, n + 1)
                reached(act, dx_ready, n - 1)
                reached(act, part3, n - 1)
                nc.scalar.activation(xn[:, b % 2], nat_ps[:], ACT.Identity, bias=stats[:, par, b, 1:2],
                                     scale=stats[:, par, b, 0:1]).then_inc(xhat_ready, 1)

            def split(n, par, spar, b):
                act.wait_ge(xn_ready, n + 1)
                reached(act, parts_out[par], 48 * n - 48 * par)
                nc.scalar.activation(parts[:, par, 0], xn[:, par], ACT.Copy).then_inc(part1, 1)
                reached(act, sq_done, n)
                nc.scalar.activation(squares[:], xn[:, par], ACT.Square, accum_out=stats[:, spar, b, 2:3]).then_inc(sq_done, 1)
                act.wait_ge(rest1, n + 1)
                nc.scalar.activation(parts[:, par, 1], rest[:, par], ACT.Copy).then_inc(part2, 1)

            def step(q, par, main, nat, late):
                for b in range(4):
                    for c in (2 * b, 2 * b + 1):
                        if main:
                            tap0(q, c)
                        if (main or c == 0) and not (isinstance(q, int) and q == 0 and c == 0):
                            n = DC * q + c - 1
                            act.wait_ge(conv_ready, n + 1)
                            sc = (c - 1) % DC
                            spar = par if c > 0 else 1 - par
                            if sc == 0:
                                reached(act, proj_ready, 4 * q - 4)
                            nc.scalar.activation(xc[:, spar, sc], conv[:, sc % 2].rearrange("p b t -> p (b t)"), ACT.Silu).then_inc(silu_ready, 1)
                    if nat:
                        if b == 0:
                            reached(act, taken, q - 2)
                        normalise(4 * q + b - 4, 1 - par, b)
                        if late or b > 0:
                            split(4 * q + b - 5, (b + 1) % 2, 1 - par if b > 0 else par, (b - 1) % 4)
            quads(act, step)
            split(NB - 1, 1, 1, 3)

        @block.gpsimd
        def _(pool):
            pool.wait_ge(consts, 64)

            def gains(n, u):
                pool.wait_ge(xhat_ready, n + 1)
                nc.gpsimd.tensor_tensor(xn[:, u], xn[:, u], rows[:, 0], ALU.mult).then_inc(xn_step, 1)
                pool.wait_ge(xn_step, n + 1)
                nc.gpsimd.tensor_tensor(xn[:, u], xn[:, u], rows[:, 1], ALU.add).then_inc(xn_ready, 1)
                pool.wait_ge(xn_ready, n + 1)
                reached(pool, dx_out[u], 8 * n - 8 * u)
                nc.gpsimd.tensor_tensor(dx[:, u], xn[:, u], rows[:, 2], ALU.mult).then_inc(dx_ready, 1)

            def step(q, par, main, nat, late):
                for b in range(4):
                    if nat:
                        n = 4 * q + b - 4
                        pool.wait_ge(mom_ready, n + 1)
                        if b == 0:
                            reached(pool, taken, q - 2)
                        nc.gpsimd.tensor_tensor(stats[:, 1 - par, b, 0:1], var[:, b % 2], k["powers"][:, 0:1], ALU.pow).then_inc(rs_step, 1)
                        pool.wait_ge(rs_step, 2 * n + 1)
                        nc.gpsimd.tensor_tensor(stats[:, 1 - par, b, 1:2], moments[:, b % 2, 0:1], stats[:, 1 - par, b, 0:1], ALU.mult).then_inc(rs_step, 1)
                        pool.wait_ge(rs_step, 2 * n + 2)
                        nc.gpsimd.tensor_tensor(stats[:, 1 - par, b, 1:2], stats[:, 1 - par, b, 1:2], k["powers"][:, 2:3], ALU.mult).then_inc(rs_ready, 1)
                        gains(n, b % 2)
            quads(pool, step)


def projections(nc, d, k):
    with ExitStack() as ctx:
        m = Memory(nc, ctx, "pr_")
        shift = m.sb("shift", [P, NB, NP])
        norm = m.sb("norm", [P, NB])
        half = m.sb("half", [P, NB])
        b_all = m.sb("b_all", [P, NB, NS])
        b_rest = m.sb("b_rest", [P, 2, NB, NS])
        b_parts = m.sb("b_parts", [P, 3, NB * NS], BF16)
        c_all = m.sb("c_all", [P, NB * NS])
        dt_all = m.sb("dt_all", [P, NB * NS])
        dtT = m.sb("dtT", [P, NG * S])
        chunks = m.sb("chunks", [P, 2, NTB, 2, GH, TB])
        minus_a = m.sb("minus_a", [P, 1])
        cT_ps, dtT_ps, dt_ps = m.ps("cT_ps", [P, NG, S]), m.ps("dtT_ps", [P, NG, S]), m.ps("dt_ps", [P, NG * S])
        sem = m.sem
        dve, capped, rooted, tanh_a, b_out, turned_c, turned_dt = (sem("dve"), sem("capped"), sem("rooted"), sem("tanh_a"), sem("b_out"),
                                                                  sem("turned_c"), sem("turned_dt"))
        dtT_ready, dt_ready, tanh_ready, chunks_ready, chunk_out, split, natural = (sem("dtT_ready"), sem("dt_ready"), sem("tanh_ready"),
            sem("chunks_ready"), sem("chunk_out"), sem("split"), sem("natural"))
        block = ctx.enter_context(nc.Block())
        proj, stats, fold = k["proj"], k["stats"], k["fold"]

        @block.vector
        def _(dv):
            done = 0

            def chained(op):
                nonlocal done
                done += 1
                op.then_inc(dve, 1)
                dv.wait_ge(dve, done)

            nc.vector.tensor_scalar(norm[:], stats[:, :, 2], 1.0, None, ALU.min).then_inc(capped, 1)
            chained(nc.vector.tensor_tensor(proj[:], proj[:], over(stats[:, :, 0:1], [P, NB, NP]), ALU.mult))
            chained(nc.vector.tensor_tensor(shift[:], over(stats[:, :, 1:2], [P, NB, NP]),
                                            over(fold[:, 0].unsqueeze(1), [P, NB, NP]), ALU.mult))
            chained(nc.vector.tensor_tensor(proj[:], proj[:], shift[:], ALU.add))
            chained(nc.vector.tensor_tensor(proj[:], proj[:], over(fold[:, 1].unsqueeze(1), [P, NB, NP]), ALU.add))
            nc.vector.tensor_copy(dt_all[:].rearrange("p (b s) -> p b s", s=NS), proj[:, :, 2 * NS:NP]).then_inc(natural, 1)
            nc.vector.tensor_copy(c_all[:].rearrange("p (b s) -> p b s", s=NS), proj[:, :, NS:2 * NS]).then_inc(natural, 1)
            dv.wait_ge(rooted, 1)
            chained(nc.vector.tensor_tensor(b_all[:], proj[:, :, 0:NS], over(half[:].unsqueeze(2), [P, NB, NS]), ALU.mult))
            flat = b_all[:].rearrange("p b s -> p (b s)")
            for i in range(3):
                rest = flat if i == 0 else b_rest[:, i - 1].rearrange("p b s -> p (b s)")
                op = nc.vector.tensor_copy(b_parts[:, i], rest)
                if i == 2:
                    op.then_inc(split, 1)
                else:
                    chained(op)
                    chained(nc.vector.tensor_tensor(b_rest[:, i].rearrange("p b s -> p (b s)"), rest, b_parts[:, i], ALU.subtract))
            dv.wait_ge(turned_dt, 1)
            nc.vector.tensor_copy(dtT[:], dtT_ps[:].rearrange("p g t -> p (g t)")).then_inc(dtT_ready, 1)
            dv.wait_ge(turned_c, 1)
            for g in range(NG):
                nc.vector.tensor_copy(chunks[:, g // GH, :, 1, g % GH], cT_ps[:, g].rearrange("p (n t) -> p n t", t=TB))
            dv.wait_ge(tanh_a, 1)
            chained(nc.vector.tensor_scalar(minus_a[:], k["alog"][:], -0.01, None, ALU.mult))
            dv.wait_ge(tanh_ready, 2)
            for g in range(NG):
                op = nc.vector.tensor_scalar(chunks[:, g // GH, :, 0, g % GH], dtT[:, g * S:(g + 1) * S].rearrange("p (n t) -> p n t", t=TB),
                                             minus_a[:], 1.0, ALU.mult, ALU.add)
            chained(op)
            nc.vector.memset(chunks[:, :, 0, 0, :, 0:1], 0.0).then_inc(chunks_ready, 1)

        @block.gpsimd
        def _(pool):
            pool.wait_ge(capped, 1)
            nc.gpsimd.tensor_tensor(half[:], norm[:], over(k["powers"][:, 1:2], [P, NB]), ALU.pow).then_inc(rooted, 1)

        @block.tensor
        def _(pe):
            for i, (src, ps, turned) in enumerate(((dt_all, dtT_ps, turned_dt), (c_all, cT_ps, turned_c))):
                pe.wait_ge(natural, i + 1)
                for g in range(NG):
                    mm = pe.transpose(ps[:, g], src[:, g * P:(g + 1) * P], k["ident"][:])
                mm.then_inc(turned, 1)
            pe.wait_ge(dtT_ready, 1)
            for i in range(2):
                pe.matmul(dt_ps[:, i * 512:(i + 1) * 512], k["blockdt"][:], dtT[:, i * 512:(i + 1) * 512],
                          start=True, stop=True).then_inc(dt_ready, 1)

        @block.scalar
        def _(act):
            nc.scalar.activation(k["alog"][:], k["alog"][:], ACT.Tanh).then_inc(tanh_a, 1)
            act.wait_ge(dt_ready, 2)
            for i in range(2):
                nc.scalar.activation(dtT[:, i * 512:(i + 1) * 512], dt_ps[:, i * 512:(i + 1) * 512], ACT.Tanh,
                                     bias=k["bdt"][:]).then_inc(tanh_ready, 1)

        @block.sync
        def _(sp):
            sp.wait_ge(split, 1)
            for i in range(3):
                sp.dma_start(d["bparts"][i].rearrange("g t c -> t g c"), b_parts[:, i].rearrange("t (g c) -> t g c", c=P)).then_inc(b_out, 16)
            sp.wait_ge(chunks_ready, 1)
            for h in range(2):
                sp.dma_start(d["chunks"][h].rearrange("n p c -> p n c"), chunks[:, h].rearrange("p n a g t -> p n (a g t)")).then_inc(chunk_out, 16)
            sp.wait_ge(b_out, 48)
            sp.wait_ge(chunk_out, 32)


def scan(nc, d, k):
    with ExitStack() as ctx:
        m = Memory(nc, ctx, "sc_")
        x_rows = m.sb("x_rows", [KR, 2, GH, TB * 512], BF16)
        b_rows = m.sb("b_rows", [KR, 2, GH, TB, P], BF16)
        mask = m.sb("mask", [KR, P], BF16)
        ac = m.sb("ac", [P, 2, 2, GH, TB])
        c_cols = m.sb("c_cols", [P, 2, GH, TB, 32])
        state = m.sb("state", [P, 2, GH, 512])
        raw = m.sb("raw", [P, GH, 512])
        dx = m.sb("dx", [P, 2, 2, 512])
        y = m.sb("y", [P, 2, 512])
        bx_ps = [m.ps(f"bx_ps{g}", [P, 512]) for g in range(GH)]
        y_ps = [m.ps(f"y_ps{i}", [P, 512]) for i in range(2)]
        sem = m.sem
        x_loaded, b_loaded, ac_loaded, dx_loaded = ([sem(f"{n}{i}") for i in range(2)] for n in ("x_loaded", "b_loaded", "ac_loaded", "dx_loaded"))
        b_masked, c_ready, bx_ready, raw_ready, clipped, y_done, y_added = (sem("b_masked"), sem("c_ready"), sem("bx_ready"),
            sem("raw_ready"), sem("clipped"), sem("y_done"), sem("y_added"))
        y_out = [sem("y_out0"), sem("y_out1")]
        mask_ready = sem("mask_ready")
        Y_BIAS, ADD_BIAS, OUT_BIAS = TB + 1, 3, 16
        block = ctx.enter_context(nc.Block())

        def blocks(engine, step):
            for hb in range(2):
                with engine.Fori(0, 2) as dh:
                    with engine.Fori(0, NTB // 2) as j:
                        for par in range(2):
                            step(hb, dh, j, par, hb * 2 * NTB + dh * NTB + 2 * j + par)

        @block.sync
        def _(sp):
            def step(hb, dh, j, par, n):
                sp.wait_ge(y_done, TB * n + 1)
                b0 = hb * HALF
                for i, (px, pb) in enumerate(PAIRS):
                    rows = slice(GB * i, GB * (i + 1))
                    src = d["xparts"][px, bass.ds(dh, 1), b0:b0 + HALF, bass.ds(2 * TB * j + TB * par, TB)]
                    sp.dma_start(x_rows[rows, par], src.rearrange("o (g b) t c -> (o b) g (t c)", b=GB)).then_inc(x_loaded[par], 16)
                    src = d["bparts"][pb:pb + 1, hb * GH:(hb + 1) * GH, bass.ds(2 * TB * j + TB * par, TB)]
                    sp.dma_start(b_rows[rows, par].rearrange("b g t c -> b g (t c)"),
                                 over(src.rearrange("o g t c -> o g (t c)"), [GB, GH, TB * P])).then_inc(b_loaded[par], 16)
                sp.dma_start(ac[:, par].rearrange("p a g t -> p (a g t)"),
                             d["chunks"][hb, bass.ds(2 * j + par, 1)].rearrange("o p c -> (o p) c")).then_inc(ac_loaded[par], 16)
                sp.wait_ge(y_added, 2 * n + 1)
                for u in range(2):
                    src = d["dx"][b0:b0 + HALF, bass.ds(2 * TB * j + TB * par + 4 * u, 4), bass.ds(512 * dh, 512)]
                    sp.dma_start(dx[:, par, u], src).then_inc(dx_loaded[par], 16)
            blocks(sp, step)

        @block.gpsimd
        def _(pool):
            pool.wait_ge(mask_ready, 1)

            def step(hb, dh, j, par, n):
                jj = hb * NTB + dh * (NTB // 2) + j
                pool.wait_ge(b_loaded[par], 96 * jj + 96)
                for g in range(GH):
                    op = nc.gpsimd.tensor_tensor(b_rows[:, par, g], b_rows[:, par, g], over(mask[:].unsqueeze(1), [KR, TB, P]), ALU.mult)
                op.then_inc(b_masked, 1)
                pool.wait_ge(ac_loaded[par], 16 * jj + 16)
                pool.wait_ge(y_done, TB * n + 1)
                for g in range(GH):
                    for u in range(2):
                        op = nc.gpsimd.tensor_tensor(c_cols[:, par, g, 4 * u:4 * u + 4], k["head_mask"][:],
                                                     over(ac[:, par, 1, g, 4 * u:4 * u + 4].unsqueeze(2), [P, 4, 32]), ALU.mult)
                op.then_inc(c_ready, 1)
            blocks(pool, step)

        @block.tensor
        def _(pe):
            def step(hb, dh, j, par, n):
                jj = hb * NTB + dh * (NTB // 2) + j
                pe.wait_ge(x_loaded[par], 96 * jj + 96)
                pe.wait_ge(b_masked, n + 1)

                def drive(t):
                    for g in range(GH):
                        pe.wait_ge(raw_ready, GH * TB * n + GH * t + g + 1)
                        pe.matmul(bx_ps[g][:], b_rows[:, par, g, t], x_rows[:, par, g, t * 512:(t + 1) * 512],
                                  start=True, stop=True).then_inc(bx_ready, 1)

                def read(t):
                    if t % 4 == 0:
                        pe.wait_ge(y_added, 2 * n + t // 4 + 2)
                    pe.wait_ge(clipped, GH * TB * n + GH * (t + 1) + GH)
                    for g in range(GH):
                        mm = pe.matmul(y_ps[t // 4][32 * g:32 * g + 32, :], c_cols[:, par, g, t], state[:, t % 2, g],
                                       start=t % 4 == 0, stop=t % 4 == 3)
                    mm.then_inc(y_done, 1)

                drive(0)
                pe.wait_ge(c_ready, n + 1)
                for t in range(TB):
                    if t < TB - 1:
                        drive(t + 1)
                    read(t)
            blocks(pe, step)

        @block.vector
        def _(dv):
            nc.vector.memset(state[:, 0], 0.0).then_inc(y_done, Y_BIAS)
            nc.vector.memset(y[:], 0.0).then_inc(y_added, ADD_BIAS)
            for u in range(2):
                nc.vector.memset(raw[:, u], 0.0).then_inc(y_out[u], OUT_BIAS)
            nc.vector.memset(raw[:, 2:GH], 0.0).then_inc(raw_ready, GH)
            nc.vector.tensor_copy(mask[:], k["pick_mask"][:]).then_inc(mask_ready, 1)
            nc.vector.memset(state[:, 1], 0.0).then_inc(clipped, GH)

            def step(hb, dh, j, par, n):
                jj = hb * NTB + dh * (NTB // 2) + j
                dv.wait_ge(ac_loaded[par], 16 * jj + 16)

                def advance(t, g):
                    at = GH * TB * n + GH * t + g
                    dv.wait_ge(bx_ready, at + 1)
                    dv.wait_ge(clipped, at + 1)
                    nc.vector.scalar_tensor_tensor(out=raw[:, g], in0=state[:, (t + 1) % 2, g], scalar=ac[:, par, 0, g, t:t + 1],
                                                   in1=bx_ps[g][:], op0=ALU.mult, op1=ALU.add).then_inc(raw_ready, 1)

                def clip(t, g):
                    at = GH * TB * n + GH * t + g
                    dv.wait_ge(raw_ready, at + 1 + GH)
                    if g == 0:
                        dv.wait_ge(y_done, TB * n + t + Y_BIAS - 1)
                    nc.vector.tensor_scalar(state[:, t % 2, g], raw[:, g], CLIP, -CLIP, ALU.min, ALU.max).then_inc(clipped, 1)

                def add(u):
                    dv.wait_ge(y_done, TB * n + 4 * u + 4 + Y_BIAS)
                    dv.wait_ge(dx_loaded[par], 32 * jj + 32)
                    dv.wait_ge(y_out[u], 16 * n + OUT_BIAS)
                    nc.vector.tensor_tensor(y[:, u], y_ps[u][:], dx[:, par, u], ALU.add).then_inc(y_added, 1)

                for t in range(TB):
                    advance(t, 0)
                    for g in range(1, GH):
                        advance(t, g)
                        clip(t, g - 1)
                    clip(t, GH - 1)
                    if t == 4:
                        add(0)
                add(1)
            blocks(dv, step)

        @block.scalar
        def _(act):
            def step(hb, dh, j, par, n):
                b0 = hb * HALF
                for u in range(2):
                    act.wait_ge(y_added, 2 * n + u + 1 + ADD_BIAS)
                    dst = d["y"][b0:b0 + HALF, bass.ds(2 * TB * j + TB * par + 4 * u, 4), bass.ds(512 * dh, 512)]
                    act.dma_start(dst, y[:, u]).then_inc(y_out[u], 16)
            blocks(act, step)
            for u in range(2):
                act.wait_ge(y_out[u], 16 * 4 * NTB + OUT_BIAS)


def back(nc, d, k):
    with ExitStack() as ctx:
        m = Memory(nc, ctx, "ba_")
        wgate, wout = m.sb("wgate", [P, KC, DI]), m.sb("wout", [P, DC, D])
        wq, wk, wv, ww, wu = (m.sb(n, [P, KC, D]) for n in ("wq", "wk", "wv", "ww", "wu"))
        xT = m.sb("xT", [P, KC, 4 * S])
        y = m.sb("y", [P, 4, DI])
        gate = m.sb("gate", [P, 2, 4 * S])
        z = m.sb("z", [P, DC, 4 * S])
        probs = z[:, 0:4]
        probsT = z[:, 4:8]
        x_in, style, xs = m.sb("x_in", [P, 2, D]), m.sb("style", [P, 2, D]), m.sb("xs", [P, 2, D])
        x2 = m.sb("x2", [P, 4, D])
        nT = m.sb("nT", [P, KC, 4 * S])
        qT, kT, vT, oT = (m.sb(n, [P, KC, 4 * S]) for n in ("qT", "kT", "vT", "oT"))
        v = m.sb("v", [P, 4, D])
        fu = m.sb("fu", [P, 4 * S])
        recip = m.sb("recip", [P, KC, S])
        result = m.sb("result", [P, 2, D])
        ones = m.sb("ones", [P, HD])
        scale = m.sb("scale", [P, 4, KC, 4])
        scale_wu = m.sb("scale_wu", [P, 2, KC, 4])
        bn, moments, var, norm = m.sb("bn", [P, 2, 6]), m.sb("moments", [P, 2, 2]), m.sb("var", [P, 2, 1]), m.sb("norm", [P, 2, 2])
        largest, pause = m.sb("largest", [P, 4, 4]), m.sb("pause", [P, 1])
        main = [m.ps(f"main{i}", [P, 512]) for i in range(2)]
        side = [m.ps(f"side{i}", [P, 4, S]) for i in range(2)]
        scores = m.ps("scores", [P, 4, 4, S])
        names = """consts x_loaded y_loaded gate_ready silu_done yT_ready z_done wo_ready x2_done xs_ready bn_step mom_ready
            rs_step rs_ready n_ready nT_ready nT_copied v_ready v_copied vT_ready vT_done q_ready q_done k_ready k_copied s_ready
            max_done sub_done exp_done pT_ready pT_copied o_ready rec_done o_done w_ready u_ready fw_done fu_done f_done fT_ready
            out_done scaled ones_ready""".split()
        s = {n: m.sem(n) for n in names}
        xin_loaded, style_loaded, stored = ([m.sem(f"{n}{i}") for i in range(2)] for n in ("xin_loaded", "style_loaded", "stored"))
        block = ctx.enter_context(nc.Block())

        def quads(engine, step):
            step(0, True, False)
            step(1, True, True)
            with engine.Fori(2, NQ) as q:
                step(q, True, True)
            step(NQ, False, True)

        def quad_slice(q):
            return bass.ds(4 * q, 4)

        @block.sync
        def _(sp):
            for w, name in ((wout, "Wout"), (wq, "Wq"), (wk, "Wk"), (wv, "Wv"), (ww, "Ww"), (wu, "Wu")):
                sp.dma_start(w[:], d[name]).then_inc(s["consts"], 16)
            sp.dma_start(wgate[:], d["Win"][:, :, DI:2 * DI]).then_inc(s["consts"], 16)

            def step(q, now, before):
                if now:
                    reached(sp, s["gate_ready"], DC * q)
                    sp.dma_start(xT[:], d["xT"][bass.ds(q, 1)].rearrange("o p c n -> (o p) c n")).then_inc(s["x_loaded"], 16)
                    reached(sp, s["yT_ready"], DC * q)
                    sp.dma_start(y[:], d["y"][quad_slice(q)].rearrange("b t c -> t b c")).then_inc(s["y_loaded"], 16)
                    for b in range(4):
                        reached(sp, s["x2_done"], 4 * q + b - 1)
                        sp.dma_start(x_in[:, b % 2], d["x"][bass.ds(4 * q + b, 1)].rearrange("o t c -> (o t) c")).then_inc(xin_loaded[b % 2], 16)
                        reached(sp, s["xs_ready"], 4 * q + b - 1)
                        sp.dma_start(style[:, b % 2], over(d["style_rows"][bass.ds(4 * q + b, 1), 0:D], [P, D])).then_inc(style_loaded[b % 2], 16)
            quads(sp, step)

        @block.gpsimd
        def _(pool):
            def step(q, now, before):
                if now:
                    for b in range(4):
                        n, u = 4 * q + b, b % 2
                        pool.wait_ge(s["mom_ready"], n + 1)
                        reached(pool, s["n_ready"], n - 1)
                        nc.gpsimd.tensor_tensor(norm[:, u, 0:1], var[:, u], k["powers"][:, 0:1], ALU.pow).then_inc(s["rs_step"], 1)
                        pool.wait_ge(s["rs_step"], 2 * n + 1)
                        nc.gpsimd.tensor_tensor(norm[:, u, 1:2], moments[:, u, 0:1], norm[:, u, 0:1], ALU.mult).then_inc(s["rs_step"], 1)
                        pool.wait_ge(s["rs_step"], 2 * n + 2)
                        nc.gpsimd.tensor_tensor(norm[:, u, 1:2], norm[:, u, 1:2], k["powers"][:, 2:3], ALU.mult).then_inc(s["rs_ready"], 1)
                if before:
                    for b in range(4):
                        pool.wait_ge(s["out_done"], 4 * q - 3 + b)
                        pool.dma_start(d["out"][bass.ds(4 * q - 4 + b, 1)].rearrange("o t c -> (o t) c"), result[:, b % 2]).then_inc(stored[b % 2], 16)
            def ordered(q, now, before):
                step(q, False, before)
                step(q, now, False)
            quads(pool, ordered)
            for u in range(2):
                pool.wait_ge(stored[u], 16 * NB // 2)

        @block.tensor
        def _(pe):
            pe.wait_ge(s["consts"], 16 * 7)
            pe.wait_ge(s["ones_ready"], 1)

            def products(out, lhs, rhs, sem, chunks=KC):
                for c in range(chunks):
                    mm = pe.matmul(out, lhs(c), rhs(c), start=c == 0, stop=c == chunks - 1)
                mm.then_inc(s[sem], 1)

            def gate_chunk(q, c):
                reached(pe, s["silu_done"], DC * q + c - 1)
                products(main[c % 2][:], lambda i: wgate[:, i, c * P:(c + 1) * P], lambda i: xT[:, i], "gate_ready")
                reached(pe, s["z_done"], DC * q + c - 1)
                for b in range(4):
                    mm = pe.transpose(side[c % 2][:, b], y[:, b, c * P:(c + 1) * P], k["ident"][:])
                mm.then_inc(s["yT_ready"], 1)

            def last_products(q):
                reached(pe, s["o_done"], 4 * q)
                for c in range(KC):
                    reached(pe, s["fw_done"], 4 * q - 4 + c)
                    products(main[0][:], lambda i: ww[:, i, c * P:(c + 1) * P], lambda i: oT[:, i], "w_ready")
                    reached(pe, s["fu_done"], 4 * q - 4 + c)
                    products(main[1][:], lambda i: wu[:, i, c * P:(c + 1) * P], lambda i: vT[:, i], "u_ready")
                pe.wait_ge(s["f_done"], 4 * q)
                for b in range(4):
                    reached(pe, s["out_done"], 4 * q - 4 + b - 1 if b >= 2 else 0)
                    for c in range(KC):
                        mm = pe.transpose(main[b % 2][:, c * P:(c + 1) * P], nT[:, c, b * S:(b + 1) * S], k["ident"][:])
                    mm.then_inc(s["fT_ready"], 1)

            def turn_norm(q, b):
                pe.wait_ge(s["n_ready"], 4 * q + b + 1)
                reached(pe, s["nT_copied"], 4 * q + b - 1 if b >= 2 else 0)
                for c in range(KC):
                    mm = pe.transpose(side[b % 2][:, c], xs[:, b % 2, c * P:(c + 1) * P], k["ident"][:])
                mm.then_inc(s["nT_ready"], 1)

            def v_rows(q, b):
                pe.wait_ge(s["nT_copied"], 4 * q + b + 1)
                if b < 2:
                    pe.wait_ge(s["x2_done"], 4 * q + b + 3)
                else:
                    pe.wait_ge(s["v_copied"], 4 * q + b - 1)
                products(main[b % 2][:], lambda i: nT[:, i, b * S:(b + 1) * S], lambda i: wv[:, i], "v_ready")

            def turn_v(q, b):
                pe.wait_ge(s["v_copied"], 4 * q + b + 1)
                for c in range(KC):
                    mm = pe.transpose(scores[:, b, c], v[:, b, c * P:(c + 1) * P], k["ident"][:])
                mm.then_inc(s["vT_ready"], 1)

            def q_chunk(q, c):
                reached(pe, s["v_copied"], 4 * q + 4)
                reached(pe, s["q_done"], 4 * q + c - 1 if c >= 2 else 0)
                products(main[c % 2][:], lambda i: wq[:, i, c * P:(c + 1) * P], lambda i: nT[:, i], "q_ready")

            def k_chunk(q, c):
                pe.wait_ge(s["q_done"], 4 * q + min(c, 1) + 3)
                reached(pe, s["k_copied"], 4 * q + c - 1 if c >= 2 else 0)
                products(main[c % 2][:], lambda i: wk[:, i, c * P:(c + 1) * P], lambda i: nT[:, i], "k_ready")

            def score(q, b):
                if b == 0:
                    pe.wait_ge(s["vT_done"], 4 * q + 4)
                    pe.wait_ge(s["k_copied"], 4 * q + 4)
                reached(pe, s["sub_done"], 4 * q + b)
                for i in range(4):
                    for j in range(4):
                        r = slice(32 * j, 32 * j + 32)
                        mm = pe.matmul(scores[:, j, i], qT[r, i, b * S:(b + 1) * S], kT[r, i, b * S:(b + 1) * S], start=True, stop=True)
                mm.then_inc(s["s_ready"], 1)

            def turn_probs(q, b):
                pe.wait_ge(s["exp_done"], 4 * q + b + 1)
                for i in range(4):
                    if not (b == 0 and i < 2):
                        pe.wait_ge(s["pT_copied"], 16 * q + 4 * b + i - 1)
                    for j in range(4):
                        mm = pe.transpose(main[i % 2][:, j * P:(j + 1) * P], probs[:, j, i * S:(i + 1) * S], k["ident"][:])
                    mm.then_inc(s["pT_ready"], 1)

            def mix(q, b):
                pe.wait_ge(s["pT_copied"], 16 * q + 4 * b + 4)
                if b == 0:
                    pe.wait_ge(s["nT_copied"], 4 * q + 4)
                else:
                    pe.wait_ge(s["o_done"], 4 * q + b)
                for i in range(4):
                    for out, lhs in ((side[0], None), (side[1], ones)):
                        for j in range(4):
                            h = 4 * i + j
                            mm = pe.matmul(out[32 * j:32 * j + 32, i], ones[:] if lhs is not None else v[:, b, h * HD:(h + 1) * HD],
                                           probsT[:, i, j * S:(j + 1) * S], start=True, stop=True)
                mm.then_inc(s["o_ready"], 1)

            def step(q, now, before):
                if now:
                    pe.wait_ge(s["x_loaded"], 16 * q + 16)
                    pe.wait_ge(s["y_loaded"], 16 * q + 16)
                    reached(pe, s["pT_copied"], 16 * q)
                    reached(pe, s["o_done"], 4 * q)
                    for c in range(DC):
                        gate_chunk(q, c)
                    pe.wait_ge(s["silu_done"], DC * q + DC)
                if before:
                    last_products(q)
                    pe.wait_ge(s["out_done"], 4 * q)
                if now:
                    pe.wait_ge(s["z_done"], DC * q + DC)
                    for b in range(4):
                        reached(pe, s["x2_done"], 4 * q + b - 1 if b >= 2 else 0)
                        products(main[b % 2][:], lambda i: z[:, i, b * S:(b + 1) * S], lambda i: wout[:, i], "wo_ready", DC)
                    turn_norm(q, 0)
                    turn_norm(q, 1)
                    v_rows(q, 0)
                    turn_norm(q, 2)
                    v_rows(q, 1)
                    turn_v(q, 0)
                    turn_norm(q, 3)
                    v_rows(q, 2)
                    turn_v(q, 1)
                    v_rows(q, 3)
                    turn_v(q, 2)
                    q_chunk(q, 0)
                    turn_v(q, 3)
                    for c in range(1, KC):
                        q_chunk(q, c)
                    for c in range(KC):
                        k_chunk(q, c)
                    score(q, 0)
                    for b in range(4):
                        if b < 3:
                            score(q, b + 1)
                        turn_probs(q, b)
                        mix(q, b)
            quads(pe, step)

        @block.scalar
        def _(act):
            def step(q, now, before):
                if not now:
                    return
                for c in range(DC):
                    act.wait_ge(s["gate_ready"], DC * q + c + 1)
                    reached(act, s["z_done"], DC * q + c - 1)
                    nc.scalar.activation(gate[:, c % 2], main[c % 2][:], ACT.Silu).then_inc(s["silu_done"], 1)

                def normalise(b):
                    act.wait_ge(s["rs_ready"], 4 * q + b + 1)
                    nc.scalar.activation(xs[:, b % 2], xs[:, b % 2], ACT.Identity, bias=norm[:, b % 2, 1:2],
                                         scale=norm[:, b % 2, 0:1]).then_inc(s["n_ready"], 1)

                def copy_norm(b):
                    act.wait_ge(s["nT_ready"], 4 * q + b + 1)
                    if b == 0:
                        reached(act, s["fT_ready"], 4 * q)
                    nc.scalar.activation(nT[:, :, b * S:(b + 1) * S], side[b % 2][:], ACT.Copy).then_inc(s["nT_copied"], 1)

                def copy_v(b):
                    act.wait_ge(s["v_ready"], 4 * q + b + 1)
                    nc.scalar.activation(v[:, b], main[b % 2][:], ACT.Copy).then_inc(s["v_copied"], 1)

                normalise(0)
                normalise(1)
                copy_norm(0)
                normalise(2)
                copy_norm(1)
                normalise(3)
                copy_v(0)
                copy_norm(2)
                copy_v(1)
                copy_norm(3)
                copy_v(2)
                copy_v(3)
                for c in range(KC):
                    act.wait_ge(s["k_ready"], 4 * q + c + 1)
                    nc.scalar.activation(kT[:, c], main[c % 2][:], ACT.Copy).then_inc(s["k_copied"], 1)
                for b in range(4):
                    act.wait_ge(s["sub_done"], 4 * q + b + 1)
                    nc.scalar.activation(probs, probs, ACT.Exp).then_inc(s["exp_done"], 1)
                    for i in range(4):
                        act.wait_ge(s["pT_ready"], 16 * q + 4 * b + i + 1)
                        if i == 0:
                            reached(act, s["o_ready"], 4 * q + b)
                        nc.scalar.activation(probsT[:, i], main[i % 2][:], ACT.Copy).then_inc(s["pT_copied"], 1)
            quads(act, step)

        @block.vector
        def _(dv):
            nc.vector.memset(ones[:], 1.0).then_inc(s["ones_ready"], 1)

            def step(q, now, before):
                if before:
                    nc.vector.tensor_copy(scale_wu[:], k["scales"][:, 2:4, :, bass.ds(4 * q - 4, 4)]).then_inc(s["scaled"], 1)
                if now:
                    reached(dv, s["o_done"], 4 * q)
                    nc.vector.tensor_copy(scale[:, 0:2], k["scales"][:, 0:2, :, quad_slice(q)]).then_inc(s["scaled"], 1)
                    for c in range(DC):
                        dv.wait_ge(s["silu_done"], DC * q + c + 1)
                        dv.wait_ge(s["yT_ready"], DC * q + c + 1)
                        if c == 0:
                            reached(dv, s["o_ready"], 4 * q)
                        nc.vector.tensor_tensor(z[:, c], side[c % 2][:].rearrange("p b t -> p (b t)"), gate[:, c % 2], ALU.mult).then_inc(s["z_done"], 1)
                if before:
                    dv.wait_ge(s["scaled"], 2 * q)
                    for c in range(KC):
                        n = 4 * q - 4 + c
                        r = nT[:, c].rearrange("p (b t) -> p b t", b=4)
                        dv.wait_ge(s["w_ready"], n + 1)
                        nc.vector.tensor_tensor(r, main[0][:].rearrange("p (b t) -> p b t", b=4),
                                                over(scale_wu[:, 0, c].unsqueeze(2), [P, 4, S]), ALU.mult).then_inc(s["fw_done"], 1)
                        dv.wait_ge(s["u_ready"], n + 1)
                        reached(dv, s["f_done"], n)
                        nc.vector.tensor_tensor(fu[:].rearrange("p (b t) -> p b t", b=4), main[1][:].rearrange("p (b t) -> p b t", b=4),
                                                over(scale_wu[:, 1, c].unsqueeze(2), [P, 4, S]), ALU.mult).then_inc(s["fu_done"], 1)
                        dv.wait_ge(s["fu_done"], n + 1)
                        nc.vector.tensor_tensor(nT[:, c], nT[:, c], fu[:], ALU.add).then_inc(s["f_done"], 1)
                    for b in range(4):
                        n = 4 * q - 4 + b
                        dv.wait_ge(s["fT_ready"], n + 1)
                        reached(dv, stored[b % 2], 32 * (q - 1) + 16 * (b // 2))
                        nc.vector.tensor_tensor(result[:, b % 2], main[b % 2][:], x2[:, b], ALU.add).then_inc(s["out_done"], 1)
                if not now:
                    return
                for b in range(4):
                    n, u = 4 * q + b, b % 2
                    dv.wait_ge(s["wo_ready"], n + 1)
                    dv.wait_ge(xin_loaded[u], 32 * q + 16 * (b // 2) + 16)
                    nc.vector.tensor_tensor(x2[:, b], main[u][:], x_in[:, u], ALU.add).then_inc(s["x2_done"], 1)
                    dv.wait_ge(s["x2_done"], n + 1)
                    dv.wait_ge(style_loaded[u], 32 * q + 16 * (b // 2) + 16)
                    reached(dv, s["nT_ready"], n - 1)
                    nc.vector.tensor_tensor(xs[:, u], x2[:, b], style[:, u], ALU.mult).then_inc(s["xs_ready"], 1)
                    dv.wait_ge(s["xs_ready"], n + 1)
                    nc.vector.bn_stats(bn[:, u], xs[:, u]).then_inc(s["bn_step"], 1)
                    reached(dv, s["rs_ready"], n - 1)
                    dv.wait_ge(s["bn_step"], 2 * n + 1)
                    nc.vector.memset(pause[:], 0.0)
                    nc.vector.bn_aggr(moments[:, u], bn[:, u]).then_inc(s["bn_step"], 1)
                    dv.wait_ge(s["bn_step"], 2 * n + 2)
                    nc.vector.tensor_scalar(var[:, u], moments[:, u, 1:2], LN_EPS, None, ALU.add).then_inc(s["mom_ready"], 1)

                def scale_v(b):
                    dv.wait_ge(s["vT_ready"], 4 * q + b + 1)
                    nc.vector.tensor_tensor(vT[:, :, b * S:(b + 1) * S], scores[:, b], over(scale[:, 1, :, b:b + 1], [P, KC, S]),
                                            ALU.mult).then_inc(s["vT_done"], 1)

                def scale_q(c):
                    dv.wait_ge(s["q_ready"], 4 * q + c + 1)
                    nc.vector.tensor_tensor(qT[:, c].rearrange("p (b t) -> p b t", b=4), main[c % 2][:].rearrange("p (b t) -> p b t", b=4),
                                            over(scale[:, 0, c].unsqueeze(2), [P, 4, S]), ALU.mult).then_inc(s["q_done"], 1)

                dv.wait_ge(s["scaled"], 2 * q + 1)
                scale_v(0)
                scale_v(1)
                scale_v(2)
                scale_q(0)
                scale_v(3)
                for c in range(1, KC):
                    scale_q(c)

                def most(b):
                    dv.wait_ge(s["s_ready"], 4 * q + b + 1)
                    nc.vector.tensor_reduce(largest[:], scores[:], AX_X, ALU.max).then_inc(s["max_done"], 1)

                def subtract(b):
                    dv.wait_ge(s["max_done"], 4 * q + b + 1)
                    if b == 0:
                        dv.wait_ge(s["wo_ready"], 4 * q + 4)
                    else:
                        dv.wait_ge(s["pT_ready"], 16 * q + 4 * b)
                    nc.vector.tensor_tensor(probs.rearrange("p j (i t) -> p (j i) t", i=4), scores[:].rearrange("p j i t -> p (j i) t"),
                                            over(largest[:].rearrange("p j i -> p (j i)").unsqueeze(2), [P, 16, S]), ALU.subtract).then_inc(s["sub_done"], 1)

                def output(b):
                    n = 4 * q + b
                    dv.wait_ge(s["o_ready"], n + 1)
                    nc.vector.reciprocal(recip[:], side[1][:]).then_inc(s["rec_done"], 1)
                    dv.wait_ge(s["rec_done"], n + 1)
                    for i in range(KC):
                        op = nc.vector.scalar_tensor_tensor(out=oT[:, i, b * S:(b + 1) * S], in0=side[0][:, i], scalar=scale[:, 1, i, b:b + 1],
                                                            in1=recip[:, i], op0=ALU.mult, op1=ALU.mult)
                    op.then_inc(s["o_done"], 1)

                most(0)
                subtract(0)
                for b in range(4):
                    if b < 3:
                        most(b + 1)
                        subtract(b + 1)
                    output(b)
            quads(dv, step)


def program(nc, d):
    with ExitStack() as ctx:
        m = Memory(nc, ctx, "")
        k = {"ident": m.sb("ident", [P, P]), "powers": m.sb("powers", [P, 3]), "scales": m.sb("scales", [P, 4, KC, NB])}
        with ExitStack() as ctx2:
            m = Memory(nc, ctx2, "")
            k["head_mask"] = m.sb("head_mask", [P, 4, 32])
            k["pick_mask"] = m.sb("pick_mask", [KR, P])
            with ExitStack() as ctx3:
                m = Memory(nc, ctx3, "")
                for name, shape in (("temb", [P, DC, NB]), ("conv_w", [P, DC, 4]), ("conv_b", [P, DC]), ("bdt", [P, 1]), ("alog", [P, 1]),
                                    ("blockdt", [P, P]), ("wxg", [P, DC, NP]), ("fold", [P, 2, NP]),
                                    ("proj", [P, NB, NP]), ("stats", [P, NB, 4])):
                    k[name] = m.sb(name, shape)
                coefficients(nc, d, k)
                front(nc, d, k)
                projections(nc, d, k)
            scan(nc, d, k)
        back(nc, d, k)


def kernel(x, cond_2048, L0_cond_W_in, L0_cond_W_conv, L0_cond_b_conv, L0_cond_ln_g, L0_cond_ln_b, L0_cond_W_xproj, L0_cond_W_dt,
           L0_cond_b_dt, L0_cond_A_log, L0_cond_D, L0_cond_W_out, L1_cond_q_weight, L1_cond_k_weight, L1_cond_v_weight,
           L1_cond_w_weight, L1_cond_u_weight):
    import concourse.bacc as bacc
    import numpy as np
    from concourse.bass_utils import run_bass_kernel_spmd

    def chunked(a):
        a = np.asarray(a)
        return a.reshape(a.shape[0] // P, P, -1).transpose(1, 0, 2)

    x = np.asarray(x)
    block_dt = np.zeros((GB, NS, GB, NS), np.float32)
    head_mask = np.zeros((GB, NS, 4, GB, 4), np.float32)
    pick_mask = np.zeros((len(PAIRS), GB, GB, NS), np.float32)
    for b in range(GB):
        block_dt[b, :, b, :] = np.asarray(L0_cond_W_dt).T
        pick_mask[:, b, b] = 1.0
        for t in range(4):
            head_mask[b, :, t, b, t] = 1.0
    arrays = {
        "x": x,
        "xT": x.reshape(NQ, 4, S, KC, P).transpose(0, 4, 3, 1, 2).reshape(NQ, P, KC, 4 * S),
        "temb": chunked(np.asarray(cond_2048).T),
        "style_rows": cond_2048,
        "Win": chunked(np.asarray(L0_cond_W_in).T),
        "conv_w": chunked(np.asarray(L0_cond_W_conv).reshape(DI, 4)),
        "conv_b": np.asarray(L0_cond_b_conv).reshape(DC, P).T,
        "ln_g": np.asarray(L0_cond_ln_g).reshape(DC, P).T,
        "ln_b": np.asarray(L0_cond_ln_b).reshape(DC, P).T,
        "ln_g_row": np.asarray(L0_cond_ln_g).reshape(1, DI),
        "ln_b_row": np.asarray(L0_cond_ln_b).reshape(1, DI),
        "D_row": np.asarray(L0_cond_D).reshape(1, DI),
        "Wx": chunked(np.asarray(L0_cond_W_xproj).T),
        "W_dt": block_dt.reshape(P, P),
        "b_dt": np.tile(np.asarray(L0_cond_b_dt), GB).reshape(P, 1),
        "A_log": np.tile(np.asarray(L0_cond_A_log), GB).reshape(P, 1),
        "Wout": chunked(np.asarray(L0_cond_W_out).T),
        "Wq": chunked(np.asarray(L1_cond_q_weight).T),
        "Wk": chunked(np.asarray(L1_cond_k_weight).T),
        "Wv": chunked(np.asarray(L1_cond_v_weight).T),
        "Ww": chunked(np.asarray(L1_cond_w_weight).T),
        "Wu": chunked(np.asarray(L1_cond_u_weight).T),
        "ident": np.eye(P, dtype=np.float32),
        "head_mask": head_mask.reshape(P, 4, 32),
        "pick_mask": pick_mask.reshape(KR, P),
    }
    nc = bacc.Bacc("TRN2", target_bir_lowering=False, num_devices=1)
    fed, d = {}, {}
    for name, a in arrays.items():
        a = np.ascontiguousarray(a)
        fed[f"in_{name}"] = a
        d[name] = nc.dram_tensor(f"in_{name}", a.shape, mybir.dt.from_np(a.dtype), kind="ExternalInput").ap()
    d["xparts"] = nc.dram_tensor("xparts", (3, 2, NB, S, 512), BF16, kind="Internal").ap()
    d["bparts"] = nc.dram_tensor("bparts", (3, NG, S, P), BF16, kind="Internal").ap()
    d["chunks"] = nc.dram_tensor("chunks", (2, NTB, P, 2 * GH * TB), F32, kind="Internal").ap()
    d["dx"] = nc.dram_tensor("dx", (NB, S, DI), F32, kind="Internal").ap()
    d["y"] = nc.dram_tensor("y", (NB, S, DI), F32, kind="Internal").ap()
    d["out"] = nc.dram_tensor("out", (NB, S, D), F32, kind="ExternalOutput").ap()
    program(nc, d)
    result = run_bass_kernel_spmd(nc, [fed], core_ids=[0])
    return result.results[0]["out"]
```

```python
from contextlib import ExitStack

import concourse.bass as bass
from concourse import mybir

F32 = mybir.dt.float32
BF16 = mybir.dt.bfloat16
F32R = mybir.dt.float32r
ALU = mybir.AluOpType
ACT = mybir.ActivationFunctionType
AX_X = mybir.AxisListType.X

P = 128
NB, S, D, DI, NS = 64, 128, 512, 1024, 16
NP = 3 * NS
NQ = NB // 4
KC, DC = D // P, DI // P
GB = P // NS
NG = NB // GB
HALF = NB // 2
GH = NG // 2
TB = 8
NTB = S // TB
PAIRS = [(0, 0), (0, 1), (0, 2), (1, 0), (1, 1), (2, 0)]
KR = GB * len(PAIRS)
NH, HD = 16, 32
LN_EPS, DC_EPS = 1e-5, 1e-8
CLIP = 10.0


class Memory:

    def __init__(self, nc, ctx, prefix):
        self.nc, self.ctx, self.prefix = nc, ctx, prefix

    def sb(self, name, shape, dtype=F32):
        return self.ctx.enter_context(self.nc.sbuf_tensor(self.prefix + name, shape, dtype))

    def ps(self, name, shape):
        return self.ctx.enter_context(self.nc.psum_tensor(self.prefix + name, shape, F32))

    def sem(self, name):
        return self.ctx.enter_context(self.nc.semaphore(self.prefix + name))


def reached(engine, semaphore, value):
    if not (isinstance(value, int) and value <= 0):
        engine.wait_ge(semaphore, value)


def over(ap, shape):
    return ap.to_broadcast(shape)


def coefficients(nc, d, k):
    with ExitStack() as ctx:
        m = Memory(nc, ctx, "co_")
        weight = m.sb("weight", [P, 2, KC, D])
        squared = m.sb("squared", [P, KC, D])
        style = k["temb"]
        style_sq = m.sb("style_sq", [P, 2 * KC, NB])
        dc = m.sb("dc", [P, 5, KC, NB])
        wx = m.sb("wx", [P, DC, NP])
        wxb = m.sb("wxb", [P, DC, NP])
        lng, lnb = m.sb("lng", [P, DC]), m.sb("lnb", [P, DC])
        ones = m.sb("ones", [P, P])
        sums = [m.ps(f"sums{i}", [P, KC, NB]) for i in range(2)]
        fold = m.ps("fold", [P, 2, NP])
        loaded, w_loaded = m.sem("loaded"), [m.sem(f"w_loaded{i}") for i in range(2)]
        sq_ready, sums_ready, dc_rooted, dve = m.sem("sq_ready"), m.sem("sums_ready"), m.sem("dc_rooted"), m.sem("dve")
        style_ready, fold_ready, biased, sums_taken = m.sem("style_ready"), m.sem("fold_ready"), m.sem("biased"), m.sem("sums_taken")
        n_loads = 12
        block = ctx.enter_context(nc.Block())
        weights = [d["Wq"], d["Wk"], d["Wv"], d["Ww"], d["Wu"]]

        @block.sync
        def _(sp):
            for out, src in [(wx[:], d["Wx"]), (lng[:], d["ln_g"]), (lnb[:], d["ln_b"]),
                             (k["ident"][:], d["ident"]), (k["bdt"][:], d["b_dt"]), (k["alog"][:], d["A_log"]),
                             (k["blockdt"][:], d["W_dt"]),
                             (k["head_mask"][:], d["head_mask"]), (k["pick_mask"][:], d["pick_mask"]),
                             (k["conv_w"][:], d["conv_w"]), (k["conv_b"][:], d["conv_b"]),
                             (k["temb"][:], d["temb"])]:
                sp.dma_start(out, src).then_inc(loaded, 16)
            for i, w in enumerate(weights):
                reached(sp, sq_ready, i - 1)
                sp.dma_start(weight[:, i % 2], w).then_inc(w_loaded[i % 2], 16)

        @block.scalar
        def _(act):
            act.wait_ge(loaded, 16 * n_loads)
            nc.scalar.activation(style_sq[:], style[:], ACT.Square).then_inc(style_ready, 1)
            for i in range(5):
                act.wait_ge(w_loaded[i % 2], 16 * (i // 2 + 1))
                reached(act, sums_ready, i)
                nc.scalar.activation(squared[:], weight[:, i % 2], ACT.Square).then_inc(sq_ready, 1)
            act.wait_ge(biased, 5)
            nc.scalar.activation(dc[:], dc[:], ACT.Sqrt).then_inc(dc_rooted, 1)

        @block.tensor
        def _(pe):
            pe.wait_ge(style_ready, 1)
            for i in range(5):
                pe.wait_ge(sq_ready, i + 1)
                reached(pe, biased, i - 1)
                half = KC * (i >= 3)
                for o in range(KC):
                    for c in range(KC):
                        mm = pe.matmul(sums[i % 2][:, o], squared[:, c, o * P:(o + 1) * P], style_sq[:, half + c],
                                       start=c == 0, stop=c == KC - 1)
                mm.then_inc(sums_ready, 1)
            pe.wait_ge(dve, 3)
            for i, w in enumerate((k["wxg"], wxb)):
                for c in range(DC):
                    mm = pe.matmul(fold[:, i], ones[:], w[:, c], start=c == 0, stop=c == DC - 1)
            mm.then_inc(fold_ready, 1)

        @block.vector
        def _(dv):
            nc.vector.memset(ones[:], 1.0).then_inc(dve, 1)
            dv.wait_ge(loaded, 16 * n_loads)
            nc.vector.tensor_tensor(k["wxg"][:], wx[:], over(lng[:].unsqueeze(2), [P, DC, NP]), ALU.mult).then_inc(dve, 1)
            nc.vector.tensor_tensor(wxb[:], wx[:], over(lnb[:].unsqueeze(2), [P, DC, NP]), ALU.mult).then_inc(dve, 1)
            for i in range(5):
                dv.wait_ge(sums_ready, i + 1)
                nc.vector.tensor_scalar(dc[:, i], sums[i % 2][:], DC_EPS, None, ALU.add).then_inc(biased, 1)
            dv.wait_ge(fold_ready, 1)
            nc.vector.tensor_copy(k["fold"][:], fold[:]).then_inc(dve, 1)
            dv.wait_ge(dc_rooted, 1)
            nc.vector.reciprocal(dc[:], dc[:]).then_inc(dve, 1)
            dv.wait_ge(dve, 5)
            nc.vector.scalar_tensor_tensor(out=k["scales"][:, 0], in0=dc[:, 0], scalar=float(HD) ** -0.5,
                                           in1=dc[:, 1], op0=ALU.mult, op1=ALU.mult).then_inc(dve, 1)
            nc.vector.tensor_tensor(k["scales"][:, 1], dc[:, 2], style[:, KC:2 * KC], ALU.mult).then_inc(dve, 1)
            nc.vector.tensor_copy(k["scales"][:, 2:4], dc[:, 3:5]).then_inc(dve, 1)
            for i, value in enumerate((-0.5, 0.5, -1.0, 1.0)):
                nc.vector.memset(k["powers"][:, i:i + 1], value).then_inc(dve, 1)


def front(nc, d, k):
    with ExitStack() as ctx:
        m = Memory(nc, ctx, "fr_")
        win = m.sb("win", [P, KC, DI])
        xT = m.sb("xT", [P, 2, KC, 4 * S])
        padded = m.sb("padded", [P, 2, 4, S + 3])
        conv = m.sb("conv", [P, 2, 4, S])
        xc = m.sb("xc", [P, 2, DC, 4 * S])
        xn = m.sb("xn", [P, 2, DI])
        parts = m.sb("parts", [P, 2, 3, DI], BF16)
        rest = m.sb("rest", [P, 2, DI])
        dx = m.sb("dx", [P, 2, DI])
        rows = m.sb("rows", [P, 3, DI])
        bn = m.sb("bn", [P, 2, 2, 6])
        pause = m.sb("pause", [P, 1])
        moments = m.sb("moments", [P, 2, 2])
        var = m.sb("var", [P, 2, 1])
        squares = m.sb("squares", [P, DI])
        stats = m.sb("stats", [P, 2, 4, 4])
        xr_ps = [m.ps(f"xr_ps{i}", [P, 4, S]) for i in range(4)]
        nat_ps = m.ps("nat_ps", [P, DI])
        proj_ps = m.ps("proj_ps", [P, 4, 64])
        sem = m.sem
        consts, x_loaded = sem("consts"), [sem("x_loaded0"), sem("x_loaded1")]
        xr_ready, xp_ready, tap_ready, conv_step, conv_ready = sem("xr_ready"), sem("xp_ready"), sem("tap_ready"), sem("conv_step"), sem("conv_ready")
        silu_ready, nat_ready, proj_ready, proj_taken = sem("silu_ready"), sem("nat_ready"), sem("proj_ready"), sem("proj_taken")
        mom_step, mom_ready, rs_step, rs_ready, xhat_ready, xn_step, xn_ready = (sem("mom_step"), sem("mom_ready"), sem("rs_step"), sem("rs_ready"),
                                                              sem("xhat_ready"), sem("xn_step"), sem("xn_ready"))
        dx_ready, part1, rest1, part2, part3, sq_done = sem("dx_ready"), sem("part1"), sem("rest1"), sem("part2"), sem("part3"), sem("sq_done")
        parts_out, dx_out = [sem("parts_out0"), sem("parts_out1")], [sem("dx_out0"), sem("dx_out1")]
        taken, zeroed = sem("taken"), sem("zeroed")
        block = ctx.enter_context(nc.Block())

        def quads(engine, step):
            step(0, 0, True, False, False)
            step(1, 1, True, True, False)
            with engine.Fori(0, NQ // 2 - 2) as j:
                step(2 * j + 2, 0, True, True, True)
                step(2 * j + 3, 1, True, True, True)
            step(NQ - 2, 0, True, True, True)
            step(NQ - 1, 1, True, True, True)
            step(NQ, 0, False, True, True)


        @block.sync
        def _(sp):
            sp.dma_start(win[:], d["Win"][:, :, 0:DI]).then_inc(consts, 16)
            for i, name in enumerate(("ln_g_row", "ln_b_row", "D_row")):
                sp.dma_start(rows[:, i], over(d[name], [P, DI])).then_inc(consts, 16)
            sp.dma_start(xT[:, 0], d["xT"][0]).then_inc(x_loaded[0], 16)

            def store(b, par, slot):
                n = b
                sp.wait_ge(part3, n + 1)
                for i in range(3):
                    for h in range(2):
                        sp.dma_start(d["xparts"][i, h, bass.ds(b, 1)].rearrange("o t c -> (o t) c"),
                                     parts[:, par, i, h * 512:(h + 1) * 512]).then_inc(parts_out[par], 16)
                sp.wait_ge(dx_ready, n + 1)
                sp.dma_start(d["dx"][bass.ds(b, 1)].rearrange("o t c -> (o t) c"), dx[:, par]).then_inc(dx_out[par], 16)

            def step(q, par, main, nat, late):
                if main:
                    reached(sp, xr_ready, DC * q)
                    if not (isinstance(q, int) and q == NQ - 1):
                        sp.dma_start(xT[:, 1 - par], d["xT"][bass.ds(q + 1, 1)].rearrange("o p c n -> (o p) c n")).then_inc(x_loaded[1 - par], 16)
                for b in range(4):
                    if nat and (late or b > 0):
                        store(4 * q + b - 5, (b + 1) % 2, b)
            quads(sp, step)
            store(NB - 1, 1, 0)
            for par in range(2):
                sp.wait_ge(parts_out[par], 16 * 6 * NB // 2)
                sp.wait_ge(dx_out[par], 16 * NB // 2)

        @block.tensor
        def _(pe):
            pe.wait_ge(consts, 64)

            def inner(q, par, c):
                n = DC * q + c
                if c == 0:
                    pe.wait_ge(x_loaded[par], 8 * q + 16 if par == 0 else 8 * q + 8)
                reached(pe, xp_ready, n - 3)
                for i in range(KC):
                    mm = pe.matmul(xr_ps[c % 4][:].rearrange("p b t -> p (b t)"), win[:, i, c * P:(c + 1) * P], xT[:, par, i],
                                   start=i == 0, stop=i == KC - 1)
                mm.then_inc(xr_ready, 1)

            def natural(q, par, b):
                n = 4 * q + b
                if b == 0:
                    pe.wait_ge(silu_ready, DC * q + DC)
                reached(pe, xhat_ready, n)
                for c in range(DC):
                    mm = pe.transpose(nat_ps[:, c * P:(c + 1) * P], xc[:, par, c, b * S:(b + 1) * S], k["ident"][:])
                mm.then_inc(nat_ready, 1)
                if b == 0:
                    reached(pe, proj_taken, q)
                for c in range(DC):
                    mm = pe.matmul(proj_ps[:, b, 0:NP], xc[:, par, c, b * S:(b + 1) * S], k["wxg"][:, c],
                                   start=c == 0, stop=c == DC - 1)
                mm.then_inc(proj_ready, 1)

            def step(q, par, main, nat, late):
                for b in range(4):
                    if main:
                        inner(q, par, 2 * b)
                        inner(q, par, 2 * b + 1)
                    if nat:
                        natural(q - 1, 1 - par, b)
            quads(pe, step)

        @block.vector
        def _(dv):
            nc.vector.memset(padded[:], 0.0).then_inc(zeroed, 1)
            nc.vector.memset(stats[:], 0.0).then_inc(zeroed, 1)
            dv.wait_ge(zeroed, 2)

            def add_temb(q, par, c):
                n = DC * q + c
                dv.wait_ge(xr_ready, n + 1)
                reached(dv, conv_ready, n - 1)
                emb = k["temb"][:, c, bass.ds(4 * q, 4)].unsqueeze(2)
                nc.vector.tensor_tensor(padded[:, c % 2, :, 3:], xr_ps[c % 4][:], over(emb, [P, 4, S]),
                                        ALU.add).then_inc(xp_ready, 1)

            def taps(n, c):
                dv.wait_ge(tap_ready, n + 1)
                for i in range(1, 4):
                    if i > 1:
                        dv.wait_ge(conv_step, 2 * n + i - 1)
                    op = nc.vector.scalar_tensor_tensor(out=conv[:, c % 2], in0=padded[:, c % 2, :, i:i + S], scalar=k["conv_w"][:, c, i:i + 1],
                                                        in1=conv[:, c % 2], op0=ALU.mult, op1=ALU.add)
                    op.then_inc(conv_step if i < 3 else conv_ready, 1)

            def moment(n, b):
                u = b % 2
                dv.wait_ge(nat_ready, n + 1)
                reached(dv, rs_ready, n - 1)
                nc.vector.bn_stats(bn[:, u, 0], nat_ps[:, 0:512])
                nc.vector.bn_stats(bn[:, u, 1], nat_ps[:, 512:1024]).then_inc(mom_step, 1)
                dv.wait_ge(mom_step, 2 * n + 1)
                nc.vector.memset(pause[:], 0.0)
                nc.vector.bn_aggr(moments[:, u], bn[:, u].rearrange("p a b -> p (a b)")).then_inc(mom_step, 1)
                dv.wait_ge(mom_step, 2 * n + 2)
                nc.vector.tensor_scalar(var[:, u], moments[:, u, 1:2], LN_EPS, None, ALU.add).then_inc(mom_ready, 1)

            def split(n, par):
                dv.wait_ge(part1, n + 1)
                nc.vector.tensor_tensor(rest[:, par], xn[:, par], parts[:, par, 0], ALU.subtract).then_inc(rest1, 1)
                dv.wait_ge(part2, n + 1)
                nc.vector.tensor_tensor(parts[:, par, 2], rest[:, par], parts[:, par, 1], ALU.subtract).then_inc(part3, 1)

            def step(q, par, main, nat, late):
                for b in range(4):
                    for c in (2 * b, 2 * b + 1):
                        if main:
                            add_temb(q, par, c)
                        if (main or c == 0) and not (isinstance(q, int) and q == 0 and c == 0):
                            taps(DC * q + c - 1, (c - 1) % DC)
                    if nat:
                        moment(4 * q + b - 4, b)
                        if late or b > 0:
                            split(4 * q + b - 5, (b + 1) % 2)
                        if b == 0 and late:
                            dv.wait_ge(proj_ready, 4 * q - 4)
                            nc.vector.tensor_copy(k["proj"][:, bass.ds(4 * q - 8, 4)], proj_ps[:, :, 0:NP]).then_inc(proj_taken, 1)
                            dv.wait_ge(sq_done, 4 * q - 4)
                            nc.vector.tensor_copy(k["stats"][:, bass.ds(4 * q - 8, 4)], stats[:, par]).then_inc(taken, 1)
            quads(dv, step)
            split(NB - 1, 1)
            dv.wait_ge(proj_ready, NB)
            nc.vector.tensor_copy(k["proj"][:, NB - 4:NB], proj_ps[:, :, 0:NP]).then_inc(proj_taken, 1)
            dv.wait_ge(sq_done, NB)
            nc.vector.tensor_copy(k["stats"][:, NB - 4:NB], stats[:, 1]).then_inc(taken, 1)

        @block.scalar
        def _(act):
            def tap0(q, c):
                n = DC * q + c
                act.wait_ge(xp_ready, n + 1)
                reached(act, silu_ready, n - 1)
                nc.scalar.activation(conv[:, c % 2], padded[:, c % 2, :, 0:S], ACT.Identity, bias=k["conv_b"][:, c:c + 1],
                                     scale=k["conv_w"][:, c, 0:1]).then_inc(tap_ready, 1)

            def normalise(n, par, b):
                act.wait_ge(rs_ready, n + 1)
                reached(act, dx_ready, n - 1)
                reached(act, part3, n - 1)
                nc.scalar.activation(xn[:, b % 2], nat_ps[:], ACT.Identity, bias=stats[:, par, b, 1:2],
                                     scale=stats[:, par, b, 0:1]).then_inc(xhat_ready, 1)

            def split(n, par, spar, b):
                act.wait_ge(xn_ready, n + 1)
                reached(act, parts_out[par], 48 * n - 48 * par)
                nc.scalar.activation(parts[:, par, 0], xn[:, par], ACT.Copy).then_inc(part1, 1)
                reached(act, sq_done, n)
                nc.scalar.activation(squares[:], xn[:, par], ACT.Square, accum_out=stats[:, spar, b, 2:3]).then_inc(sq_done, 1)
                act.wait_ge(rest1, n + 1)
                nc.scalar.activation(parts[:, par, 1], rest[:, par], ACT.Copy).then_inc(part2, 1)

            def step(q, par, main, nat, late):
                for b in range(4):
                    for c in (2 * b, 2 * b + 1):
                        if main:
                            tap0(q, c)
                        if (main or c == 0) and not (isinstance(q, int) and q == 0 and c == 0):
                            n = DC * q + c - 1
                            act.wait_ge(conv_ready, n + 1)
                            sc = (c - 1) % DC
                            spar = par if c > 0 else 1 - par
                            if sc == 0:
                                reached(act, proj_ready, 4 * q - 4)
                            nc.scalar.activation(xc[:, spar, sc], conv[:, sc % 2].rearrange("p b t -> p (b t)"), ACT.Silu).then_inc(silu_ready, 1)
                    if nat:
                        if b == 0:
                            reached(act, taken, q - 2)
                        normalise(4 * q + b - 4, 1 - par, b)
                        if late or b > 0:
                            split(4 * q + b - 5, (b + 1) % 2, 1 - par if b > 0 else par, (b - 1) % 4)
            quads(act, step)
            split(NB - 1, 1, 1, 3)

        @block.gpsimd
        def _(pool):
            pool.wait_ge(consts, 64)

            def gains(n, u):
                pool.wait_ge(xhat_ready, n + 1)
                nc.gpsimd.tensor_tensor(xn[:, u], xn[:, u], rows[:, 0], ALU.mult).then_inc(xn_step, 1)
                pool.wait_ge(xn_step, n + 1)
                nc.gpsimd.tensor_tensor(xn[:, u], xn[:, u], rows[:, 1], ALU.add).then_inc(xn_ready, 1)
                pool.wait_ge(xn_ready, n + 1)
                reached(pool, dx_out[u], 8 * n - 8 * u)
                nc.gpsimd.tensor_tensor(dx[:, u], xn[:, u], rows[:, 2], ALU.mult).then_inc(dx_ready, 1)

            def step(q, par, main, nat, late):
                for b in range(4):
                    if nat:
                        n = 4 * q + b - 4
                        pool.wait_ge(mom_ready, n + 1)
                        if b == 0:
                            reached(pool, taken, q - 2)
                        nc.gpsimd.tensor_tensor(stats[:, 1 - par, b, 0:1], var[:, b % 2], k["powers"][:, 0:1], ALU.pow).then_inc(rs_step, 1)
                        pool.wait_ge(rs_step, 2 * n + 1)
                        nc.gpsimd.tensor_tensor(stats[:, 1 - par, b, 1:2], moments[:, b % 2, 0:1], stats[:, 1 - par, b, 0:1], ALU.mult).then_inc(rs_step, 1)
                        pool.wait_ge(rs_step, 2 * n + 2)
                        nc.gpsimd.tensor_tensor(stats[:, 1 - par, b, 1:2], stats[:, 1 - par, b, 1:2], k["powers"][:, 2:3], ALU.mult).then_inc(rs_ready, 1)
                        gains(n, b % 2)
            quads(pool, step)


def projections(nc, d, k):
    with ExitStack() as ctx:
        m = Memory(nc, ctx, "pr_")
        shift = m.sb("shift", [P, NB, NP])
        norm = m.sb("norm", [P, NB])
        half = m.sb("half", [P, NB])
        b_all = m.sb("b_all", [P, NB * NS])
        b_rest = m.sb("b_rest", [P, 2, NB * NS])
        b_parts = m.sb("b_parts", [P, 3, NB * NS], BF16)
        c_all = m.sb("c_all", [P, NB * NS])
        dt_all = m.sb("dt_all", [P, NB * NS])
        a = m.sb("a", [P, NG * S])
        zeros = m.sb("zeros", [P, S])
        run = m.sb("run", [P, NG * S])
        inverse = m.sb("inverse", [P, NG * S])
        chunks = m.sb("chunks", [P, 2, NTB, 3, GH, TB])
        minus_a = m.sb("minus_a", [P, 1])
        cT_ps, dtT_ps, dt_ps = m.ps("cT_ps", [P, NG * S]), m.ps("dtT_ps", [P, NG * S]), m.ps("dt_ps", [P, NG * S])
        inv_ps = m.ps("inv_ps", [P, NG * S])
        sem = m.sem
        dve, capped, rooted, tanh_a, b_out, turned_c, turned_dt = (sem("dve"), sem("capped"), sem("rooted"), sem("tanh_a"), sem("b_out"),
                                                                  sem("turned_c"), sem("turned_dt"))
        dtT_ready, dt_ready, tanh_ready, chunks_ready, chunk_out, split, natural = (sem("dtT_ready"), sem("dt_ready"), sem("tanh_ready"),
            sem("chunks_ready"), sem("chunk_out"), sem("split"), sem("natural"))
        inverse_ready, turned_inv = sem("inverse_ready"), sem("turned_inv")
        block = ctx.enter_context(nc.Block())
        proj, stats, fold = k["proj"], k["stats"], k["fold"]

        @block.vector
        def _(dv):
            done = 0

            def chained(op):
                nonlocal done
                done += 1
                op.then_inc(dve, 1)
                dv.wait_ge(dve, done)

            def blocks_of(g, kind):
                return chunks[:, g // GH, :, kind, g % GH]

            def row(tile, g):
                return tile[:, g * S:(g + 1) * S].rearrange("p (n t) -> p n t", t=TB)

            nc.vector.tensor_scalar(norm[:], stats[:, :, 2], 1.0, None, ALU.min).then_inc(capped, 1)
            chained(nc.vector.tensor_tensor(proj[:], proj[:], over(stats[:, :, 0:1], [P, NB, NP]), ALU.mult))
            chained(nc.vector.tensor_tensor(shift[:], over(stats[:, :, 1:2], [P, NB, NP]),
                                            over(fold[:, 0].unsqueeze(1), [P, NB, NP]), ALU.mult))
            chained(nc.vector.tensor_tensor(proj[:], proj[:], shift[:], ALU.add))
            chained(nc.vector.tensor_tensor(proj[:], proj[:], over(fold[:, 1].unsqueeze(1), [P, NB, NP]), ALU.add))
            nc.vector.tensor_copy(dt_all[:].rearrange("p (b s) -> p b s", s=NS), proj[:, :, 2 * NS:NP]).then_inc(natural, 1)
            nc.vector.tensor_copy(c_all[:].rearrange("p (b s) -> p b s", s=NS), proj[:, :, NS:2 * NS]).then_inc(natural, 1)
            chained(nc.vector.memset(zeros[:], 0.0))
            dv.wait_ge(turned_dt, 1)
            nc.vector.tensor_copy(a[:], dtT_ps[:]).then_inc(dtT_ready, 1)
            dv.wait_ge(rooted, 1)
            chained(nc.vector.tensor_tensor(b_all[:].rearrange("p (b s) -> p b s", s=NS), proj[:, :, 0:NS],
                                            over(half[:].unsqueeze(2), [P, NB, NS]), ALU.mult))
            dv.wait_ge(tanh_a, 1)
            chained(nc.vector.tensor_scalar(minus_a[:], k["alog"][:], -0.01, None, ALU.mult))
            dv.wait_ge(tanh_ready, 2)
            chained(nc.vector.tensor_scalar(a[:], a[:], minus_a[:], 1.0, ALU.mult, ALU.add))
            chained(nc.vector.memset(a[:].rearrange("p (g t) -> p g t", t=S)[:, :, 0:1], 1.0))
            for g in range(NG):
                op = nc.vector.tensor_tensor_scan(run[:, g * S:(g + 1) * S], a[:, g * S:(g + 1) * S], zeros[:], 1.0, ALU.mult, ALU.add)
            chained(op)
            nc.vector.reciprocal(inverse[:], run[:]).then_inc(inverse_ready, 1)
            dv.wait_ge(inverse_ready, 1)
            dv.wait_ge(turned_c, 1)
            for g in range(NG):
                nc.vector.tensor_tensor(blocks_of(g, 2), row(cT_ps, g), row(run, g), ALU.mult)
                nc.vector.tensor_scalar(blocks_of(g, 0), row(inverse, g), CLIP, None, ALU.mult)
                op = nc.vector.tensor_scalar(blocks_of(g, 1), row(inverse, g), -CLIP, None, ALU.mult)
            op.then_inc(chunks_ready, 1)
            dv.wait_ge(turned_inv, 1)
            chained(nc.vector.tensor_tensor(b_all[:], b_all[:], inv_ps[:], ALU.mult))
            for i in range(3):
                rest = b_all[:] if i == 0 else b_rest[:, i - 1]
                op = nc.vector.tensor_copy(b_parts[:, i], rest)
                if i == 2:
                    op.then_inc(split, 1)
                else:
                    chained(op)
                    chained(nc.vector.tensor_tensor(b_rest[:, i], rest, b_parts[:, i], ALU.subtract))

        @block.gpsimd
        def _(pool):
            pool.wait_ge(capped, 1)
            nc.gpsimd.tensor_tensor(half[:], norm[:], over(k["powers"][:, 1:2], [P, NB]), ALU.pow).then_inc(rooted, 1)

        @block.tensor
        def _(pe):
            def turn(src, ps, turned):
                for g in range(NG):
                    mm = pe.transpose(ps[:, g * P:(g + 1) * P], src[:, g * P:(g + 1) * P], k["ident"][:])
                mm.then_inc(turned, 1)

            pe.wait_ge(natural, 1)
            turn(dt_all, dtT_ps, turned_dt)
            pe.wait_ge(natural, 2)
            turn(c_all, cT_ps, turned_c)
            pe.wait_ge(dtT_ready, 1)
            for i in range(2):
                pe.matmul(dt_ps[:, i * 512:(i + 1) * 512], k["blockdt"][:], a[:, i * 512:(i + 1) * 512],
                          start=True, stop=True).then_inc(dt_ready, 1)
            pe.wait_ge(inverse_ready, 1)
            turn(inverse, inv_ps, turned_inv)

        @block.scalar
        def _(act):
            nc.scalar.activation(k["alog"][:], k["alog"][:], ACT.Tanh).then_inc(tanh_a, 1)
            act.wait_ge(dt_ready, 2)
            for i in range(2):
                nc.scalar.activation(a[:, i * 512:(i + 1) * 512], dt_ps[:, i * 512:(i + 1) * 512], ACT.Tanh,
                                     bias=k["bdt"][:]).then_inc(tanh_ready, 1)

        @block.sync
        def _(sp):
            sp.wait_ge(chunks_ready, 1)
            for h in range(2):
                sp.dma_start(d["chunks"][h].rearrange("n p c -> p n c"), chunks[:, h].rearrange("p n a g t -> p n (a g t)")).then_inc(chunk_out, 16)
            sp.wait_ge(split, 1)
            for i in range(3):
                sp.dma_start(d["bparts"][i].rearrange("g t c -> t g c"), b_parts[:, i].rearrange("t (g c) -> t g c", c=P)).then_inc(b_out, 16)
            sp.wait_ge(b_out, 48)
            sp.wait_ge(chunk_out, 32)


def scan(nc, d, k):
    with ExitStack() as ctx:
        m = Memory(nc, ctx, "sc_")
        x_rows = m.sb("x_rows", [KR, 2, GH, TB * 512], BF16)
        b_rows = m.sb("b_rows", [KR, 2, GH, TB, P], BF16)
        mask = m.sb("mask", [KR, P], BF16)
        kc = m.sb("kc", [P, 2, 3, GH, TB])
        c_cols = m.sb("c_cols", [P, 2, GH, TB, 32])
        state = m.sb("state", [P, 2, GH, 512])
        dx = m.sb("dx", [P, 2, 2, 512])
        y = m.sb("y", [P, 2, 512])
        w_high, w_low = (m.sb(n, [P, KC, DI], F32R) for n in ("w_high", "w_low"))
        x_raw = m.sb("x_raw", [P, KC, 4 * S])
        x_high, x_low = (m.sb(n, [P, KC, 4 * S], F32R) for n in ("x_high", "x_low"))
        gate = m.sb("gate", [P, 2, 4 * S])
        u_ps = [m.ps(f"u_ps{g}", [P, 512]) for g in range(GH)]
        y_ps = [m.ps(f"y_ps{i}", [P, 512]) for i in range(2)]
        gate_ps = [m.ps(f"gate_ps{i}", [P, 4 * S]) for i in range(2)]
        sem = m.sem
        x_loaded, b_loaded, kc_loaded, dx_loaded = ([sem(f"{n}{i}") for i in range(2)] for n in ("x_loaded", "b_loaded", "kc_loaded", "dx_loaded"))
        b_masked, c_ready, added, clipped, copied, y_done, y_added = (sem("b_masked"), sem("c_ready"), sem("added"),
            sem("clipped"), sem("copied"), sem("y_done"), sem("y_added"))
        y_out, gate_out = [sem("y_out0"), sem("y_out1")], [sem("gate_out0"), sem("gate_out1")]
        zeroed, mask_ready, w_loaded, w_split = sem("zeroed"), sem("mask_ready"), sem("w_loaded"), sem("w_split")
        raw_loaded, raw_copied, raw_split, gate_made, gate_done = sem("raw_loaded"), sem("raw_copied"), sem("raw_split"), sem("gate_made"), sem("gate_done")
        Y_BIAS, ADD_BIAS, OUT_BIAS, GATE_BIAS = TB + 1, 3, 16, 1
        UNROLL = 4
        block = ctx.enter_context(nc.Block())

        def passes(engine, step, start=None):
            for hb in range(2):
                with engine.Fori(0, 2) as dh:
                    if start is not None:
                        start(hb * 2 + dh)
                    with engine.Fori(0, NTB // UNROLL) as j:
                        for i in range(UNROLL):
                            step(hb, dh, j, i, hb * 2 * NTB + dh * NTB + UNROLL * j + i, hb * (NQ // 2) + dh * (NQ // 4) + j)

        def first_position(j, i):
            return UNROLL * TB * j + TB * i

        def same_parity(n, i):
            return n - i % 2

        @block.sync
        def _(sp):
            for c in range(KC):
                sp.dma_start(x_raw[:, c], d["Win"][:, c, DI:DI + 512]).then_inc(w_loaded, 16)
            for c in range(KC):
                if c == 0:
                    sp.wait_ge(w_split, 1)
                sp.dma_start(x_raw[:, c], d["Win"][:, c, DI + 512:2 * DI]).then_inc(w_loaded, 16)
            sp.wait_ge(w_split, 2)

            def step(hb, dh, j, i, n, q):
                par = i % 2
                sp.wait_ge(y_done, TB * n + 1)
                b0 = hb * HALF
                for r, (px, pb) in enumerate(PAIRS):
                    rows = slice(GB * r, GB * (r + 1))
                    src = d["xparts"][px, bass.ds(dh, 1), b0:b0 + HALF, bass.ds(first_position(j, i), TB)]
                    sp.dma_start(x_rows[rows, par], src.rearrange("o (g b) t c -> (o b) g (t c)", b=GB)).then_inc(x_loaded[par], 16)
                    src = d["bparts"][pb:pb + 1, hb * GH:(hb + 1) * GH, bass.ds(first_position(j, i), TB)]
                    sp.dma_start(b_rows[rows, par].rearrange("b g t c -> b g (t c)"),
                                 over(src.rearrange("o g t c -> o g (t c)"), [GB, GH, TB * P])).then_inc(b_loaded[par], 16)
                sp.dma_start(kc[:, par].rearrange("p a g t -> p (a g t)"),
                             d["chunks"][hb, bass.ds(UNROLL * j + i, 1)].rearrange("o p c -> (o p) c")).then_inc(kc_loaded[par], 16)
                if i == 0:
                    sp.wait_ge(raw_split, q + 1)
                    sp.dma_start(x_raw[:], d["xT"][bass.ds(q, 1)].rearrange("o p c n -> (o p) c n")).then_inc(raw_loaded, 16)
                sp.wait_ge(y_added, 2 * n + 1)
                for u in range(2):
                    src = d["dx"][b0:b0 + HALF, bass.ds(first_position(j, i) + 4 * u, 4), bass.ds(512 * dh, 512)]
                    sp.dma_start(dx[:, par, u], src).then_inc(dx_loaded[par], 16)
            passes(sp, step)

        @block.gpsimd
        def _(pool):
            pool.wait_ge(mask_ready, 1)

            def step(hb, dh, j, i, n, q):
                par = i % 2
                pool.wait_ge(b_loaded[par], 48 * same_parity(n, i) + 96)
                for g in range(GH):
                    op = nc.gpsimd.tensor_tensor(b_rows[:, par, g], b_rows[:, par, g], over(mask[:].unsqueeze(1), [KR, TB, P]), ALU.mult)
                op.then_inc(b_masked, 1)
                pool.wait_ge(kc_loaded[par], 8 * same_parity(n, i) + 16)
                pool.wait_ge(y_done, TB * n + 1)
                for g in range(GH):
                    for u in range(2):
                        op = nc.gpsimd.tensor_tensor(c_cols[:, par, g, 4 * u:4 * u + 4], k["head_mask"][:],
                                                     over(kc[:, par, 2, g, 4 * u:4 * u + 4].unsqueeze(2), [P, 4, 32]), ALU.mult)
                op.then_inc(c_ready, 1)
                if i == 0:
                    pool.wait_ge(raw_loaded, 16 * q + 16)
                    pool.wait_ge(gate_made, DC * q + GATE_BIAS)
                    nc.gpsimd.tensor_tensor(x_high[:].rearrange("p c n -> p (c n)"), x_raw[:].rearrange("p c n -> p (c n)"),
                                            over(k["powers"][:, 3:4], [P, KC * 4 * S]), ALU.mult).then_inc(raw_copied, 1)
                    pool.wait_ge(raw_copied, q + 1)
                    nc.gpsimd.tensor_tensor(x_low[:], x_raw[:], x_high[:].bitcast(F32), ALU.subtract).then_inc(raw_split, 1)
            passes(pool, step)

        @block.tensor
        def _(pe):
            def step(hb, dh, j, i, n, q):
                par = i % 2
                if i == 0:
                    pe.wait_ge(zeroed, hb * 2 + dh + 1)
                pe.wait_ge(x_loaded[par], 48 * same_parity(n, i) + 96)
                pe.wait_ge(b_masked, n + 1)

                def drive(t, g):
                    pe.wait_ge(copied, GH * TB * n + GH * t + g + 1)
                    pe.matmul(u_ps[g][:], b_rows[:, par, g, t], x_rows[:, par, g, t * 512:(t + 1) * 512],
                              start=False, stop=False, skip_group_check=True).then_inc(added, 1)

                def gate_part(t, g):
                    at = GH * (TB * i + t) + g
                    if at >= 12 * DC:
                        return
                    c, part = at // 12, at % 12
                    w, x = ((w_high, x_high), (w_low, x_high), (w_high, x_low))[part // KC]
                    if part == 0:
                        if c == 0:
                            pe.wait_ge(raw_split, q + 2)
                        pe.wait_ge(gate_done, DC * q + c + 1)
                    mm = pe.matmul(gate_ps[c % 2][:], w[:, part % KC, c * P:(c + 1) * P], x[:, part % KC], start=part == 0, stop=part == 11)
                    if part == 11:
                        mm.then_inc(gate_made, 1)

                def read(block_n, at_par, t):
                    if t == 0:
                        pe.wait_ge(c_ready, block_n + 1)
                    if t % 4 == 0:
                        pe.wait_ge(y_added, 2 * block_n + t // 4 + 2)
                    pe.wait_ge(copied, GH * TB * block_n + GH * (t + 1) + GH)
                    for g in range(GH):
                        mm = pe.matmul(y_ps[t // 4][32 * g:32 * g + 32, :], c_cols[:, at_par, g, t], state[:, t % 2, g],
                                       start=t % 4 == 0, stop=t % 4 == 3)
                    mm.then_inc(y_done, 1)

                for t in range(TB):
                    for g in range(GH):
                        drive(t, g)
                        gate_part(t, g)
                    if t > 0:
                        read(n, par, t - 1)
                    elif i > 0:
                        read(n - 1, 1 - par, TB - 1)
                if i == UNROLL - 1:
                    read(n, par, TB - 1)
            passes(pe, step)

        @block.vector
        def _(dv):
            nc.vector.memset(state[:, 0], 0.0).then_inc(y_done, Y_BIAS)
            nc.vector.memset(y[:], 0.0).then_inc(y_added, ADD_BIAS)
            nc.vector.memset(state[:, 1, 0], 0.0).then_inc(copied, GH)
            for u in range(2):
                nc.vector.memset(state[:, 1, 1 + u], 0.0).then_inc(y_out[u], OUT_BIAS)
                nc.vector.memset(gate[:, u], 0.0).then_inc(gate_out[u], OUT_BIAS)
            nc.vector.memset(state[:, 1, 3], 0.0).then_inc(gate_done, 2)
            nc.vector.tensor_copy(mask[:], k["pick_mask"][:]).then_inc(mask_ready, 1)
            for i in range(2):
                dv.wait_ge(w_loaded, 64 * (i + 1))
                cols = slice(512 * i, 512 * i + 512)
                nc.vector.tensor_copy(w_high[:, :, cols], x_raw[:]).then_inc(mask_ready, 1)
                dv.wait_ge(mask_ready, i + 2)
                nc.vector.tensor_tensor(w_low[:, :, cols], x_raw[:], w_high[:, :, cols].bitcast(F32), ALU.subtract).then_inc(w_split, 1)
            nc.vector.memset(dx[:, 0, 0], 0.0).then_inc(gate_made, GATE_BIAS)
            nc.vector.memset(dx[:, 0, 1], 0.0).then_inc(raw_split, 1)

            def start(n):
                dv.wait_ge(copied, GH * TB * NTB * n + GH)
                for g in range(GH):
                    op = nc.vector.memset(u_ps[g][:], 0.0)
                op.then_inc(zeroed, 1)

            def step(hb, dh, j, i, n, q):
                par = i % 2
                dv.wait_ge(kc_loaded[par], 8 * same_parity(n, i) + 16)

                def clip(t, g):
                    dv.wait_ge(added, GH * TB * n + GH * t + g + 1)
                    nc.vector.tensor_scalar(u_ps[g][:], u_ps[g][:], kc[:, par, 0, g, t:t + 1], kc[:, par, 1, g, t:t + 1],
                                            ALU.min, ALU.max).then_inc(clipped, 1)

                def add(block_n, at_par, u, jj):
                    dv.wait_ge(y_done, TB * block_n + 4 * u + 4 + Y_BIAS)
                    dv.wait_ge(dx_loaded[at_par], 16 * jj + 32)
                    dv.wait_ge(y_out[u], 16 * block_n + OUT_BIAS)
                    nc.vector.tensor_tensor(y[:, u], y_ps[u][:], dx[:, at_par, u], ALU.add).then_inc(y_added, 1)

                for t in range(TB):
                    for g in range(GH):
                        clip(t, g)
                        if g == 0 and t == 5:
                            add(n, par, 0, same_parity(n, i))
                        if g == 0 and t == 1 and i > 0:
                            add(n - 1, 1 - par, 1, same_parity(n - 1, i - 1))
                if i == UNROLL - 1:
                    add(n, par, 1, same_parity(n, i))
            passes(dv, step, start)

        @block.scalar
        def _(act):
            def step(hb, dh, j, i, n, q):
                b0 = hb * HALF

                def copy(t, g):
                    at = GH * TB * n + GH * t + g
                    act.wait_ge(clipped, at + 1)
                    if g == 0:
                        act.wait_ge(y_done, TB * n + t + Y_BIAS - 1)
                    nc.scalar.activation(state[:, t % 2, g], u_ps[g][:], ACT.Copy).then_inc(copied, 1)

                def store(block_n, position, u):
                    act.wait_ge(y_added, 2 * block_n + u + 1 + ADD_BIAS)
                    dst = d["y"][b0:b0 + HALF, bass.ds(position + 4 * u, 4), bass.ds(512 * dh, 512)]
                    act.dma_start(dst, y[:, u]).then_inc(y_out[u], 16)

                for t in range(TB):
                    for g in range(GH):
                        copy(t, g)
                    if t == 6:
                        store(n, first_position(j, i), 0)
                    if t == 2 and i > 0:
                        store(n - 1, first_position(j, i - 1), 1)
                    at = TB * i + t
                    if at % 3 == 2 and at // 3 < DC:
                        c = at // 3
                        act.wait_ge(gate_made, DC * q + c + 1 + GATE_BIAS)
                        act.wait_ge(gate_out[c % 2], 64 * q + 16 * (c // 2) + OUT_BIAS)
                        nc.scalar.activation(gate[:, c % 2], gate_ps[c % 2][:], ACT.Silu).then_inc(gate_done, 1)
                        act.wait_ge(gate_done, DC * q + c + 3)
                        act.dma_start(d["gate"][bass.ds(q, 1), :, c].rearrange("o p n -> (o p) n"), gate[:, c % 2]).then_inc(gate_out[c % 2], 16)
                if i == UNROLL - 1:
                    store(n, first_position(j, i), 1)
            passes(act, step)
            for u in range(2):
                act.wait_ge(y_out[u], 16 * 4 * NTB + OUT_BIAS)
                act.wait_ge(gate_out[u], 16 * NQ * DC // 2 + OUT_BIAS)


def back(nc, d, k):
    with ExitStack() as ctx:
        m = Memory(nc, ctx, "ba_")
        wout = m.sb("wout", [P, DC, D])
        wq, wk, wv, ww, wu = (m.sb(n, [P, KC, D]) for n in ("wq", "wk", "wv", "ww", "wu"))
        y = m.sb("y", [P, 4, DI])
        gate = m.sb("gate", [P, DC, 4 * S])
        z = m.sb("z", [P, DC, 4 * S])
        probs = z[:, 0:4]
        probsT = z[:, 4:8]
        x_in, style, xs = m.sb("x_in", [P, 2, D]), m.sb("style", [P, 2, D]), m.sb("xs", [P, 2, D])
        x2 = m.sb("x2", [P, 4, D])
        nT = m.sb("nT", [P, KC, 4 * S])
        qT, kT, vT, oT = (m.sb(n, [P, KC, 4 * S]) for n in ("qT", "kT", "vT", "oT"))
        v = m.sb("v", [P, 4, D])
        fu = m.sb("fu", [P, 4 * S])
        recip = m.sb("recip", [P, KC, S])
        result = m.sb("result", [P, 2, D])
        ones = m.sb("ones", [P, HD])
        scale = m.sb("scale", [P, 4, KC, 4])
        scale_wu = m.sb("scale_wu", [P, 2, KC, 4])
        bn, moments, var, norm = m.sb("bn", [P, 2, 6]), m.sb("moments", [P, 2, 2]), m.sb("var", [P, 2, 1]), m.sb("norm", [P, 2, 2])
        largest, pause = m.sb("largest", [P, 4, 4]), m.sb("pause", [P, 1])
        main = [m.ps(f"main{i}", [P, 512]) for i in range(2)]
        side = [m.ps(f"side{i}", [P, 4, S]) for i in range(2)]
        scores = m.ps("scores", [P, 4, 4, S])
        names = """consts y_loaded gate_loaded yT_ready z_done wo_ready x2_done xs_ready bn_step mom_ready
            rs_step rs_ready n_ready nT_ready nT_copied v_ready v_copied vT_ready vT_done q_ready q_done k_ready k_copied s_ready
            max_done sub_done exp_done pT_ready pT_copied o_ready rec_done o_done w_ready u_ready fw_done fu_done f_done fT_ready
            out_done scaled ones_ready""".split()
        s = {n: m.sem(n) for n in names}
        xin_loaded, style_loaded, stored = ([m.sem(f"{n}{i}") for i in range(2)] for n in ("xin_loaded", "style_loaded", "stored"))
        block = ctx.enter_context(nc.Block())

        def quads(engine, step):
            step(0, True, False)
            step(1, True, True)
            with engine.Fori(2, NQ) as q:
                step(q, True, True)
            step(NQ, False, True)

        def quad_slice(q):
            return bass.ds(4 * q, 4)

        @block.sync
        def _(sp):
            for w, name in ((wout, "Wout"), (wq, "Wq"), (wk, "Wk"), (wv, "Wv"), (ww, "Ww"), (wu, "Wu")):
                sp.dma_start(w[:], d[name]).then_inc(s["consts"], 16)

            def step(q, now, before):
                if now:
                    reached(sp, s["z_done"], DC * q)
                    sp.dma_start(gate[:], d["gate"][bass.ds(q, 1)].rearrange("o p c n -> (o p) c n")).then_inc(s["gate_loaded"], 16)
                    sp.dma_start(y[:], d["y"][quad_slice(q)].rearrange("b t c -> t b c")).then_inc(s["y_loaded"], 16)
                    for b in range(4):
                        reached(sp, s["x2_done"], 4 * q + b - 1)
                        sp.dma_start(x_in[:, b % 2], d["x"][bass.ds(4 * q + b, 1)].rearrange("o t c -> (o t) c")).then_inc(xin_loaded[b % 2], 16)
                        reached(sp, s["xs_ready"], 4 * q + b - 1)
                        sp.dma_start(style[:, b % 2], over(d["style_rows"][bass.ds(4 * q + b, 1), 0:D], [P, D])).then_inc(style_loaded[b % 2], 16)
            quads(sp, step)

        @block.gpsimd
        def _(pool):
            def step(q, now, before):
                if now:
                    for b in range(4):
                        n, u = 4 * q + b, b % 2
                        pool.wait_ge(s["mom_ready"], n + 1)
                        reached(pool, s["n_ready"], n - 1)
                        nc.gpsimd.tensor_tensor(norm[:, u, 0:1], var[:, u], k["powers"][:, 0:1], ALU.pow).then_inc(s["rs_step"], 1)
                        pool.wait_ge(s["rs_step"], 2 * n + 1)
                        nc.gpsimd.tensor_tensor(norm[:, u, 1:2], moments[:, u, 0:1], norm[:, u, 0:1], ALU.mult).then_inc(s["rs_step"], 1)
                        pool.wait_ge(s["rs_step"], 2 * n + 2)
                        nc.gpsimd.tensor_tensor(norm[:, u, 1:2], norm[:, u, 1:2], k["powers"][:, 2:3], ALU.mult).then_inc(s["rs_ready"], 1)
                if before:
                    for b in range(4):
                        pool.wait_ge(s["out_done"], 4 * q - 3 + b)
                        pool.dma_start(d["out"][bass.ds(4 * q - 4 + b, 1)].rearrange("o t c -> (o t) c"), result[:, b % 2]).then_inc(stored[b % 2], 16)
            def ordered(q, now, before):
                step(q, False, before)
                step(q, now, False)
            quads(pool, ordered)
            for u in range(2):
                pool.wait_ge(stored[u], 16 * NB // 2)

        @block.tensor
        def _(pe):
            pe.wait_ge(s["consts"], 16 * 6)
            pe.wait_ge(s["ones_ready"], 1)

            def products(out, lhs, rhs, sem, chunks=KC):
                for c in range(chunks):
                    mm = pe.matmul(out, lhs(c), rhs(c), start=c == 0, stop=c == chunks - 1)
                mm.then_inc(s[sem], 1)

            def turn_y(q, c):
                reached(pe, s["z_done"], DC * q + c - 1)
                for b in range(4):
                    mm = pe.transpose(side[c % 2][:, b], y[:, b, c * P:(c + 1) * P], k["ident"][:])
                mm.then_inc(s["yT_ready"], 1)

            def last_products(q):
                reached(pe, s["o_done"], 4 * q)
                for c in range(KC):
                    reached(pe, s["fw_done"], 4 * q - 4 + c)
                    products(main[0][:], lambda i: ww[:, i, c * P:(c + 1) * P], lambda i: oT[:, i], "w_ready")
                    reached(pe, s["fu_done"], 4 * q - 4 + c)
                    products(main[1][:], lambda i: wu[:, i, c * P:(c + 1) * P], lambda i: vT[:, i], "u_ready")
                pe.wait_ge(s["f_done"], 4 * q)
                for b in range(4):
                    reached(pe, s["out_done"], 4 * q - 4 + b - 1 if b >= 2 else 0)
                    for c in range(KC):
                        mm = pe.transpose(main[b % 2][:, c * P:(c + 1) * P], nT[:, c, b * S:(b + 1) * S], k["ident"][:])
                    mm.then_inc(s["fT_ready"], 1)

            def turn_norm(q, b):
                pe.wait_ge(s["n_ready"], 4 * q + b + 1)
                reached(pe, s["nT_copied"], 4 * q + b - 1 if b >= 2 else 0)
                for c in range(KC):
                    mm = pe.transpose(side[b % 2][:, c], xs[:, b % 2, c * P:(c + 1) * P], k["ident"][:])
                mm.then_inc(s["nT_ready"], 1)

            def v_rows(q, b):
                pe.wait_ge(s["nT_copied"], 4 * q + b + 1)
                if b < 2:
                    pe.wait_ge(s["x2_done"], 4 * q + b + 3)
                else:
                    pe.wait_ge(s["v_copied"], 4 * q + b - 1)
                products(main[b % 2][:], lambda i: nT[:, i, b * S:(b + 1) * S], lambda i: wv[:, i], "v_ready")

            def turn_v(q, b):
                pe.wait_ge(s["v_copied"], 4 * q + b + 1)
                for c in range(KC):
                    mm = pe.transpose(scores[:, b, c], v[:, b, c * P:(c + 1) * P], k["ident"][:])
                mm.then_inc(s["vT_ready"], 1)

            def q_chunk(q, c):
                reached(pe, s["v_copied"], 4 * q + 4)
                reached(pe, s["q_done"], 4 * q + c - 1 if c >= 2 else 0)
                products(main[c % 2][:], lambda i: wq[:, i, c * P:(c + 1) * P], lambda i: nT[:, i], "q_ready")

            def k_chunk(q, c):
                pe.wait_ge(s["q_done"], 4 * q + min(c, 1) + 3)
                reached(pe, s["k_copied"], 4 * q + c - 1 if c >= 2 else 0)
                products(main[c % 2][:], lambda i: wk[:, i, c * P:(c + 1) * P], lambda i: nT[:, i], "k_ready")

            def score(q, b):
                if b == 0:
                    pe.wait_ge(s["vT_done"], 4 * q + 4)
                    pe.wait_ge(s["k_copied"], 4 * q + 4)
                reached(pe, s["sub_done"], 4 * q + b)
                for i in range(4):
                    for j in range(4):
                        r = slice(32 * j, 32 * j + 32)
                        mm = pe.matmul(scores[:, j, i], qT[r, i, b * S:(b + 1) * S], kT[r, i, b * S:(b + 1) * S], start=True, stop=True)
                mm.then_inc(s["s_ready"], 1)

            def turn_probs(q, b):
                pe.wait_ge(s["exp_done"], 4 * q + b + 1)
                for i in range(4):
                    if not (b == 0 and i < 2):
                        pe.wait_ge(s["pT_copied"], 16 * q + 4 * b + i - 1)
                    for j in range(4):
                        mm = pe.transpose(main[i % 2][:, j * P:(j + 1) * P], probs[:, j, i * S:(i + 1) * S], k["ident"][:])
                    mm.then_inc(s["pT_ready"], 1)

            def mix(q, b):
                pe.wait_ge(s["pT_copied"], 16 * q + 4 * b + 4)
                if b == 0:
                    pe.wait_ge(s["nT_copied"], 4 * q + 4)
                else:
                    pe.wait_ge(s["o_done"], 4 * q + b)
                for i in range(4):
                    for out, lhs in ((side[0], None), (side[1], ones)):
                        for j in range(4):
                            h = 4 * i + j
                            mm = pe.matmul(out[32 * j:32 * j + 32, i], ones[:] if lhs is not None else v[:, b, h * HD:(h + 1) * HD],
                                           probsT[:, i, j * S:(j + 1) * S], start=True, stop=True)
                mm.then_inc(s["o_ready"], 1)

            def step(q, now, before):
                if now:
                    pe.wait_ge(s["y_loaded"], 16 * q + 16)
                    reached(pe, s["pT_copied"], 16 * q)
                    reached(pe, s["o_done"], 4 * q)
                    for c in range(DC):
                        turn_y(q, c)
                if before:
                    last_products(q)
                    pe.wait_ge(s["out_done"], 4 * q)
                if now:
                    pe.wait_ge(s["z_done"], DC * q + DC)
                    for b in range(4):
                        reached(pe, s["x2_done"], 4 * q + b - 1 if b >= 2 else 0)
                        products(main[b % 2][:], lambda i: z[:, i, b * S:(b + 1) * S], lambda i: wout[:, i], "wo_ready", DC)
                    turn_norm(q, 0)
                    turn_norm(q, 1)
                    v_rows(q, 0)
                    turn_norm(q, 2)
                    v_rows(q, 1)
                    turn_v(q, 0)
                    turn_norm(q, 3)
                    v_rows(q, 2)
                    turn_v(q, 1)
                    v_rows(q, 3)
                    turn_v(q, 2)
                    q_chunk(q, 0)
                    turn_v(q, 3)
                    for c in range(1, KC):
                        q_chunk(q, c)
                    for c in range(KC):
                        k_chunk(q, c)
                    score(q, 0)
                    for b in range(4):
                        if b < 3:
                            score(q, b + 1)
                        turn_probs(q, b)
                        mix(q, b)
            quads(pe, step)

        @block.scalar
        def _(act):
            def step(q, now, before):
                if not now:
                    return

                def normalise(b):
                    act.wait_ge(s["rs_ready"], 4 * q + b + 1)
                    nc.scalar.activation(xs[:, b % 2], xs[:, b % 2], ACT.Identity, bias=norm[:, b % 2, 1:2],
                                         scale=norm[:, b % 2, 0:1]).then_inc(s["n_ready"], 1)

                def copy_norm(b):
                    act.wait_ge(s["nT_ready"], 4 * q + b + 1)
                    if b == 0:
                        reached(act, s["fT_ready"], 4 * q)
                    nc.scalar.activation(nT[:, :, b * S:(b + 1) * S], side[b % 2][:], ACT.Copy).then_inc(s["nT_copied"], 1)

                def copy_v(b):
                    act.wait_ge(s["v_ready"], 4 * q + b + 1)
                    nc.scalar.activation(v[:, b], main[b % 2][:], ACT.Copy).then_inc(s["v_copied"], 1)

                normalise(0)
                normalise(1)
                copy_norm(0)
                normalise(2)
                copy_norm(1)
                normalise(3)
                copy_v(0)
                copy_norm(2)
                copy_v(1)
                copy_norm(3)
                copy_v(2)
                copy_v(3)
                for c in range(KC):
                    act.wait_ge(s["k_ready"], 4 * q + c + 1)
                    nc.scalar.activation(kT[:, c], main[c % 2][:], ACT.Copy).then_inc(s["k_copied"], 1)
                for b in range(4):
                    act.wait_ge(s["sub_done"], 4 * q + b + 1)
                    nc.scalar.activation(probs, probs, ACT.Exp).then_inc(s["exp_done"], 1)
                    for i in range(4):
                        act.wait_ge(s["pT_ready"], 16 * q + 4 * b + i + 1)
                        if i == 0:
                            reached(act, s["o_ready"], 4 * q + b)
                        nc.scalar.activation(probsT[:, i], main[i % 2][:], ACT.Copy).then_inc(s["pT_copied"], 1)
            quads(act, step)

        @block.vector
        def _(dv):
            nc.vector.memset(ones[:], 1.0).then_inc(s["ones_ready"], 1)

            def step(q, now, before):
                if before:
                    nc.vector.tensor_copy(scale_wu[:], k["scales"][:, 2:4, :, bass.ds(4 * q - 4, 4)]).then_inc(s["scaled"], 1)
                if now:
                    reached(dv, s["o_done"], 4 * q)
                    nc.vector.tensor_copy(scale[:, 0:2], k["scales"][:, 0:2, :, quad_slice(q)]).then_inc(s["scaled"], 1)
                    dv.wait_ge(s["gate_loaded"], 16 * q + 16)
                    for c in range(DC):
                        dv.wait_ge(s["yT_ready"], DC * q + c + 1)
                        if c == 0:
                            reached(dv, s["o_ready"], 4 * q)
                        nc.vector.tensor_tensor(z[:, c], side[c % 2][:].rearrange("p b t -> p (b t)"), gate[:, c], ALU.mult).then_inc(s["z_done"], 1)
                if before:
                    dv.wait_ge(s["scaled"], 2 * q)
                    for c in range(KC):
                        n = 4 * q - 4 + c
                        r = nT[:, c].rearrange("p (b t) -> p b t", b=4)
                        dv.wait_ge(s["w_ready"], n + 1)
                        nc.vector.tensor_tensor(r, main[0][:].rearrange("p (b t) -> p b t", b=4),
                                                over(scale_wu[:, 0, c].unsqueeze(2), [P, 4, S]), ALU.mult).then_inc(s["fw_done"], 1)
                        dv.wait_ge(s["u_ready"], n + 1)
                        reached(dv, s["f_done"], n)
                        nc.vector.tensor_tensor(fu[:].rearrange("p (b t) -> p b t", b=4), main[1][:].rearrange("p (b t) -> p b t", b=4),
                                                over(scale_wu[:, 1, c].unsqueeze(2), [P, 4, S]), ALU.mult).then_inc(s["fu_done"], 1)
                        dv.wait_ge(s["fu_done"], n + 1)
                        nc.vector.tensor_tensor(nT[:, c], nT[:, c], fu[:], ALU.add).then_inc(s["f_done"], 1)
                    for b in range(4):
                        n = 4 * q - 4 + b
                        dv.wait_ge(s["fT_ready"], n + 1)
                        reached(dv, stored[b % 2], 32 * (q - 1) + 16 * (b // 2))
                        nc.vector.tensor_tensor(result[:, b % 2], main[b % 2][:], x2[:, b], ALU.add).then_inc(s["out_done"], 1)
                if not now:
                    return
                for b in range(4):
                    n, u = 4 * q + b, b % 2
                    dv.wait_ge(s["wo_ready"], n + 1)
                    dv.wait_ge(xin_loaded[u], 32 * q + 16 * (b // 2) + 16)
                    nc.vector.tensor_tensor(x2[:, b], main[u][:], x_in[:, u], ALU.add).then_inc(s["x2_done"], 1)
                    dv.wait_ge(s["x2_done"], n + 1)
                    dv.wait_ge(style_loaded[u], 32 * q + 16 * (b // 2) + 16)
                    reached(dv, s["nT_ready"], n - 1)
                    nc.vector.tensor_tensor(xs[:, u], x2[:, b], style[:, u], ALU.mult).then_inc(s["xs_ready"], 1)
                    dv.wait_ge(s["xs_ready"], n + 1)
                    nc.vector.bn_stats(bn[:, u], xs[:, u]).then_inc(s["bn_step"], 1)
                    reached(dv, s["rs_ready"], n - 1)
                    dv.wait_ge(s["bn_step"], 2 * n + 1)
                    nc.vector.memset(pause[:], 0.0)
                    nc.vector.bn_aggr(moments[:, u], bn[:, u]).then_inc(s["bn_step"], 1)
                    dv.wait_ge(s["bn_step"], 2 * n + 2)
                    nc.vector.tensor_scalar(var[:, u], moments[:, u, 1:2], LN_EPS, None, ALU.add).then_inc(s["mom_ready"], 1)

                def scale_v(b):
                    dv.wait_ge(s["vT_ready"], 4 * q + b + 1)
                    nc.vector.tensor_tensor(vT[:, :, b * S:(b + 1) * S], scores[:, b], over(scale[:, 1, :, b:b + 1], [P, KC, S]),
                                            ALU.mult).then_inc(s["vT_done"], 1)

                def scale_q(c):
                    dv.wait_ge(s["q_ready"], 4 * q + c + 1)
                    nc.vector.tensor_tensor(qT[:, c].rearrange("p (b t) -> p b t", b=4), main[c % 2][:].rearrange("p (b t) -> p b t", b=4),
                                            over(scale[:, 0, c].unsqueeze(2), [P, 4, S]), ALU.mult).then_inc(s["q_done"], 1)

                dv.wait_ge(s["scaled"], 2 * q + 1)
                scale_v(0)
                scale_v(1)
                scale_v(2)
                scale_q(0)
                scale_v(3)
                for c in range(1, KC):
                    scale_q(c)

                def most(b):
                    dv.wait_ge(s["s_ready"], 4 * q + b + 1)
                    nc.vector.tensor_reduce(largest[:], scores[:], AX_X, ALU.max).then_inc(s["max_done"], 1)

                def subtract(b):
                    dv.wait_ge(s["max_done"], 4 * q + b + 1)
                    if b == 0:
                        dv.wait_ge(s["wo_ready"], 4 * q + 4)
                    else:
                        dv.wait_ge(s["pT_ready"], 16 * q + 4 * b)
                    nc.vector.tensor_tensor(probs.rearrange("p j (i t) -> p (j i) t", i=4), scores[:].rearrange("p j i t -> p (j i) t"),
                                            over(largest[:].rearrange("p j i -> p (j i)").unsqueeze(2), [P, 16, S]), ALU.subtract).then_inc(s["sub_done"], 1)

                def output(b):
                    n = 4 * q + b
                    dv.wait_ge(s["o_ready"], n + 1)
                    nc.vector.reciprocal(recip[:], side[1][:]).then_inc(s["rec_done"], 1)
                    dv.wait_ge(s["rec_done"], n + 1)
                    for i in range(KC):
                        op = nc.vector.scalar_tensor_tensor(out=oT[:, i, b * S:(b + 1) * S], in0=side[0][:, i], scalar=scale[:, 1, i, b:b + 1],
                                                            in1=recip[:, i], op0=ALU.mult, op1=ALU.mult)
                    op.then_inc(s["o_done"], 1)

                most(0)
                subtract(0)
                for b in range(4):
                    if b < 3:
                        most(b + 1)
                        subtract(b + 1)
                    output(b)
            quads(dv, step)


def program(nc, d):
    with ExitStack() as ctx:
        m = Memory(nc, ctx, "")
        k = {"ident": m.sb("ident", [P, P]), "powers": m.sb("powers", [P, 4]), "scales": m.sb("scales", [P, 4, KC, NB])}
        with ExitStack() as ctx2:
            m = Memory(nc, ctx2, "")
            k["head_mask"] = m.sb("head_mask", [P, 4, 32])
            k["pick_mask"] = m.sb("pick_mask", [KR, P])
            with ExitStack() as ctx3:
                m = Memory(nc, ctx3, "")
                for name, shape in (("temb", [P, DC, NB]), ("conv_w", [P, DC, 4]), ("conv_b", [P, DC]), ("bdt", [P, 1]), ("alog", [P, 1]),
                                    ("blockdt", [P, P]), ("wxg", [P, DC, NP]), ("fold", [P, 2, NP]),
                                    ("proj", [P, NB, NP]), ("stats", [P, NB, 4])):
                    k[name] = m.sb(name, shape)
                coefficients(nc, d, k)
                front(nc, d, k)
                projections(nc, d, k)
            scan(nc, d, k)
        back(nc, d, k)


def kernel(x, cond_2048, L0_cond_W_in, L0_cond_W_conv, L0_cond_b_conv, L0_cond_ln_g, L0_cond_ln_b, L0_cond_W_xproj, L0_cond_W_dt,
           L0_cond_b_dt, L0_cond_A_log, L0_cond_D, L0_cond_W_out, L1_cond_q_weight, L1_cond_k_weight, L1_cond_v_weight,
           L1_cond_w_weight, L1_cond_u_weight):
    import concourse.bacc as bacc
    import numpy as np
    from concourse.bass_utils import run_bass_kernel_spmd

    def chunked(a):
        a = np.asarray(a)
        return a.reshape(a.shape[0] // P, P, -1).transpose(1, 0, 2)

    x = np.asarray(x)
    block_dt = np.zeros((GB, NS, GB, NS), np.float32)
    head_mask = np.zeros((GB, NS, 4, GB, 4), np.float32)
    pick_mask = np.zeros((len(PAIRS), GB, GB, NS), np.float32)
    for b in range(GB):
        block_dt[b, :, b, :] = np.asarray(L0_cond_W_dt).T
        pick_mask[:, b, b] = 1.0
        for t in range(4):
            head_mask[b, :, t, b, t] = 1.0
    arrays = {
        "x": x,
        "xT": x.reshape(NQ, 4, S, KC, P).transpose(0, 4, 3, 1, 2).reshape(NQ, P, KC, 4 * S),
        "temb": chunked(np.asarray(cond_2048).T),
        "style_rows": cond_2048,
        "Win": chunked(np.asarray(L0_cond_W_in).T),
        "conv_w": chunked(np.asarray(L0_cond_W_conv).reshape(DI, 4)),
        "conv_b": np.asarray(L0_cond_b_conv).reshape(DC, P).T,
        "ln_g": np.asarray(L0_cond_ln_g).reshape(DC, P).T,
        "ln_b": np.asarray(L0_cond_ln_b).reshape(DC, P).T,
        "ln_g_row": np.asarray(L0_cond_ln_g).reshape(1, DI),
        "ln_b_row": np.asarray(L0_cond_ln_b).reshape(1, DI),
        "D_row": np.asarray(L0_cond_D).reshape(1, DI),
        "Wx": chunked(np.asarray(L0_cond_W_xproj).T),
        "W_dt": block_dt.reshape(P, P),
        "b_dt": np.tile(np.asarray(L0_cond_b_dt), GB).reshape(P, 1),
        "A_log": np.tile(np.asarray(L0_cond_A_log), GB).reshape(P, 1),
        "Wout": chunked(np.asarray(L0_cond_W_out).T),
        "Wq": chunked(np.asarray(L1_cond_q_weight).T),
        "Wk": chunked(np.asarray(L1_cond_k_weight).T),
        "Wv": chunked(np.asarray(L1_cond_v_weight).T),
        "Ww": chunked(np.asarray(L1_cond_w_weight).T),
        "Wu": chunked(np.asarray(L1_cond_u_weight).T),
        "ident": np.eye(P, dtype=np.float32),
        "head_mask": head_mask.reshape(P, 4, 32),
        "pick_mask": pick_mask.reshape(KR, P),
    }
    nc = bacc.Bacc("TRN2", target_bir_lowering=False, num_devices=1)
    fed, d = {}, {}
    for name, a in arrays.items():
        a = np.ascontiguousarray(a)
        fed[f"in_{name}"] = a
        d[name] = nc.dram_tensor(f"in_{name}", a.shape, mybir.dt.from_np(a.dtype), kind="ExternalInput").ap()
    d["xparts"] = nc.dram_tensor("xparts", (3, 2, NB, S, 512), BF16, kind="Internal").ap()
    d["bparts"] = nc.dram_tensor("bparts", (3, NG, S, P), BF16, kind="Internal").ap()
    d["chunks"] = nc.dram_tensor("chunks", (2, NTB, P, 3 * GH * TB), F32, kind="Internal").ap()
    d["dx"] = nc.dram_tensor("dx", (NB, S, DI), F32, kind="Internal").ap()
    d["gate"] = nc.dram_tensor("gate", (NQ, P, DC, 4 * S), F32, kind="Internal").ap()
    d["y"] = nc.dram_tensor("y", (NB, S, DI), F32, kind="Internal").ap()
    d["out"] = nc.dram_tensor("out", (NB, S, D), F32, kind="ExternalOutput").ap()
    program(nc, d)
    result = run_bass_kernel_spmd(nc, [fed], core_ids=[0])
    return result.results[0]["out"]
```

```python
from contextlib import ExitStack

import concourse.bass as bass
from concourse import mybir

F32 = mybir.dt.float32
BF16 = mybir.dt.bfloat16
F32R = mybir.dt.float32r
ALU = mybir.AluOpType
ACT = mybir.ActivationFunctionType
AX_X = mybir.AxisListType.X

P = 128
NB, S, D, DI, NS = 64, 128, 512, 1024, 16
NP = 3 * NS
NQ = NB // 4
KC, DC = D // P, DI // P
GB = P // NS
NG = NB // GB
HALF = NB // 2
GH = NG // 2
TB = 8
NTB = S // TB
PAIRS = [(0, 0), (0, 1), (0, 2), (1, 0), (1, 1), (2, 0)]
KR = GB * len(PAIRS)
NH, HD = 16, 32
LN_EPS, DC_EPS = 1e-5, 1e-8
CLIP = 10.0


class Memory:

    def __init__(self, nc, ctx, prefix):
        self.nc, self.ctx, self.prefix = nc, ctx, prefix

    def sb(self, name, shape, dtype=F32):
        return self.ctx.enter_context(self.nc.sbuf_tensor(self.prefix + name, shape, dtype))

    def twice(self, name, rounded_name, shape):
        with self.nc.sbuf_tensor(self.prefix + rounded_name, shape, F32R) as rounded:
            pass
        return self.sb(name, shape), rounded

    def ps(self, name, shape):
        return self.ctx.enter_context(self.nc.psum_tensor(self.prefix + name, shape, F32))

    def sem(self, name):
        return self.ctx.enter_context(self.nc.semaphore(self.prefix + name))


def reached(engine, semaphore, value):
    if not (isinstance(value, int) and value <= 0):
        engine.wait_ge(semaphore, value)


def over(ap, shape):
    return ap.to_broadcast(shape)


def coefficients(nc, d, k):
    with ExitStack() as ctx:
        m = Memory(nc, ctx, "co_")
        wx = m.sb("wx", [P, DC, NP])
        wxb = m.sb("wxb", [P, DC, NP])
        lng, lnb = m.sb("lng", [P, DC]), m.sb("lnb", [P, DC])
        ones = m.sb("ones", [P, P])
        fold = m.ps("fold", [P, 2, NP])
        loaded, later_loaded, ones_ready, wx_ready, fold_ready, dve = (m.sem(n) for n in ("loaded", "later_loaded", "ones_ready", "wx_ready", "fold_ready", "dve"))
        block = ctx.enter_context(nc.Block())
        later = [(k["win"][:], d["Win"][:, :, 0:DI]), (k["temb"][:], d["temb"]), (k["ident"][:], d["ident"]), (k["bdt"][:], d["b_dt"]),
                 (k["alog"][:], d["A_log"]), (k["blockdt"][:], d["W_dt"]), (k["head_mask"][:], d["head_mask"]),
                 (k["pick_mask"][:], d["pick_mask"]), (k["conv_w"][:], d["conv_w"]), (k["conv_b"][:], d["conv_b"])]

        @block.sync
        def _(sp):
            for out, src in [(wx[:], d["Wx"]), (lng[:], d["ln_g"]), (lnb[:], d["ln_b"])]:
                sp.dma_start(out, src).then_inc(loaded, 16)
            for out, src in later:
                sp.dma_start(out, src).then_inc(later_loaded, 16)
            sp.wait_ge(later_loaded, 16 * len(later))

        @block.tensor
        def _(pe):
            pe.wait_ge(ones_ready, 1)
            pe.wait_ge(wx_ready, 2)
            for i, w in enumerate((k["wxg"], wxb)):
                for c in range(DC):
                    mm = pe.matmul(fold[:, i], ones[:], w[:, c], start=c == 0, stop=c == DC - 1)
            mm.then_inc(fold_ready, 1)

        @block.vector
        def _(dv):
            nc.vector.memset(ones[:], 1.0).then_inc(ones_ready, 1)
            for i, value in enumerate((-0.5, 0.5, -1.0, 1.0)):
                nc.vector.memset(k["powers"][:, i:i + 1], value).then_inc(dve, 1)
            dv.wait_ge(loaded, 16 * 3)
            nc.vector.tensor_tensor(k["wxg"][:], wx[:], over(lng[:].unsqueeze(2), [P, DC, NP]), ALU.mult).then_inc(wx_ready, 1)
            nc.vector.tensor_tensor(wxb[:], wx[:], over(lnb[:].unsqueeze(2), [P, DC, NP]), ALU.mult).then_inc(wx_ready, 1)
            dv.wait_ge(fold_ready, 1)
            nc.vector.tensor_copy(k["fold"][:], fold[:]).then_inc(dve, 1)


def front(nc, d, k):
    with ExitStack() as ctx:
        m = Memory(nc, ctx, "fr_")
        win = k["win"]
        xT = m.sb("xT", [P, 2, KC, 4 * S])
        padded = m.sb("padded", [P, 2, 4, S + 3])
        conv = m.sb("conv", [P, 2, 4, S])
        xc = m.sb("xc", [P, 2, DC, 4 * S])
        xn = m.sb("xn", [P, 4, DI])
        parts = m.sb("parts", [P, 4, 3, DI], BF16)
        rest = m.sb("rest", [P, 2, DI])
        dx = m.sb("dx", [P, 2, DI])
        rows = m.sb("rows", [P, 3, DI])
        bn = m.sb("bn", [P, 2, 2, 6])
        pause = m.sb("pause", [P, 1])
        moments = m.sb("moments", [P, 2, 2])
        var = m.sb("var", [P, 2, 1])
        squares = m.sb("squares", [P, DI])
        second = xc[:, 1].rearrange("p a n -> p (a n)")
        w_high, w_low = (k[n][:].rearrange("p c n -> p (c n)") for n in ("w_high", "w_low"))
        stats = m.sb("stats", [P, 2, 4, 4])
        xr_ps = [m.ps(f"xr_ps{i}", [P, 4, S]) for i in range(3)]
        nat_ps = [m.ps(f"nat_ps{i}", [P, DI]) for i in range(2)]
        proj_ps = m.ps("proj_ps", [P, 4, 64])
        names = """consts xr_ready xp_ready tap_ready conv_step conv_ready silu_ready nat_ready proj_ready proj_taken
            mom_step mom_ready rs_step rs_ready xhat_ready xn_step xn_ready dx_ready part1 rest1 part2 part3 sq_done
            taken zeroed second_loaded high_ready low_ready""".split()
        s = {n: m.sem(n) for n in names}
        x_loaded, dx_out = ([m.sem(f"{n}{i}") for i in range(2)] for n in ("x_loaded", "dx_out"))
        parts_out = [m.sem(f"parts_out{i}") for i in range(4)]
        block = ctx.enter_context(nc.Block())

        def steps(engine, slot):
            def step(q, par):
                for b in range(4):
                    slot(q, par, b)
            for q in range(4):
                step(q, q % 2)
            with engine.Fori(2, NQ // 2 - 1) as j:
                step(2 * j, 0)
                step(2 * j + 1, 1)
            for q in range(NQ - 2, NQ + 1):
                step(q, q % 2)
            step(NQ + 1, 1)

        def is_main(q):
            return not isinstance(q, int) or q < NQ

        def lagged(q, par, b, lag):
            quad, place, p = (q - 1, b - lag, 1 - par) if b >= lag else (q - 2, b - lag + 4, par)
            if isinstance(q, int) and not 0 <= quad < NQ:
                return None
            return 4 * quad + place, quad, p, place

        def scaled_rows(engine, ops, n, quad, r):
            engine.wait_ge(s["xn_ready"], n + 1)
            reached(engine, s["dx_ready"], n)
            reached(engine, dx_out[r % 2], 16 * (2 * quad + r // 2))
            ops.tensor_tensor(dx[:, r % 2], xn[:, r], rows[:, 2], ALU.mult).then_inc(s["dx_ready"], 1)

        @block.sync
        def _(sp):
            sp.dma_start(xT[:, 0], d["xT"][0]).then_inc(x_loaded[0], 16)
            for i, name in enumerate(("ln_g_row", "ln_b_row", "D_row")):
                sp.dma_start(rows[:, i], over(d[name], [P, DI])).then_inc(s["consts"], 16)
            sp.dma_start(xc[:, 1].rearrange("p (c h) n -> p c (h n)", h=2), d["Win"][:, :, DI:2 * DI]).then_inc(s["second_loaded"], 16)

            def slot(q, par, b):
                if b == 0 and not (isinstance(q, int) and q >= NQ - 1):
                    reached(sp, s["xr_ready"], DC * q)
                    sp.dma_start(xT[:, 1 - par], d["xT"][bass.ds(q + 1, 1)].rearrange("o p c n -> (o p) c n")).then_inc(x_loaded[1 - par], 16)
                if lagged(q, par, b, 2):
                    n, quad, p, r = lagged(q, par, b, 2)
                    sp.wait_ge(s["dx_ready"], n + 1)
                    sp.dma_start(d["dx"][bass.ds(n, 1)].rearrange("o t c -> (o t) c"), dx[:, r % 2]).then_inc(dx_out[r % 2], 16)
                if lagged(q, par, b, 4):
                    n, quad, p, r = lagged(q, par, b, 4)
                    sp.wait_ge(s["part3"], n + 1)
                    for i in range(3):
                        for h in range(2):
                            sp.dma_start(d["xparts"][i, h, bass.ds(n, 1)].rearrange("o t c -> (o t) c"),
                                         parts[:, r, i, h * 512:(h + 1) * 512]).then_inc(parts_out[r], 16)
            steps(sp, slot)
            for r in range(4):
                sp.wait_ge(parts_out[r], 96 * NQ)
            for u in range(2):
                sp.wait_ge(dx_out[u], 16 * NB // 2)

        @block.tensor
        def _(pe):
            def inner(q, par, c):
                n = DC * q + c
                if c == 0:
                    pe.wait_ge(x_loaded[par], 8 * q + 16 if par == 0 else 8 * q + 8)
                reached(pe, s["xp_ready"], n - 1 if c < 2 else n - 4 if c == 2 else n - 2)
                for i in range(KC):
                    mm = pe.matmul(xr_ps[c % 3][:].rearrange("p b t -> p (b t)"), win[:, i, c * P:(c + 1) * P], xT[:, par, i],
                                   start=i == 0, stop=i == KC - 1)
                mm.then_inc(s["xr_ready"], 1)

            def natural(n, quad, p, b):
                if b == 0:
                    pe.wait_ge(s["silu_ready"], DC * quad + DC)
                reached(pe, s["xhat_ready"], n - 1)
                for c in range(DC):
                    mm = pe.transpose(nat_ps[b % 2][:, c * P:(c + 1) * P], xc[:, p, c, b * S:(b + 1) * S], k["ident"][:])
                mm.then_inc(s["nat_ready"], 1)
                if b == 0:
                    reached(pe, s["proj_taken"], quad)
                for c in range(DC):
                    mm = pe.matmul(proj_ps[:, b, 0:NP], xc[:, p, c, b * S:(b + 1) * S], k["wxg"][:, c],
                                   start=c == 0, stop=c == DC - 1)
                mm.then_inc(s["proj_ready"], 1)

            def slot(q, par, b):
                if is_main(q):
                    inner(q, par, 2 * b)
                    inner(q, par, 2 * b + 1)
                if lagged(q, par, b, 1):
                    natural(*lagged(q, par, b, 1))
            steps(pe, slot)

        @block.vector
        def _(dv):
            nc.vector.memset(padded[:], 0.0).then_inc(s["zeroed"], 1)
            nc.vector.memset(stats[:], 0.0).then_inc(s["zeroed"], 1)
            dv.wait_ge(s["zeroed"], 2)

            def add_temb(q, par, c):
                n = DC * q + c
                dv.wait_ge(s["xr_ready"], n + 1)
                reached(dv, s["conv_ready"], n - 1)
                emb = k["temb"][:, c, bass.ds(4 * q, 4)].unsqueeze(2)
                nc.vector.tensor_tensor(padded[:, c % 2, :, 3:], xr_ps[c % 3][:], over(emb, [P, 4, S]),
                                        ALU.add).then_inc(s["xp_ready"], 1)

            def taps(n, c):
                dv.wait_ge(s["tap_ready"], n + 1)
                for i in range(1, 4):
                    if i > 1:
                        dv.wait_ge(s["conv_step"], 2 * n + i - 1)
                    op = nc.vector.scalar_tensor_tensor(out=conv[:, c % 2], in0=padded[:, c % 2, :, i:i + S], scalar=k["conv_w"][:, c, i:i + 1],
                                                        in1=conv[:, c % 2], op0=ALU.mult, op1=ALU.add)
                    op.then_inc(s["conv_step" if i < 3 else "conv_ready"], 1)

            def moment(n, quad, p, r):
                u = r % 2
                dv.wait_ge(s["nat_ready"], n + 1)
                reached(dv, s["rs_ready"], n - 1)
                nc.vector.bn_stats(bn[:, u, 0], nat_ps[u][:, 0:512])
                nc.vector.bn_stats(bn[:, u, 1], nat_ps[u][:, 512:1024]).then_inc(s["mom_step"], 1)
                dv.wait_ge(s["mom_step"], 2 * n + 1)
                nc.vector.memset(pause[:], 0.0)
                nc.vector.bn_aggr(moments[:, u], bn[:, u].rearrange("p a b -> p (a b)")).then_inc(s["mom_step"], 1)
                dv.wait_ge(s["mom_step"], 2 * n + 2)
                nc.vector.tensor_scalar(var[:, u], moments[:, u, 1:2], LN_EPS, None, ALU.add).then_inc(s["mom_ready"], 1)

            def cut_rest(n, quad, p, r):
                dv.wait_ge(s["part1"], n + 1)
                reached(dv, s["part3"], n - 1)
                nc.vector.tensor_tensor(rest[:, r % 2], xn[:, r], parts[:, r, 0], ALU.subtract).then_inc(s["rest1"], 1)

            def cut_third(n, quad, p, r):
                dv.wait_ge(s["part2"], n + 1)
                nc.vector.tensor_tensor(parts[:, r, 2], rest[:, r % 2], parts[:, r, 1], ALU.subtract).then_inc(s["part3"], 1)

            def slot(q, par, b):
                older = lagged(q, par, 0, 4)
                for c in (2 * b, 2 * b + 1):
                    if is_main(q):
                        add_temb(q, par, c)
                    n = DC * q + c - 1
                    if not isinstance(n, int) or 0 <= n < DC * NQ:
                        taps(n, (c - 1) % DC)
                if lagged(q, par, b, 3):
                    cut_rest(*lagged(q, par, b, 3))
                if lagged(q, par, b, 1):
                    moment(*lagged(q, par, b, 1))
                if lagged(q, par, b, 4):
                    cut_third(*lagged(q, par, b, 4))
                if lagged(q, par, b, 2) and not is_main(q):
                    n, quad, p, r = lagged(q, par, b, 2)
                    scaled_rows(dv, nc.vector, n, quad, r)
                if b == 0 and older:
                    dv.wait_ge(s["proj_ready"], older[0] + 4)
                    nc.vector.tensor_copy(k["proj"][:, bass.ds(older[0], 4)], proj_ps[:, :, 0:NP]).then_inc(s["proj_taken"], 1)
                if b == 3 and older:
                    dv.wait_ge(s["sq_done"], older[0] + 4)
                    nc.vector.tensor_copy(k["stats"][:, bass.ds(older[0], 4)], stats[:, par]).then_inc(s["taken"], 1)
            steps(dv, slot)

        @block.scalar
        def _(act):
            def tap0(q, c):
                n = DC * q + c
                act.wait_ge(s["xp_ready"], n + 1)
                reached(act, s["silu_ready"], n - 1)
                nc.scalar.activation(conv[:, c % 2], padded[:, c % 2, :, 0:S], ACT.Identity, bias=k["conv_b"][:, c:c + 1],
                                     scale=k["conv_w"][:, c, 0:1]).then_inc(s["tap_ready"], 1)

            def silu(q, par, c):
                n = DC * q + c - 1
                if isinstance(n, int) and not 0 <= n < DC * NQ:
                    return
                act.wait_ge(s["conv_ready"], n + 1)
                sc = (c - 1) % DC
                if isinstance(n, int) and n == DC:
                    act.wait_ge(s["low_ready"], 1)
                if sc == 0:
                    reached(act, s["proj_ready"], 4 * q - 4)
                nc.scalar.activation(xc[:, par if c > 0 else 1 - par, sc], conv[:, sc % 2].rearrange("p b t -> p (b t)"), ACT.Silu).then_inc(s["silu_ready"], 1)

            def normalise(n, quad, p, r):
                act.wait_ge(s["rs_ready"], n + 1)
                reached(act, s["dx_ready"], n - 3)
                reached(act, s["rest1"], n - 3)
                reached(act, s["sq_done"], n - 3)
                nc.scalar.activation(xn[:, r], nat_ps[r % 2][:], ACT.Identity, bias=stats[:, p, r, 1:2],
                                     scale=stats[:, p, r, 0:1]).then_inc(s["xhat_ready"], 1)

            def cut_first(n, quad, p, r):
                act.wait_ge(s["xn_ready"], n + 1)
                reached(act, parts_out[r], 96 * quad)
                nc.scalar.activation(parts[:, r, 0], xn[:, r], ACT.Copy).then_inc(s["part1"], 1)

            def square(n, quad, p, r):
                reached(act, s["sq_done"], n)
                nc.scalar.activation(squares[:], xn[:, r], ACT.Square, accum_out=stats[:, p, r, 2:3]).then_inc(s["sq_done"], 1)

            def cut_second(n, quad, p, r):
                act.wait_ge(s["rest1"], n + 1)
                nc.scalar.activation(parts[:, r, 1], rest[:, r % 2], ACT.Copy).then_inc(s["part2"], 1)

            def slot(q, par, b):
                if lagged(q, par, b, 2):
                    normalise(*lagged(q, par, b, 2))
                if lagged(q, par, b, 4):
                    cut_second(*lagged(q, par, b, 4))
                if is_main(q):
                    tap0(q, 2 * b)
                if lagged(q, par, b, 3):
                    cut_first(*lagged(q, par, b, 3))
                silu(q, par, 2 * b)
                if is_main(q):
                    tap0(q, 2 * b + 1)
                if lagged(q, par, b, 3):
                    square(*lagged(q, par, b, 3))
                silu(q, par, 2 * b + 1)
                if isinstance(q, int) and q == 0 and b == 1:
                    act.wait_ge(s["second_loaded"], 16)
                    nc.scalar.activation(w_high, second, ACT.Copy).then_inc(s["high_ready"], 1)
            steps(act, slot)

        @block.gpsimd
        def _(pool):
            pool.wait_ge(s["high_ready"], 1)
            nc.gpsimd.tensor_tensor(w_low, second, w_high.bitcast(F32), ALU.subtract).then_inc(s["low_ready"], 1)
            pool.wait_ge(s["consts"], 48)

            def gains(n, quad, p, r, in_tail):
                pool.wait_ge(s["xhat_ready"], n + 1)
                nc.gpsimd.tensor_tensor(xn[:, r], xn[:, r], rows[:, 0], ALU.mult).then_inc(s["xn_step"], 1)
                pool.wait_ge(s["xn_step"], n + 1)
                nc.gpsimd.tensor_tensor(xn[:, r], xn[:, r], rows[:, 1], ALU.add).then_inc(s["xn_ready"], 1)
                if not in_tail:
                    scaled_rows(pool, nc.gpsimd, n, quad, r)

            def root(n, quad, p, r):
                u = r % 2
                pool.wait_ge(s["mom_ready"], n + 1)
                if r == 0:
                    reached(pool, s["taken"], quad - 1)
                nc.gpsimd.tensor_tensor(stats[:, p, r, 0:1], var[:, u], k["powers"][:, 0:1], ALU.pow).then_inc(s["rs_step"], 1)
                pool.wait_ge(s["rs_step"], 2 * n + 1)
                nc.gpsimd.tensor_tensor(stats[:, p, r, 1:2], moments[:, u, 0:1], stats[:, p, r, 0:1], ALU.mult).then_inc(s["rs_step"], 1)
                pool.wait_ge(s["rs_step"], 2 * n + 2)
                nc.gpsimd.tensor_tensor(stats[:, p, r, 1:2], stats[:, p, r, 1:2], k["powers"][:, 2:3], ALU.mult).then_inc(s["rs_ready"], 1)

            def slot(q, par, b):
                if is_main(q):
                    if lagged(q, par, b, 2):
                        gains(*lagged(q, par, b, 2), False)
                    if lagged(q, par, b, 1):
                        root(*lagged(q, par, b, 1))
                    return
                if lagged(q, par, b, 1):
                    root(*lagged(q, par, b, 1))
                if lagged(q, par, b, 2):
                    gains(*lagged(q, par, b, 2), True)
            steps(pool, slot)


def projections(nc, d, k):
    with ExitStack() as ctx:
        m = Memory(nc, ctx, "pr_")
        shift = m.sb("shift", [P, NB, NP])
        norm = m.sb("norm", [P, NB])
        half = m.sb("half", [P, NB])
        b_all = m.sb("b_all", [P, NB * NS])
        b_rest = m.sb("b_rest", [P, 2, NB * NS])
        b_parts = m.sb("b_parts", [P, 3, NB * NS], BF16)
        c_all = m.sb("c_all", [P, NB * NS])
        dt_all = m.sb("dt_all", [P, NB * NS])
        a = m.sb("a", [P, NG * S])
        zeros = m.sb("zeros", [P, S])
        run = m.sb("run", [P, NG * S])
        inverse = m.sb("inverse", [P, NG * S])
        chunks = m.sb("chunks", [P, 2, NTB, 3, GH, TB])
        minus_a = m.sb("minus_a", [P, 1])
        cT_ps, dtT_ps, dt_ps = m.ps("cT_ps", [P, NG * S]), m.ps("dtT_ps", [P, NG * S]), m.ps("dt_ps", [P, NG * S])
        inv_ps = dtT_ps
        weight = m.sb("weight", [P, 5, KC, D])
        squared = m.sb("squared", [P, 2, KC, D])
        style = k["temb"]
        style_sq = m.sb("style_sq", [P, 2 * KC, NB])
        dc = m.sb("dc", [P, 5, KC, NB])
        sums = [m.ps(f"sums{i}", [P, KC, NB]) for i in range(2)]
        w_loaded = [m.sem(f"w_loaded{i}") for i in range(5)]
        style_ready, sq_ready, sums_ready, biased, dc_ready, scales_ready = (m.sem(n) for n in
            ("style_ready", "sq_ready", "sums_ready", "biased", "dc_ready", "scales_ready"))
        sem = m.sem
        dve, capped, rooted, tanh_a, b_out, turned_c, turned_dt = (sem("dve"), sem("capped"), sem("rooted"), sem("tanh_a"), sem("b_out"),
                                                                  sem("turned_c"), sem("turned_dt"))
        dtT_ready, dt_ready, tanh_ready, chunks_ready, chunk_out, split, natural = (sem("dtT_ready"), sem("dt_ready"), sem("tanh_ready"),
            sem("chunks_ready"), sem("chunk_out"), sem("split"), sem("natural"))
        inverse_ready, turned_inv = sem("inverse_ready"), sem("turned_inv")
        block = ctx.enter_context(nc.Block())
        proj, stats, fold = k["proj"], k["stats"], k["fold"]

        @block.vector
        def _(dv):
            done = 0

            def chained(op):
                nonlocal done
                done += 1
                op.then_inc(dve, 1)
                dv.wait_ge(dve, done)

            def blocks_of(g, kind):
                return chunks[:, g // GH, :, kind, g % GH]

            def row(tile, g):
                return tile[:, g * S:(g + 1) * S].rearrange("p (n t) -> p n t", t=TB)

            nc.vector.tensor_scalar(norm[:], stats[:, :, 2], 1.0, None, ALU.min).then_inc(capped, 1)
            chained(nc.vector.tensor_tensor(proj[:], proj[:], over(stats[:, :, 0:1], [P, NB, NP]), ALU.mult))
            chained(nc.vector.tensor_tensor(shift[:], over(stats[:, :, 1:2], [P, NB, NP]),
                                            over(fold[:, 0].unsqueeze(1), [P, NB, NP]), ALU.mult))
            chained(nc.vector.tensor_tensor(proj[:], proj[:], shift[:], ALU.add))
            chained(nc.vector.tensor_tensor(proj[:], proj[:], over(fold[:, 1].unsqueeze(1), [P, NB, NP]), ALU.add))
            nc.vector.tensor_copy(dt_all[:].rearrange("p (b s) -> p b s", s=NS), proj[:, :, 2 * NS:NP]).then_inc(natural, 1)
            nc.vector.tensor_copy(c_all[:].rearrange("p (b s) -> p b s", s=NS), proj[:, :, NS:2 * NS]).then_inc(natural, 1)
            chained(nc.vector.memset(zeros[:], 0.0))

            def bias(i):
                dv.wait_ge(sums_ready, i + 1)
                nc.vector.tensor_scalar(dc[:, i], sums[i % 2][:], DC_EPS, None, ALU.add).then_inc(biased, 1)

            dv.wait_ge(turned_dt, 1)
            nc.vector.tensor_copy(a[:], dtT_ps[:]).then_inc(dtT_ready, 1)
            dv.wait_ge(rooted, 1)
            chained(nc.vector.tensor_tensor(b_all[:].rearrange("p (b s) -> p b s", s=NS), proj[:, :, 0:NS],
                                            over(half[:].unsqueeze(2), [P, NB, NS]), ALU.mult))
            dv.wait_ge(tanh_a, 1)
            chained(nc.vector.tensor_scalar(minus_a[:], k["alog"][:], -0.01, None, ALU.mult))
            dv.wait_ge(tanh_ready, 2)
            chained(nc.vector.tensor_scalar(a[:], a[:], minus_a[:], 1.0, ALU.mult, ALU.add))
            chained(nc.vector.memset(a[:].rearrange("p (g t) -> p g t", t=S)[:, :, 0:1], 1.0))
            for g in range(NG):
                op = nc.vector.tensor_tensor_scan(run[:, g * S:(g + 1) * S], a[:, g * S:(g + 1) * S], zeros[:], 1.0, ALU.mult, ALU.add)
            chained(op)
            bias(0)
            nc.vector.reciprocal(inverse[:], run[:]).then_inc(inverse_ready, 1)
            dv.wait_ge(inverse_ready, 1)
            dv.wait_ge(turned_c, 1)
            for g in range(NG):
                nc.vector.tensor_tensor(blocks_of(g, 2), row(cT_ps, g), row(run, g), ALU.mult)
                nc.vector.tensor_scalar(blocks_of(g, 0), row(inverse, g), CLIP, None, ALU.mult)
                op = nc.vector.tensor_scalar(blocks_of(g, 1), row(inverse, g), -CLIP, None, ALU.mult)
            op.then_inc(chunks_ready, 1)
            bias(1)
            bias(2)
            dv.wait_ge(turned_inv, 1)
            chained(nc.vector.tensor_tensor(b_all[:], b_all[:], inv_ps[:], ALU.mult))
            for i in range(3):
                rest = b_all[:] if i == 0 else b_rest[:, i - 1]
                op = nc.vector.tensor_copy(b_parts[:, i], rest)
                if i == 2:
                    op.then_inc(split, 1)
                else:
                    chained(op)
                    chained(nc.vector.tensor_tensor(b_rest[:, i], rest, b_parts[:, i], ALU.subtract))
            bias(3)
            bias(4)
            dv.wait_ge(dc_ready, 1)
            chained(nc.vector.reciprocal(dc[:], dc[:]))
            nc.vector.scalar_tensor_tensor(out=k["scales"][:, 0], in0=dc[:, 0], scalar=float(HD) ** -0.5,
                                           in1=dc[:, 1], op0=ALU.mult, op1=ALU.mult).then_inc(scales_ready, 1)
            nc.vector.tensor_tensor(k["scales"][:, 1], dc[:, 2], style[:, KC:2 * KC], ALU.mult).then_inc(scales_ready, 1)
            nc.vector.tensor_copy(k["scales"][:, 2:4], dc[:, 3:5]).then_inc(scales_ready, 1)

        @block.gpsimd
        def _(pool):
            pool.wait_ge(capped, 1)
            nc.gpsimd.tensor_tensor(half[:], norm[:], over(k["powers"][:, 1:2], [P, NB]), ALU.pow).then_inc(rooted, 1)

        @block.tensor
        def _(pe):
            def turn(src, ps, turned):
                for g in range(NG):
                    mm = pe.transpose(ps[:, g * P:(g + 1) * P], src[:, g * P:(g + 1) * P], k["ident"][:])
                mm.then_inc(turned, 1)

            def demodulate(i):
                pe.wait_ge(sq_ready, i + 1)
                reached(pe, biased, i - 1)
                half = KC * (i >= 3)
                for o in range(KC):
                    for c in range(KC):
                        mm = pe.matmul(sums[i % 2][:, o], squared[:, i % 2, c, o * P:(o + 1) * P], style_sq[:, half + c],
                                       start=c == 0, stop=c == KC - 1)
                mm.then_inc(sums_ready, 1)

            pe.wait_ge(style_ready, 1)
            demodulate(0)
            pe.wait_ge(natural, 1)
            turn(dt_all, dtT_ps, turned_dt)
            pe.wait_ge(natural, 2)
            turn(c_all, cT_ps, turned_c)
            pe.wait_ge(dtT_ready, 1)
            for i in range(2):
                pe.matmul(dt_ps[:, i * 512:(i + 1) * 512], k["blockdt"][:], a[:, i * 512:(i + 1) * 512],
                          start=True, stop=True).then_inc(dt_ready, 1)
            demodulate(1)
            demodulate(2)
            pe.wait_ge(inverse_ready, 1)
            turn(inverse, inv_ps, turned_inv)
            demodulate(3)
            demodulate(4)

        @block.scalar
        def _(act):
            def square(i):
                act.wait_ge(w_loaded[i], 16)
                reached(act, sums_ready, i - 1)
                nc.scalar.activation(squared[:, i % 2], weight[:, i], ACT.Square).then_inc(sq_ready, 1)

            nc.scalar.activation(k["alog"][:], k["alog"][:], ACT.Tanh).then_inc(tanh_a, 1)
            nc.scalar.activation(style_sq[:], style[:], ACT.Square).then_inc(style_ready, 1)
            square(0)
            square(1)
            act.wait_ge(dt_ready, 2)
            for i in range(2):
                nc.scalar.activation(a[:, i * 512:(i + 1) * 512], dt_ps[:, i * 512:(i + 1) * 512], ACT.Tanh,
                                     bias=k["bdt"][:]).then_inc(tanh_ready, 1)
            for i in range(2, 5):
                square(i)
            act.wait_ge(biased, 5)
            nc.scalar.activation(dc[:], dc[:], ACT.Sqrt).then_inc(dc_ready, 1)

        @block.sync
        def _(sp):
            for i, name in enumerate(("Wq", "Wk", "Wv", "Ww", "Wu")):
                sp.dma_start(weight[:, i], d[name]).then_inc(w_loaded[i], 16)
            sp.wait_ge(chunks_ready, 1)
            for h in range(2):
                sp.dma_start(d["chunks"][h].rearrange("n p c -> p n c"), chunks[:, h].rearrange("p n a g t -> p n (a g t)")).then_inc(chunk_out, 16)
            sp.wait_ge(split, 1)
            for i in range(3):
                sp.dma_start(d["bparts"][i].rearrange("g t c -> t g c"), b_parts[:, i].rearrange("t (g c) -> t g c", c=P)).then_inc(b_out, 16)
            sp.wait_ge(b_out, 48)
            sp.wait_ge(chunk_out, 32)


def scan(nc, d, k):
    with ExitStack() as ctx:
        m = Memory(nc, ctx, "sc_")
        x_rows = m.sb("x_rows", [KR, 2, GH, TB * 512], BF16)
        b_rows = m.sb("b_rows", [KR, 2, GH, TB, P], BF16)
        mask = m.sb("mask", [KR, P], BF16)
        kc = m.sb("kc", [P, 2, 3, GH, TB])
        c_cols = m.sb("c_cols", [P, 2, GH, TB, 32])
        state = m.sb("state", [P, 2, GH, 512])
        dx = m.sb("dx", [P, 2, 2, 512])
        y = m.sb("y", [P, 2, 512])
        w_high, w_low = k["w_high"], k["w_low"]
        x_raw = m.sb("x_raw", [P, KC, 4 * S])
        x_high, x_low = (m.sb(n, [P, KC, 4 * S], F32R) for n in ("x_high", "x_low"))
        gate = m.sb("gate", [P, 2, 4 * S])
        begun = m.sb("begun", [P, 16])
        u_ps = [m.ps(f"u_ps{g}", [P, 512]) for g in range(GH)]
        y_ps = [m.ps(f"y_ps{i}", [P, 512]) for i in range(2)]
        gate_ps = [m.ps(f"gate_ps{i}", [P, 4 * S]) for i in range(2)]
        sem = m.sem
        x_loaded, b_loaded, kc_loaded, dx_loaded = ([sem(f"{n}{i}") for i in range(2)] for n in ("x_loaded", "b_loaded", "kc_loaded", "dx_loaded"))
        b_masked, c_ready, added, clipped, copied, y_done, y_added = (sem("b_masked"), sem("c_ready"), sem("added"),
            sem("clipped"), sem("copied"), sem("y_done"), sem("y_added"))
        y_out, gate_out = [sem("y_out0"), sem("y_out1")], [sem("gate_out0"), sem("gate_out1")]
        zeroed, mask_ready = sem("zeroed"), sem("mask_ready")
        raw_loaded, raw_copied, raw_split, gate_made, gate_done = sem("raw_loaded"), sem("raw_copied"), sem("raw_split"), sem("gate_made"), sem("gate_done")
        Y_BIAS, ADD_BIAS, OUT_BIAS, GATE_BIAS = TB + 1, 3, 16, 1
        UNROLL = 4
        block = ctx.enter_context(nc.Block())

        def passes(engine, step, start=None):
            for hb in range(2):
                with engine.Fori(0, 2) as dh:
                    if start is not None:
                        start(hb * 2 + dh)
                    with engine.Fori(0, NTB // UNROLL) as j:
                        for i in range(UNROLL):
                            step(hb, dh, j, i, hb * 2 * NTB + dh * NTB + UNROLL * j + i, hb * (NQ // 2) + dh * (NQ // 4) + j)

        def first_position(j, i):
            return UNROLL * TB * j + TB * i

        def same_parity(n, i):
            return n - i % 2

        @block.sync
        def _(sp):
            def step(hb, dh, j, i, n, q):
                par = i % 2
                sp.wait_ge(y_done, TB * n + 1)
                b0 = hb * HALF
                for r, (px, pb) in enumerate(PAIRS):
                    rows = slice(GB * r, GB * (r + 1))
                    src = d["xparts"][px, bass.ds(dh, 1), b0:b0 + HALF, bass.ds(first_position(j, i), TB)]
                    sp.dma_start(x_rows[rows, par], src.rearrange("o (g b) t c -> (o b) g (t c)", b=GB)).then_inc(x_loaded[par], 16)
                    src = d["bparts"][pb:pb + 1, hb * GH:(hb + 1) * GH, bass.ds(first_position(j, i), TB)]
                    sp.dma_start(b_rows[rows, par].rearrange("b g t c -> b g (t c)"),
                                 over(src.rearrange("o g t c -> o g (t c)"), [GB, GH, TB * P])).then_inc(b_loaded[par], 16)
                sp.dma_start(kc[:, par].rearrange("p a g t -> p (a g t)"),
                             d["chunks"][hb, bass.ds(UNROLL * j + i, 1)].rearrange("o p c -> (o p) c")).then_inc(kc_loaded[par], 16)
                if i == 0:
                    sp.wait_ge(raw_split, q + 1)
                    sp.dma_start(x_raw[:], d["xT"][bass.ds(q, 1)].rearrange("o p c n -> (o p) c n")).then_inc(raw_loaded, 16)
                sp.wait_ge(y_added, 2 * n + 1)
                for u in range(2):
                    src = d["dx"][b0:b0 + HALF, bass.ds(first_position(j, i) + 4 * u, 4), bass.ds(512 * dh, 512)]
                    sp.dma_start(dx[:, par, u], src).then_inc(dx_loaded[par], 16)
            passes(sp, step)

        @block.gpsimd
        def _(pool):
            pool.wait_ge(mask_ready, 1)

            def step(hb, dh, j, i, n, q):
                par = i % 2
                pool.wait_ge(b_loaded[par], 48 * same_parity(n, i) + 96)
                for g in range(GH):
                    op = nc.gpsimd.tensor_tensor(b_rows[:, par, g], b_rows[:, par, g], over(mask[:].unsqueeze(1), [KR, TB, P]), ALU.mult)
                op.then_inc(b_masked, 1)
                pool.wait_ge(kc_loaded[par], 8 * same_parity(n, i) + 16)
                pool.wait_ge(y_done, TB * n + 1)
                for g in range(GH):
                    for u in range(2):
                        op = nc.gpsimd.tensor_tensor(c_cols[:, par, g, 4 * u:4 * u + 4], k["head_mask"][:],
                                                     over(kc[:, par, 2, g, 4 * u:4 * u + 4].unsqueeze(2), [P, 4, 32]), ALU.mult)
                op.then_inc(c_ready, 1)
                if i == 0:
                    pool.wait_ge(raw_loaded, 16 * q + 16)
                    pool.wait_ge(gate_made, DC * q + GATE_BIAS)
                    nc.gpsimd.tensor_tensor(x_high[:].rearrange("p c n -> p (c n)"), x_raw[:].rearrange("p c n -> p (c n)"),
                                            over(k["powers"][:, 3:4], [P, KC * 4 * S]), ALU.mult).then_inc(raw_copied, 1)
                    pool.wait_ge(raw_copied, q + 1)
                    nc.gpsimd.tensor_tensor(x_low[:], x_raw[:], x_high[:].bitcast(F32), ALU.subtract).then_inc(raw_split, 1)
            passes(pool, step)

        @block.tensor
        def _(pe):
            def step(hb, dh, j, i, n, q):
                par = i % 2
                if i == 0:
                    pe.wait_ge(zeroed, hb * 2 + dh + 1)
                pe.wait_ge(x_loaded[par], 48 * same_parity(n, i) + 96)
                pe.wait_ge(b_masked, n + 1)

                def drive(t, g):
                    pe.wait_ge(copied, GH * TB * n + GH * t + g + 1)
                    pe.matmul(u_ps[g][:], b_rows[:, par, g, t], x_rows[:, par, g, t * 512:(t + 1) * 512],
                              start=False, stop=False, skip_group_check=True).then_inc(added, 1)

                def gate_part(t, g):
                    at = GH * (TB * i + t) + g
                    if at >= 12 * DC:
                        return
                    c, part = at // 12, at % 12
                    w, x = ((w_high, x_high), (w_low, x_high), (w_high, x_low))[part // KC]
                    if part == 0:
                        if c == 0:
                            pe.wait_ge(raw_split, q + 2)
                        pe.wait_ge(gate_done, DC * q + c + 1)
                    mm = pe.matmul(gate_ps[c % 2][:], w[:, part % KC, c * P:(c + 1) * P], x[:, part % KC], start=part == 0, stop=part == 11)
                    if part == 11:
                        mm.then_inc(gate_made, 1)

                def read(block_n, at_par, t):
                    if t == 0:
                        pe.wait_ge(c_ready, block_n + 1)
                    if t % 4 == 0:
                        pe.wait_ge(y_added, 2 * block_n + t // 4 + 2)
                    pe.wait_ge(clipped, GH * TB * block_n + GH * (t + 1))
                    for g in range(GH):
                        mm = pe.matmul(y_ps[t // 4][32 * g:32 * g + 32, :], c_cols[:, at_par, g, t], state[:, t % 2, g],
                                       start=t % 4 == 0, stop=t % 4 == 3)
                    mm.then_inc(y_done, 1)

                for t in range(TB):
                    for g in range(GH):
                        drive(t, g)
                        gate_part(t, g)
                    if t > 0:
                        read(n, par, t - 1)
                    elif i > 0:
                        read(n - 1, 1 - par, TB - 1)
                if i == UNROLL - 1:
                    read(n, par, TB - 1)
            passes(pe, step)

        @block.vector
        def _(dv):
            nc.vector.tensor_copy(mask[:], k["pick_mask"][:]).then_inc(mask_ready, 1)
            starts = [(y_done, Y_BIAS), (y_added, ADD_BIAS), (copied, GH), (gate_done, 2), (gate_made, GATE_BIAS), (raw_split, 1)]
            starts += [(counter, OUT_BIAS) for counter in (*y_out, *gate_out)]
            for i, (counter, count) in enumerate(starts):
                nc.vector.memset(begun[:, i:i + 1], 0.0).then_inc(counter, count)

            def start(n):
                dv.wait_ge(copied, GH * TB * NTB * n + GH)
                for g in range(GH):
                    op = nc.vector.memset(u_ps[g][:], 0.0)
                op.then_inc(zeroed, 1)

            def step(hb, dh, j, i, n, q):
                par = i % 2
                dv.wait_ge(kc_loaded[par], 8 * same_parity(n, i) + 16)

                def clip(t, g):
                    dv.wait_ge(added, GH * TB * n + GH * t + g + 1)
                    if g == 0:
                        dv.wait_ge(y_done, TB * n + t + Y_BIAS - 1)
                    nc.vector.tensor_scalar(state[:, t % 2, g], u_ps[g][:], kc[:, par, 0, g, t:t + 1], kc[:, par, 1, g, t:t + 1],
                                            ALU.min, ALU.max).then_inc(clipped, 1)

                def add(block_n, at_par, u, jj):
                    dv.wait_ge(y_done, TB * block_n + 4 * u + 4 + Y_BIAS)
                    dv.wait_ge(dx_loaded[at_par], 16 * jj + 32)
                    dv.wait_ge(y_out[u], 16 * block_n + OUT_BIAS)
                    nc.vector.tensor_tensor(y[:, u], y_ps[u][:], dx[:, at_par, u], ALU.add).then_inc(y_added, 1)

                for t in range(TB):
                    for g in range(GH):
                        clip(t, g)
                        if g == 0 and t == 5:
                            add(n, par, 0, same_parity(n, i))
                        if g == 0 and t == 1 and i > 0:
                            add(n - 1, 1 - par, 1, same_parity(n - 1, i - 1))
                if i == UNROLL - 1:
                    add(n, par, 1, same_parity(n, i))
            passes(dv, step, start)

        @block.scalar
        def _(act):
            def step(hb, dh, j, i, n, q):
                b0 = hb * HALF

                def copy(t, g):
                    at = GH * TB * n + GH * t + g
                    act.wait_ge(clipped, at + 1)
                    nc.scalar.activation(u_ps[g][:], state[:, t % 2, g], ACT.Copy).then_inc(copied, 1)

                def store(block_n, position, u):
                    act.wait_ge(y_added, 2 * block_n + u + 1 + ADD_BIAS)
                    dst = d["y"][b0:b0 + HALF, bass.ds(position + 4 * u, 4), bass.ds(512 * dh, 512)]
                    act.dma_start(dst, y[:, u]).then_inc(y_out[u], 16)

                for t in range(TB):
                    for g in range(GH):
                        copy(t, g)
                    if t == 6:
                        store(n, first_position(j, i), 0)
                    if t == 2 and i > 0:
                        store(n - 1, first_position(j, i - 1), 1)
                    at = TB * i + t
                    if at % 3 == 2 and at // 3 < DC:
                        c = at // 3
                        act.wait_ge(gate_made, DC * q + c + 1 + GATE_BIAS)
                        act.wait_ge(gate_out[c % 2], 64 * q + 16 * (c // 2) + OUT_BIAS)
                        nc.scalar.activation(gate[:, c % 2], gate_ps[c % 2][:], ACT.Silu).then_inc(gate_done, 1)
                        act.wait_ge(gate_done, DC * q + c + 3)
                        act.dma_start(d["gate"][bass.ds(q, 1), :, c].rearrange("o p n -> (o p) n"), gate[:, c % 2]).then_inc(gate_out[c % 2], 16)
                if i == UNROLL - 1:
                    store(n, first_position(j, i), 1)
            passes(act, step)
            for u in range(2):
                act.wait_ge(y_out[u], 16 * 4 * NTB + OUT_BIAS)
                act.wait_ge(gate_out[u], 16 * NQ * DC // 2 + OUT_BIAS)


def back(nc, d, k):
    with ExitStack() as ctx:
        m = Memory(nc, ctx, "ba_")
        wout = m.sb("wout", [P, DC, D])
        ww, wu = (m.sb(n, [P, KC, D]) for n in ("ww", "wu"))
        wq, wk, wv = (m.sb(n, [P, 2, KC, D], F32R) for n in ("wq", "wk", "wv"))
        y = m.sb("y", [P, 2, 4, 2 * P])
        gate = m.sb("gate", [P, 4, 4 * S])
        z = m.sb("z", [P, DC, 4 * S])
        probs = z[:, 0:4]
        probsT = z[:, 4:8]
        x_in, style, xs = m.sb("x_in", [P, 2, D]), m.sb("style", [P, 2, D]), m.sb("xs", [P, 2, D])
        x2 = m.sb("x2", [P, 2, 4, D])
        rT, n_high = m.twice("rT", "n_high", [P, KC, 4 * S])
        vT, n_low = m.twice("vT", "n_low", [P, 2, KC, 4 * S])
        qT, kT = (m.sb(n, [P, KC, 4 * S]) for n in ("qT", "kT"))
        v = m.sb("v", [P, 2, 4, D])
        fw = xs[:, 0]
        raw = {"Wv": x2[:, 1], "Wq": qT[:], "Wk": kT[:]}
        total, recip = m.sb("total", [P, 4, 4]), m.sb("recip", [P, 4, 4])
        result = m.sb("result", [P, 2, D])
        scale = m.sb("scale", [P, 4, KC, 4])
        scale_wu = m.sb("scale_wu", [P, 2, KC, 4])
        bn, moments, var, norm = m.sb("bn", [P, 2, 6]), m.sb("moments", [P, 2, 2]), m.sb("var", [P, 2, 1]), m.sb("norm", [P, 2, 2])
        largest, less = m.sb("largest", [P, 4, 4]), m.sb("less", [P, 4, 4])
        pause = m.sb("pause", [P, 1])
        main = [m.ps(f"main{i}", [P, 512]) for i in range(2)]
        side = [m.ps(f"side{i}", [P, 4, S]) for i in range(2)]
        scores = m.ps("scores", [P, 4, 4, S])
        names = """wout_loaded wu_loaded w_high_ready w_low_ready yT_ready z_done wo_ready x2_done xs_ready bn_step mom_ready
            rs_step rs_ready n_ready nT_ready nT_copied nT_low v_ready v_copied vT_ready vT_done q_ready q_done k_ready k_copied s_ready
            max_step max_done exp_done rec_done p_done pT_ready pT_copied o_ready o_done w_ready u_ready fw_done fu_done f_done fT_ready
            out_done scaled""".split()
        s = {n: m.sem(n) for n in names}
        xin_loaded, style_loaded, stored, y_loaded = ([m.sem(f"{n}{i}") for i in range(2)] for n in ("xin_loaded", "style_loaded", "stored", "y_loaded"))
        raw_loaded = {n: m.sem(f"raw_{n}") for n in raw}
        gate_loaded = [m.sem(f"gate_loaded{i}") for i in range(4)]
        block = ctx.enter_context(nc.Block())

        def quads(engine, step):
            step(0, 0, True, False, False)
            step(1, 1, True, True, False)
            step(2, 0, True, True, True)
            step(3, 1, True, True, True)
            with engine.Fori(2, NQ // 2) as j:
                step(2 * j, 0, True, True, True)
                step(2 * j + 1, 1, True, True, True)
            step(NQ, 0, False, True, True)

        def quad_slice(q):
            return bass.ds(4 * q, 4)

        @block.sync
        def _(sp):
            def weights():
                sp.dma_start(wout[:], d["Wout"]).then_inc(s["wout_loaded"], 16)
                for name, place in raw.items():
                    sp.dma_start(place, d[name]).then_inc(raw_loaded[name], 16)
                for w, name in ((ww, "Ww"), (wu, "Wu")):
                    sp.dma_start(w[:], d[name]).then_inc(s["wu_loaded"], 16)

            def step(q, par, now, before, older):
                if not now:
                    return

                def gates(chunks):
                    for c in chunks:
                        reached(sp, s["z_done"], DC * q + c - 3)
                        sp.dma_start(gate[:, c % 4], d["gate"][bass.ds(q, 1), :, c].rearrange("o p n -> (o p) n")).then_inc(gate_loaded[c % 4], 16)

                def rows(u):
                    reached(sp, s["yT_ready"], DC * q + 2 * u - 2)
                    sp.dma_start(y[:, u % 2], d["y"][quad_slice(q), :, 2 * P * u:2 * P * (u + 1)].rearrange("b t c -> t b c")).then_inc(y_loaded[u % 2], 16)

                rows(0)
                rows(1)
                gates(range(4))
                if isinstance(q, int) and q == 0:
                    weights()
                for b in range(4):
                    if b == 2:
                        rows(2)
                        gates((4, 5))
                        rows(3)
                        gates((6, 7))
                    reached(sp, s["x2_done"], 4 * q + b - 1)
                    sp.dma_start(x_in[:, b % 2], d["x"][bass.ds(4 * q + b, 1)].rearrange("o t c -> (o t) c")).then_inc(xin_loaded[b % 2], 16)
                    reached(sp, s["xs_ready"], 4 * q + b - 1)
                    sp.dma_start(style[:, b % 2], over(d["style_rows"][bass.ds(4 * q + b, 1), 0:D], [P, D])).then_inc(style_loaded[b % 2], 16)
            quads(sp, step)

        @block.gpsimd
        def _(pool):
            def store(q):
                for b in range(4):
                    pool.wait_ge(s["out_done"], 4 * q + b + 1)
                    pool.dma_start(d["out"][bass.ds(4 * q + b, 1)].rearrange("o t c -> (o t) c"), result[:, b % 2]).then_inc(stored[b % 2], 16)

            def step(q, par, now, before, older):
                if older:
                    store(q - 2)
                if now:
                    for b in range(4):
                        n, u = 4 * q + b, b % 2
                        pool.wait_ge(s["mom_ready"], n + 1)
                        reached(pool, s["n_ready"], n - 1)
                        nc.gpsimd.tensor_tensor(norm[:, u, 0:1], var[:, u], k["powers"][:, 0:1], ALU.pow).then_inc(s["rs_step"], 1)
                        pool.wait_ge(s["rs_step"], 2 * n + 1)
                        nc.gpsimd.tensor_tensor(norm[:, u, 1:2], moments[:, u, 0:1], norm[:, u, 0:1], ALU.mult).then_inc(s["rs_step"], 1)
                        pool.wait_ge(s["rs_step"], 2 * n + 2)
                        nc.gpsimd.tensor_tensor(norm[:, u, 1:2], norm[:, u, 1:2], k["powers"][:, 2:3], ALU.mult).then_inc(s["rs_ready"], 1)
                if not now:
                    store(q - 1)
            quads(pool, step)
            for u in range(2):
                pool.wait_ge(stored[u], 16 * NB // 2)

        @block.tensor
        def _(pe):
            def products(out, lhs, rhs, sem, chunks=KC):
                for c in range(chunks):
                    mm = pe.matmul(out, lhs(c), rhs(c), start=c == 0, stop=c == chunks - 1)
                mm.then_inc(s[sem], 1)

            def split_products(out, lhs, rhs, sem):
                terms = [(lp, rp, i) for lp, rp in ((0, 0), (1, 0), (0, 1)) for i in range(KC)]
                for at, (lp, rp, i) in enumerate(terms):
                    mm = pe.matmul(out, lhs(lp, i), rhs(rp, i), start=at == 0, stop=at == len(terms) - 1)
                mm.then_inc(s[sem], 1)

            def norm_part(par, part, i):
                return n_low[:, par, i] if part else n_high[:, i]

            def turn_y(q, c):
                if c % 2 == 0:
                    pe.wait_ge(y_loaded[c // 2 % 2], 32 * q + 16 * (c // 4) + 16)
                reached(pe, s["z_done"], DC * q + c - 1)
                for b in range(4):
                    mm = pe.transpose(side[c % 2][:, b], y[:, c // 2 % 2, b, c % 2 * P:(c % 2 + 1) * P], k["ident"][:])
                mm.then_inc(s["yT_ready"], 1)

            def u_product(q, par, b):
                if isinstance(q, int) and q == 1 and b == 0:
                    pe.wait_ge(s["wu_loaded"], 32)
                products(main[1][:], lambda i: wu[:, i, b * P:(b + 1) * P], lambda i: vT[:, 1 - par, i], "u_ready")

            def w_product(q, par, b):
                pe.wait_ge(s["o_done"], 4 * q)
                products(main[0][:].rearrange("p (b t) -> p b t", b=4), lambda i: ww[:, i, b * P:(b + 1) * P],
                         lambda i: v[:, 1 - par, :, i * S:(i + 1) * S], "w_ready")

            def turn_results(q, batches=range(4)):
                pe.wait_ge(s["f_done"], 4 * q + 4)
                for b in batches:
                    if b >= 2:
                        pe.wait_ge(s["out_done"], 4 * q + b - 1)
                    for c in range(KC):
                        mm = pe.transpose(main[b % 2][:, c * P:(c + 1) * P], rT[:, c, b * S:(b + 1) * S], k["ident"][:])
                    mm.then_inc(s["fT_ready"], 1)

            def turn_norm(q, b):
                pe.wait_ge(s["n_ready"], 4 * q + b + 1)
                if b >= 2:
                    pe.wait_ge(s["nT_low"], 4 * q + b - 1)
                for c in range(KC):
                    mm = pe.transpose(side[b % 2][:, c], xs[:, b % 2, c * P:(c + 1) * P], k["ident"][:])
                mm.then_inc(s["nT_ready"], 1)

            def v_rows(q, par, b):
                pe.wait_ge(s["nT_low"], 4 * q + b + 1)
                if b < 2:
                    reached(pe, s["out_done"], 4 * q - 4)
                else:
                    pe.wait_ge(s["k_copied"], 4 * q + b + 1)
                split_products(main[b % 2][:], lambda part, i: norm_part(par, part, i)[:, b * S:(b + 1) * S],
                               lambda part, i: wv[:, part, i], "v_ready")

            def turn_v(q, par, b):
                pe.wait_ge(s["v_copied"], 4 * q + b + 1)
                if b < 2:
                    pe.wait_ge(s["nT_low"], 4 * q + 4)
                else:
                    pe.wait_ge(s["vT_done"], 4 * q + b - 1)
                for c in range(KC):
                    mm = pe.transpose(side[b % 2][:, c], v[:, par, b, c * P:(c + 1) * P], k["ident"][:])
                mm.then_inc(s["vT_ready"], 1)

            def q_chunk(q, par, c):
                if c == 0:
                    pe.wait_ge(s["nT_low"], 4 * q + 4)
                pe.wait_ge(s["v_copied" if c < 2 else "q_done"], 4 * q + (c + 1 if c < 2 else c - 1))
                split_products(main[c % 2][:], lambda part, i: wq[:, part, i, c * P:(c + 1) * P], lambda part, i: norm_part(par, part, i), "q_ready")

            def k_chunk(q, par, c):
                pe.wait_ge(s["q_done" if c < 2 else "k_copied"], 4 * q + (c + 3 if c < 2 else c - 1))
                split_products(main[c % 2][:], lambda part, i: wk[:, part, i, c * P:(c + 1) * P], lambda part, i: norm_part(par, part, i), "k_ready")

            def score(q, b):
                if b == 0:
                    pe.wait_ge(s["k_copied"], 4 * q + 4)
                    pe.wait_ge(s["x2_done"], 4 * q + 4)
                else:
                    pe.wait_ge(s["exp_done"], 16 * q + 4 * b)
                for i in range(4):
                    for j in range(4):
                        r = slice(32 * j, 32 * j + 32)
                        mm = pe.matmul(scores[:, j, i], qT[r, i, b * S:(b + 1) * S], kT[r, i, b * S:(b + 1) * S], start=True, stop=True)
                mm.then_inc(s["s_ready"], 1)

            def turn_probs(q, b, before):
                for i in range(4):
                    if i % 2 == 0:
                        pe.wait_ge(s["p_done"], 8 * q + 2 * b + i // 2 + 1)
                    if before and i == 1:
                        pe.wait_ge(s["fu_done"], 4 * q - 3 + b)
                    elif b == 0 and i < 2:
                        pe.wait_ge(s["v_copied"], 4 * q + 3 + i)
                    elif before and i == 0:
                        pe.wait_ge(s["fw_done"], 4 * q - 4 + b)
                    else:
                        pe.wait_ge(s["pT_copied"], 16 * q + 4 * b + i - 1)
                    for j in range(4):
                        mm = pe.transpose(main[i % 2][:, j * P:(j + 1) * P], probs[:, j, i * S:(i + 1) * S], k["ident"][:])
                    mm.then_inc(s["pT_ready"], 1)

            def mix(q, par, b):
                pe.wait_ge(s["pT_copied"], 16 * q + 4 * b + 4)
                if b < 2:
                    pe.wait_ge(s["vT_done"], 4 * q + 4)
                else:
                    pe.wait_ge(s["o_done"], 4 * q + b - 1)
                for i in range(4):
                    for j in range(4):
                        h = 4 * i + j
                        mm = pe.matmul(side[b % 2][32 * j:32 * j + 32, i], v[:, par, b, h * HD:(h + 1) * HD],
                                       probsT[:, i, j * S:(j + 1) * S], start=True, stop=True)
                mm.then_inc(s["o_ready"], 1)

            def step(q, par, now, before, older):
                if not now:
                    turn_results(q - 2)
                    pe.wait_ge(s["out_done"], 4 * q - 4)
                    for b in range(KC):
                        if b > 0:
                            pe.wait_ge(s["fu_done"], 4 * q - 4 + b)
                        u_product(q, par, b)
                        if b > 0:
                            pe.wait_ge(s["fw_done"], 4 * q - 4 + b)
                        w_product(q, par, b)
                    turn_results(q - 1)
                    return

                def wout_chunk(c, b):
                    return pe.matmul(scores[:, b].rearrange("p i t -> p (i t)"), z[:, c, b * S:(b + 1) * S], wout[:, c],
                                     start=c == 0, stop=c == DC - 1)

                first = isinstance(q, int) and q == 0
                reached(pe, s["o_done"], 4 * q - 1)
                turn_y(q, 0)
                reached(pe, s["o_done"], 4 * q)
                turn_y(q, 1)
                if first:
                    pe.wait_ge(s["wout_loaded"], 16)
                for c in range(4):
                    pe.wait_ge(s["z_done"], DC * q + c + 1)
                    for b in range(4):
                        wout_chunk(c, b)
                    if c < 3:
                        turn_y(q, 2 * c + 2)
                        turn_y(q, 2 * c + 3)
                if older:
                    turn_results(q - 2, (0, 1))
                pe.wait_ge(s["z_done"], DC * q + DC)
                for b in range(4):
                    for c in range(4, DC):
                        mm = wout_chunk(c, b)
                    mm.then_inc(s["wo_ready"], 1)
                    if b == 0 and older:
                        turn_results(q - 2, (2, 3))
                    if b > 1:
                        turn_norm(q, b - 2)
                turn_norm(q, 2)
                if first:
                    pe.wait_ge(s["w_low_ready"], 3)
                v_rows(q, par, 0)
                turn_norm(q, 3)
                v_rows(q, par, 1)
                for c in range(KC):
                    q_chunk(q, par, c)
                for c in range(KC):
                    k_chunk(q, par, c)
                turn_v(q, par, 0)
                turn_v(q, par, 1)
                score(q, 0)
                v_rows(q, par, 2)
                v_rows(q, par, 3)
                turn_v(q, par, 2)
                turn_v(q, par, 3)
                if before:
                    pe.wait_ge(s["v_copied"], 4 * q + 4)
                    u_product(q, par, 0)
                score(q, 1)
                for b in range(4):
                    turn_probs(q, b, before)
                    if before:
                        pe.wait_ge(s["pT_copied"], 16 * q + 4 * b + 3)
                        w_product(q, par, b)
                    mix(q, par, b)
                    if before and b < 3:
                        u_product(q, par, b + 1)
                    if b < 2:
                        score(q, b + 2)
            quads(pe, step)

        @block.scalar
        def _(act):
            def step(q, par, now, before, older):
                if not now:
                    return

                def normalise(b):
                    act.wait_ge(s["rs_ready"], 4 * q + b + 1)
                    nc.scalar.activation(xs[:, b % 2], xs[:, b % 2], ACT.Identity, bias=norm[:, b % 2, 1:2],
                                         scale=norm[:, b % 2, 0:1]).then_inc(s["n_ready"], 1)

                def copy_norm(b):
                    act.wait_ge(s["nT_ready"], 4 * q + b + 1)
                    if b == 0:
                        reached(act, s["fT_ready"], 4 * q - 4)
                    nc.scalar.activation(n_high[:, :, b * S:(b + 1) * S], side[b % 2][:], ACT.Copy).then_inc(s["nT_copied"], 1)

                def copy_v(b):
                    act.wait_ge(s["v_ready"], 4 * q + b + 1)
                    nc.scalar.activation(v[:, par, b], main[b % 2][:], ACT.Copy).then_inc(s["v_copied"], 1)

                if isinstance(q, int) and q == 0:
                    for name, w in (("Wv", wv), ("Wq", wq), ("Wk", wk)):
                        act.wait_ge(raw_loaded[name], 16)
                        nc.scalar.activation(w[:, 0], raw[name], ACT.Copy).then_inc(s["w_high_ready"], 1)
                normalise(0)
                normalise(1)
                copy_norm(0)
                normalise(2)
                copy_norm(1)
                normalise(3)
                copy_norm(2)
                copy_v(0)
                copy_norm(3)
                copy_v(1)
                for c in range(KC):
                    act.wait_ge(s["k_ready"], 4 * q + c + 1)
                    nc.scalar.activation(kT[:, c], main[c % 2][:], ACT.Copy).then_inc(s["k_copied"], 1)

                def exponents(b, columns=range(4)):
                    act.wait_ge(s["max_done"], 4 * q + b + 1)
                    for i in columns:
                        if b > 0:
                            act.wait_ge(s["pT_ready"], 16 * q + 4 * b + i - 3)
                            if i == 0:
                                act.wait_ge(s["rec_done"], 8 * q + 2 * b)
                        for j in range(4):
                            op = nc.scalar.activation(probs[:, j, i * S:(i + 1) * S], scores[:, j, i], ACT.Exp, bias=less[:, i, j:j + 1],
                                                      accum_out=total[:, i, j:j + 1])
                        op.then_inc(s["exp_done"], 1)

                exponents(0, (0, 1))
                copy_v(2)
                copy_v(3)
                exponents(0, (2, 3))
                for b in range(4):
                    for i in range(4):
                        act.wait_ge(s["pT_ready"], 16 * q + 4 * b + i + 1)
                        if i == 0:
                            reached(act, s["o_ready"], 4 * q + b)
                        nc.scalar.activation(probsT[:, i], main[i % 2][:], ACT.Copy).then_inc(s["pT_copied"], 1)
                    if b < 3:
                        exponents(b + 1)
            quads(act, step)

        @block.vector
        def _(dv):
            def step(q, par, now, before, older):
                if before:
                    nc.vector.tensor_copy(scale_wu[:], k["scales"][:, 2:4, :, bass.ds(4 * q - 4, 4)]).then_inc(s["scaled"], 1)

                def scaled_u(c):
                    dv.wait_ge(s["u_ready"], 4 * q - 4 + c + 1)
                    nc.vector.tensor_tensor(rT[:, c].rearrange("p (b t) -> p b t", b=4), main[1][:].rearrange("p (b t) -> p b t", b=4),
                                            over(scale_wu[:, 1, c].unsqueeze(2), [P, 4, S]), ALU.mult).then_inc(s["fu_done"], 1)

                def scaled_w(c):
                    n = 4 * q - 4 + c
                    dv.wait_ge(s["w_ready"], n + 1)
                    reached(dv, s["f_done"], n)
                    nc.vector.tensor_tensor(fw.rearrange("p (b t) -> p b t", b=4), main[0][:].rearrange("p (b t) -> p b t", b=4),
                                            over(scale_wu[:, 0, c].unsqueeze(2), [P, 4, S]), ALU.mult).then_inc(s["fw_done"], 1)
                    dv.wait_ge(s["fw_done"], n + 1)
                    dv.wait_ge(s["fu_done"], n + 1)
                    nc.vector.tensor_tensor(rT[:, c], rT[:, c], fw, ALU.add).then_inc(s["f_done"], 1)

                def results(of, x2_par, batches=range(4)):
                    for b in batches:
                        dv.wait_ge(s["fT_ready"], 4 * of + b + 1)
                        reached(dv, stored[b % 2], 32 * of + 16 * (b // 2))
                        nc.vector.tensor_tensor(result[:, b % 2], main[b % 2][:], x2[:, x2_par, b], ALU.add).then_inc(s["out_done"], 1)

                if not now:
                    results(q - 2, par)
                    for c in range(KC):
                        scaled_u(c)
                        scaled_w(c)
                    results(q - 1, 1 - par)
                    return
                reached(dv, s["o_done"], 4 * q)
                nc.vector.tensor_copy(scale[:, 0:2], k["scales"][:, 0:2, :, quad_slice(q)]).then_inc(s["scaled"], 1)
                for c in range(DC):
                    dv.wait_ge(gate_loaded[c % 4], 32 * q + 16 * (c // 4) + 16)
                    dv.wait_ge(s["yT_ready"], DC * q + c + 1)
                    if c == 0:
                        reached(dv, s["o_ready"], 4 * q)
                    nc.vector.tensor_tensor(z[:, c], side[c % 2][:].rearrange("p b t -> p (b t)"), gate[:, c % 4], ALU.mult).then_inc(s["z_done"], 1)
                if isinstance(q, int) and q == 0:
                    for i, (name, w) in enumerate((("Wv", wv), ("Wq", wq), ("Wk", wk))):
                        dv.wait_ge(s["w_high_ready"], i + 1)
                        nc.vector.tensor_tensor(w[:, 1], raw[name], w[:, 0].bitcast(F32), ALU.subtract).then_inc(s["w_low_ready"], 1)

                def norm_low(b):
                    cols = slice(b * S, (b + 1) * S)
                    dv.wait_ge(s["nT_copied"], 4 * q + b + 1)
                    nc.vector.tensor_tensor(n_low[:, par, :, cols], side[b % 2][:], n_high[:, :, cols].bitcast(F32), ALU.subtract).then_inc(s["nT_low"], 1)

                for b in range(4):
                    if older and b < 2:
                        results(q - 2, par, (2 * b, 2 * b + 1))
                    if b == 3:
                        norm_low(0)
                    n, u = 4 * q + b, b % 2
                    dv.wait_ge(s["wo_ready"], n + 1)
                    if older:
                        dv.wait_ge(s["out_done"], n - 7)
                    dv.wait_ge(xin_loaded[u], 32 * q + 16 * (b // 2) + 16)
                    nc.vector.tensor_tensor(x2[:, par, b], scores[:, b].rearrange("p i t -> p (i t)"), x_in[:, u], ALU.add).then_inc(s["x2_done"], 1)
                    dv.wait_ge(s["x2_done"], n + 1)
                    dv.wait_ge(style_loaded[u], 32 * q + 16 * (b // 2) + 16)
                    reached(dv, s["nT_ready"], n - 1)
                    nc.vector.tensor_tensor(xs[:, u], x2[:, par, b], style[:, u], ALU.mult).then_inc(s["xs_ready"], 1)
                    dv.wait_ge(s["xs_ready"], n + 1)
                    nc.vector.bn_stats(bn[:, u], xs[:, u]).then_inc(s["bn_step"], 1)
                    reached(dv, s["rs_ready"], n - 1)
                    dv.wait_ge(s["bn_step"], 2 * n + 1)
                    nc.vector.memset(pause[:], 0.0)
                    nc.vector.bn_aggr(moments[:, u], bn[:, u]).then_inc(s["bn_step"], 1)
                    dv.wait_ge(s["bn_step"], 2 * n + 2)
                    nc.vector.tensor_scalar(var[:, u], moments[:, u, 1:2], LN_EPS, None, ALU.add).then_inc(s["mom_ready"], 1)

                for b in range(1, 4):
                    norm_low(b)

                def scale_v(b):
                    dv.wait_ge(s["vT_ready"], 4 * q + b + 1)
                    nc.vector.tensor_tensor(vT[:, par, :, b * S:(b + 1) * S], side[b % 2][:], over(scale[:, 1, :, b:b + 1], [P, KC, S]),
                                            ALU.mult).then_inc(s["vT_done"], 1)

                def scale_q(c):
                    dv.wait_ge(s["q_ready"], 4 * q + c + 1)
                    nc.vector.tensor_tensor(qT[:, c].rearrange("p (b t) -> p b t", b=4), main[c % 2][:].rearrange("p (b t) -> p b t", b=4),
                                            over(scale[:, 0, c].unsqueeze(2), [P, 4, S]), ALU.mult).then_inc(s["q_done"], 1)

                dv.wait_ge(s["scaled"], 2 * q + 1)
                for c in range(KC):
                    scale_q(c)

                def most(b):
                    n = 4 * q + b
                    dv.wait_ge(s["s_ready"], n + 1)
                    nc.vector.tensor_reduce(largest[:], scores[:].rearrange("p j i t -> p i j t"), AX_X, ALU.max).then_inc(s["max_step"], 1)
                    dv.wait_ge(s["max_step"], n + 1)
                    reached(dv, s["exp_done"], 4 * n)
                    nc.vector.tensor_scalar(less[:], largest[:], -1.0, None, ALU.mult).then_inc(s["max_done"], 1)

                def normalise(b, halves=(0, 1)):
                    for h in halves:
                        n = 8 * q + 2 * b + h
                        heads = slice(2 * h, 2 * h + 2)
                        dv.wait_ge(s["exp_done"], 16 * q + 4 * b + 2 * h + 2)
                        nc.vector.reciprocal(recip[:, heads], total[:, heads]).then_inc(s["rec_done"], 1)
                        dv.wait_ge(s["rec_done"], n + 1)
                        part = probs.rearrange("p j (i t) -> p i j t", i=4)[:, heads]
                        nc.vector.tensor_tensor(part, part, over(recip[:, heads].unsqueeze(3), [P, 2, 4, S]), ALU.mult).then_inc(s["p_done"], 1)

                def output(b):
                    dv.wait_ge(s["o_ready"], 4 * q + b + 1)
                    nc.vector.tensor_tensor(v[:, par, b].rearrange("p (i t) -> p i t", i=KC), side[b % 2][:], over(scale[:, 1, :, b:b + 1], [P, KC, S]),
                                            ALU.mult).then_inc(s["o_done"], 1)

                scale_v(0)
                scale_v(1)
                most(0)
                normalise(0, (0,))
                scale_v(2)
                scale_v(3)
                normalise(0, (1,))
                if before:
                    scaled_u(0)
                most(1)
                for b in range(4):
                    if b < 3:
                        normalise(b + 1, (0,))
                    if before:
                        scaled_w(b)
                    if b < 3:
                        normalise(b + 1, (1,))
                    output(b)
                    if before and b < 3:
                        scaled_u(b + 1)
                    if b < 2:
                        most(b + 2)
            quads(dv, step)


def program(nc, d):
    with ExitStack() as ctx:
        m = Memory(nc, ctx, "")
        k = {"ident": m.sb("ident", [P, P]), "powers": m.sb("powers", [P, 4]), "scales": m.sb("scales", [P, 4, KC, NB])}
        with ExitStack() as ctx2:
            m = Memory(nc, ctx2, "")
            k["head_mask"] = m.sb("head_mask", [P, 4, 32])
            k["pick_mask"] = m.sb("pick_mask", [KR, P])
            k["w_high"], k["w_low"] = (m.sb(n, [P, KC, DI], F32R) for n in ("w_high", "w_low"))
            with ExitStack() as ctx3:
                m = Memory(nc, ctx3, "")
                for name, shape in (("temb", [P, DC, NB]), ("conv_w", [P, DC, 4]), ("conv_b", [P, DC]), ("bdt", [P, 1]), ("alog", [P, 1]),
                                    ("blockdt", [P, P]), ("wxg", [P, DC, NP]), ("fold", [P, 2, NP]),
                                    ("proj", [P, NB, NP]), ("stats", [P, NB, 4])):
                    k[name] = m.sb(name, shape)
                with ExitStack() as ctx4:
                    k["win"] = Memory(nc, ctx4, "").sb("win", [P, KC, DI])
                    coefficients(nc, d, k)
                    front(nc, d, k)
                projections(nc, d, k)
            scan(nc, d, k)
        back(nc, d, k)


def kernel(x, cond_2048, L0_cond_W_in, L0_cond_W_conv, L0_cond_b_conv, L0_cond_ln_g, L0_cond_ln_b, L0_cond_W_xproj, L0_cond_W_dt,
           L0_cond_b_dt, L0_cond_A_log, L0_cond_D, L0_cond_W_out, L1_cond_q_weight, L1_cond_k_weight, L1_cond_v_weight,
           L1_cond_w_weight, L1_cond_u_weight):
    import concourse.bacc as bacc
    import numpy as np
    from concourse.bass_utils import run_bass_kernel_spmd

    def chunked(a):
        a = np.asarray(a)
        return a.reshape(a.shape[0] // P, P, -1).transpose(1, 0, 2)

    x = np.asarray(x)
    block_dt = np.zeros((GB, NS, GB, NS), np.float32)
    head_mask = np.zeros((GB, NS, 4, GB, 4), np.float32)
    pick_mask = np.zeros((len(PAIRS), GB, GB, NS), np.float32)
    for b in range(GB):
        block_dt[b, :, b, :] = np.asarray(L0_cond_W_dt).T
        pick_mask[:, b, b] = 1.0
        for t in range(4):
            head_mask[b, :, t, b, t] = 1.0
    arrays = {
        "x": x,
        "xT": x.reshape(NQ, 4, S, KC, P).transpose(0, 4, 3, 1, 2).reshape(NQ, P, KC, 4 * S),
        "temb": chunked(np.asarray(cond_2048).T),
        "style_rows": cond_2048,
        "Win": chunked(np.asarray(L0_cond_W_in).T),
        "conv_w": chunked(np.asarray(L0_cond_W_conv).reshape(DI, 4)),
        "conv_b": np.asarray(L0_cond_b_conv).reshape(DC, P).T,
        "ln_g": np.asarray(L0_cond_ln_g).reshape(DC, P).T,
        "ln_b": np.asarray(L0_cond_ln_b).reshape(DC, P).T,
        "ln_g_row": np.asarray(L0_cond_ln_g).reshape(1, DI),
        "ln_b_row": np.asarray(L0_cond_ln_b).reshape(1, DI),
        "D_row": np.asarray(L0_cond_D).reshape(1, DI),
        "Wx": chunked(np.asarray(L0_cond_W_xproj).T),
        "W_dt": block_dt.reshape(P, P),
        "b_dt": np.tile(np.asarray(L0_cond_b_dt), GB).reshape(P, 1),
        "A_log": np.tile(np.asarray(L0_cond_A_log), GB).reshape(P, 1),
        "Wout": chunked(np.asarray(L0_cond_W_out).T),
        "Wq": chunked(np.asarray(L1_cond_q_weight).T),
        "Wk": chunked(np.asarray(L1_cond_k_weight).T),
        "Wv": chunked(np.asarray(L1_cond_v_weight).T),
        "Ww": chunked(np.asarray(L1_cond_w_weight).T),
        "Wu": chunked(np.asarray(L1_cond_u_weight).T),
        "ident": np.eye(P, dtype=np.float32),
        "head_mask": head_mask.reshape(P, 4, 32),
        "pick_mask": pick_mask.reshape(KR, P),
    }
    nc = bacc.Bacc("TRN2", target_bir_lowering=False, num_devices=1)
    fed, d = {}, {}
    for name, a in arrays.items():
        a = np.ascontiguousarray(a)
        fed[f"in_{name}"] = a
        d[name] = nc.dram_tensor(f"in_{name}", a.shape, mybir.dt.from_np(a.dtype), kind="ExternalInput").ap()
    d["xparts"] = nc.dram_tensor("xparts", (3, 2, NB, S, 512), BF16, kind="Internal").ap()
    d["bparts"] = nc.dram_tensor("bparts", (3, NG, S, P), BF16, kind="Internal").ap()
    d["chunks"] = nc.dram_tensor("chunks", (2, NTB, P, 3 * GH * TB), F32, kind="Internal").ap()
    d["dx"] = nc.dram_tensor("dx", (NB, S, DI), F32, kind="Internal").ap()
    d["gate"] = nc.dram_tensor("gate", (NQ, P, DC, 4 * S), F32, kind="Internal").ap()
    d["y"] = nc.dram_tensor("y", (NB, S, DI), F32, kind="Internal").ap()
    d["out"] = nc.dram_tensor("out", (NB, S, D), F32, kind="ExternalOutput").ap()
    program(nc, d)
    result = run_bass_kernel_spmd(nc, [fed], core_ids=[0])
    return result.results[0]["out"]
```
